# Optimizing a Trainium2 kernel written in Bass

```python
import numpy as np
import jax
import jax.numpy as jnp

def _softmax(x, axis=-1):
    return jax.nn.softmax(x, axis=axis)

def _gelu(x):
    return jax.nn.gelu(x, approximate=True)

def _silu(x):
    return jax.nn.silu(x)

def _sigmoid(x):
    return jax.nn.sigmoid(x)

def _layernorm(x, axis=-1, eps=1e-05):
    m = jnp.mean(x, axis=axis, keepdims=True)
    v = jnp.var(x, axis=axis, keepdims=True)
    return (x - m) / jnp.sqrt(v + eps)

def _scatter_add(tgt, idx, src, axis=0):
    return tgt.at[idx].add(src)

def _segment_sum(src, seg, n):
    return jax.ops.segment_sum(src, seg, n)
kernel_name = 'mk_flamingo_gated_d2_seqx_r4_7fe27d'

def setup_inputs(seed: int=0):
    np.random.seed(seed)
    _w = jnp.asarray

    def _rec_inputs():
        import jax
        import jax.numpy as jnp
        _rk = jax.random.key(seed)
        x = 7.22e-05 + 1 * jax.random.normal(jax.random.fold_in(_rk, 1), (32, 100, 256), jnp.float32)
        _lenS = 100 - jax.random.randint(jax.random.fold_in(_rk, 7), (32,), 0, max(1, 100 // 4) + 1, jnp.int32)
        _lenS2 = 361 - jax.random.randint(jax.random.fold_in(_rk, 8), (32,), 0, max(1, 361 // 4) + 1, jnp.int32)
        _ctx_1024P = jax.random.normal(jax.random.fold_in(_rk, 11), (32, 16, 256), jnp.float32)
        _ctx_1024c = jax.random.dirichlet(jax.random.fold_in(_rk, 511), 0.3 * jnp.ones((16,), jnp.float32), (32, 361))
        _ctx_1024t = jnp.einsum('bsk,bkd->bsd', _ctx_1024c, _ctx_1024P)
        _ctx_1024t = _ctx_1024t * jax.lax.rsqrt(jnp.mean(jnp.square(_ctx_1024t)) + 1e-12) * 0.953939
        ctx_1024 = 4.13588e-05 + 0.999923 * (_ctx_1024t + 0.3 * jax.random.normal(jax.random.fold_in(_rk, 611), (32, 361, 256), jnp.float32))
        _g = jax.random.normal(jax.random.fold_in(_rk, 9001), (2, 2), jnp.float32)
        _g = jnp.sign(_g) * jnp.maximum(jnp.abs(_g), 1.0) + (_g == 0) * 1.0
        g_xattn = _g[0]
        g_ffn = _g[1]
        return (x, ctx_1024, g_xattn, g_ffn)
    x, ctx_1024, g_xattn, g_ffn = _rec_inputs()

    def _L0_xattn_setup():
        import jax, jax.numpy as jnp
        import numpy as np
        E = 256
        R = 16
        B = 4
        S = 512
        key = jax.random.key(seed)
        ks = jax.random.split(key, 12)
        inp = {'query': jax.random.normal(ks[0], (B, S, E), jnp.float32), 'key': jax.random.normal(ks[1], (B, S, E), jnp.float32), 'value': jax.random.normal(ks[2], (B, S, E), jnp.float32), 'Q_weight': jax.random.normal(ks[3], (E, E), jnp.float32) / np.sqrt(E), 'K_weight': jax.random.normal(ks[4], (E, E), jnp.float32) / np.sqrt(E), 'V_weight': jax.random.normal(ks[5], (E, E), jnp.float32) / np.sqrt(E), 'Q_A': 0.02 * jax.random.normal(ks[6], (R, E), jnp.float32), 'Q_B': 0.02 * jax.random.normal(ks[7], (E, R), jnp.float32), 'K_A': 0.02 * jax.random.normal(ks[8], (R, E), jnp.float32), 'K_B': 0.02 * jax.random.normal(ks[9], (E, R), jnp.float32), 'V_A': 0.02 * jax.random.normal(ks[10], (R, E), jnp.float32), 'V_B': 0.02 * jax.random.normal(ks[11], (E, R), jnp.float32), 'O_weight': jax.random.normal(jax.random.fold_in(key, 99), (E, E), jnp.float32) / np.sqrt(E)}
        return inp
    _L0_xattn_all = _L0_xattn_setup()
    _L0_xattn_in = {k: v for k, v in _L0_xattn_all.items() if k in ('Q_weight', 'K_weight', 'V_weight', 'Q_A', 'Q_B', 'K_A', 'K_B', 'V_A', 'V_B', 'O_weight')}
    del _L0_xattn_all

    def _L0_ffn_setup():
        import jax, jax.numpy as jnp
        import numpy as np
        TOP_K = 2
        key = jax.random.key(seed)
        ks = jax.random.split(key, 5)
        B, S, D, E = (4, 512, 256, 8)
        H = 4 * D
        scale = 0.02
        return {'x': jax.random.normal(ks[0], (B, S, D), dtype=jnp.float32), 'gate_w': jax.random.normal(ks[1], (E, D), dtype=jnp.float32) * scale, 'gate_b': jnp.zeros((E,), dtype=jnp.float32), 'w1': jax.random.normal(ks[2], (E, H, D), dtype=jnp.float32) * scale, 'b1': jnp.zeros((E, H), dtype=jnp.float32), 'w2': jax.random.normal(ks[3], (E, D, H), dtype=jnp.float32) * scale, 'b2': jnp.zeros((E, D), dtype=jnp.float32)}
    _L0_ffn_all = _L0_ffn_setup()
    _L0_ffn_in = {k: v for k, v in _L0_ffn_all.items() if k in ('gate_w', 'gate_b', 'w1', 'b1', 'w2', 'b2')}
    del _L0_ffn_all

    def _L1_xattn_setup():
        import jax, jax.numpy as jnp
        import numpy as np
        from math import sqrt
        key = jax.random.key(seed)
        kq, kk, kv = jax.random.split(key, 3)
        B, S, D = (8, 1024, 256)
        q = jax.random.normal(kq, (B, S, D), dtype=jnp.float32)
        k = jax.random.normal(kk, (B, S, D), dtype=jnp.float32)
        v = jax.random.normal(kv, (B, S, D), dtype=jnp.float32)
        return {'q': q, 'k': k, 'v': v}
    _L1_xattn_all = _L1_xattn_setup()
    _L1_xattn_in = {k: v for k, v in _L1_xattn_all.items() if k in ()}
    del _L1_xattn_all

    def _L1_ffn_setup():
        import jax, jax.numpy as jnp
        import numpy as np
        EPS = 1e-05

        def act_quant(x):
            scale = 127.0 / jnp.clip(jnp.max(jnp.abs(x), axis=-1, keepdims=True), EPS, None)
            xq = jnp.clip(jnp.round(x * scale), -128.0, 127.0)
            return (xq, scale)

        def weight_quant(w):
            scale = 1.0 / jnp.clip(jnp.mean(jnp.abs(w)), EPS, None)
            wq = jnp.clip(jnp.round(w * scale), -1.0, 1.0)
            return (wq, scale)

        def qlinear(x, w, b):
            xq, sx = act_quant(x)
            wq, sw = weight_quant(w)
            y = jnp.einsum('bsd,hd->bsh', xq, wq) / (sx * sw)
            return y + b

        def layernorm(x, gamma, beta):
            mu = jnp.mean(x, axis=-1, keepdims=True)
            var = jnp.mean(jnp.square(x - mu), axis=-1, keepdims=True)
            return (x - mu) * jax.lax.rsqrt(var + EPS) * gamma + beta
        key = jax.random.key(seed)
        ks = jax.random.split(key, 6)
        dim, hidden = (256, 1024)
        B, S = (4, 512)
        x = jax.random.normal(ks[0], (B, S, dim), dtype=jnp.float32)
        w1 = jax.random.normal(ks[1], (hidden, dim), dtype=jnp.float32) * (1.0 / np.sqrt(dim))
        b1 = jnp.zeros((hidden,), dtype=jnp.float32)
        w2 = jax.random.normal(ks[2], (dim, hidden), dtype=jnp.float32) * (1.0 / np.sqrt(hidden))
        b2 = jnp.zeros((dim,), dtype=jnp.float32)
        gamma = jnp.ones((dim,), dtype=jnp.float32)
        beta = jnp.zeros((dim,), dtype=jnp.float32)
        return {'x': x, 'w1': w1, 'b1': b1, 'w2': w2, 'b2': b2, 'gamma': gamma, 'beta': beta}
    _L1_ffn_all = _L1_ffn_setup()
    _L1_ffn_in = {k: v for k, v in _L1_ffn_all.items() if k in ('w1', 'b1', 'w2', 'b2', 'gamma', 'beta')}
    del _L1_ffn_all
    return {'x': x, 'ctx_1024': ctx_1024, 'g_xattn': g_xattn, 'g_ffn': g_ffn, 'L0_xattn_Q_weight': _L0_xattn_in['Q_weight'], 'L0_xattn_K_weight': _L0_xattn_in['K_weight'], 'L0_xattn_V_weight': _L0_xattn_in['V_weight'], 'L0_xattn_Q_A': _L0_xattn_in['Q_A'], 'L0_xattn_Q_B': _L0_xattn_in['Q_B'], 'L0_xattn_K_A': _L0_xattn_in['K_A'], 'L0_xattn_K_B': _L0_xattn_in['K_B'], 'L0_xattn_V_A': _L0_xattn_in['V_A'], 'L0_xattn_V_B': _L0_xattn_in['V_B'], 'L0_xattn_O_weight': _L0_xattn_in['O_weight'], 'L0_ffn_gate_w': _L0_ffn_in['gate_w'], 'L0_ffn_gate_b': _L0_ffn_in['gate_b'], 'L0_ffn_w1': _L0_ffn_in['w1'], 'L0_ffn_b1': _L0_ffn_in['b1'], 'L0_ffn_w2': _L0_ffn_in['w2'], 'L0_ffn_b2': _L0_ffn_in['b2'], 'L1_ffn_w1': _L1_ffn_in['w1'], 'L1_ffn_b1': _L1_ffn_in['b1'], 'L1_ffn_w2': _L1_ffn_in['w2'], 'L1_ffn_b2': _L1_ffn_in['b2'], 'L1_ffn_gamma': _L1_ffn_in['gamma'], 'L1_ffn_beta': _L1_ffn_in['beta']}

def reference(x, ctx_1024, g_xattn, g_ffn, L0_xattn_Q_weight, L0_xattn_K_weight, L0_xattn_V_weight, L0_xattn_Q_A, L0_xattn_Q_B, L0_xattn_K_A, L0_xattn_K_B, L0_xattn_V_A, L0_xattn_V_B, L0_xattn_O_weight, L0_ffn_gate_w, L0_ffn_gate_b, L0_ffn_w1, L0_ffn_b1, L0_ffn_w2, L0_ffn_b2, L1_ffn_w1, L1_ffn_b1, L1_ffn_w2, L1_ffn_b2, L1_ffn_gamma, L1_ffn_beta):
    import jax
    import jax.numpy as jnp

    def _L0_xattn_ref(query, key, value, Q_weight, K_weight, V_weight, Q_A, Q_B, K_A, K_B, V_A, V_B, O_weight):
        import jax, jax.numpy as jnp
        import numpy as np
        E = 256
        R = 16
        B = 4
        S = 512
        embed_dim = Q_weight.shape[0]
        Q = jnp.einsum('bse,fe->bsf', query, Q_weight) + jnp.einsum('bse,re->bsr', query, Q_A) @ Q_B.T
        K = jnp.einsum('bse,fe->bsf', key, K_weight) + jnp.einsum('bse,re->bsr', key, K_A) @ K_B.T
        V = jnp.einsum('bse,fe->bsf', value, V_weight) + jnp.einsum('bse,re->bsr', value, V_A) @ V_B.T
        scores = jnp.einsum('bqe,bke->bqk', Q, K) / jnp.sqrt(jnp.float32(embed_dim))
        attn = jax.nn.softmax(scores, axis=-1)
        out = jnp.einsum('bqk,bke->bqe', attn, V)
        return jnp.einsum('bse,fe->bsf', out, O_weight)

    def _L0_ffn_ref(x, gate_w, gate_b, w1, b1, w2, b2):
        import jax, jax.numpy as jnp
        import numpy as np
        TOP_K = 2
        B, S, D = x.shape
        E = gate_w.shape[0]
        logits = jnp.einsum('bsd,ed->bse', x, gate_w) + gate_b
        scores = jax.nn.softmax(logits, axis=-1)
        topk_scores, topk_idx = jax.lax.top_k(scores, TOP_K)
        onehot = jax.nn.one_hot(topk_idx, E, dtype=scores.dtype)
        dispatch = jnp.einsum('bsk,bske->bse', topk_scores, onehot)
        x_flat = x.reshape(B * S, D)
        w_flat = dispatch.reshape(B * S, E)
        out = jnp.zeros_like(x_flat)
        for i in range(E):
            wi = w_flat[:, i:i + 1]
            h = jax.nn.relu(jnp.einsum('nd,hd->nh', x_flat * wi, w1[i]) + b1[i])
            y = jnp.einsum('nh,dh->nd', h, w2[i]) + b2[i]
            out = jnp.where(wi > 0, y, out)
        return out.reshape(B, S, D)

    def _L1_xattn_ref(q, k, v):
        import jax, jax.numpy as jnp
        import numpy as np
        from math import sqrt
        S = q.shape[1]
        scale = 1.0 / sqrt(S)
        qn = q * scale
        kn = k * scale
        kv_mat = jnp.einsum('bsd,bse->bde', kn, v)
        out = jnp.einsum('bsd,bde->bse', qn, kv_mat)
        return out

    def _L1_ffn_ref(x, w1, b1, w2, b2, gamma, beta):
        import jax, jax.numpy as jnp
        import numpy as np
        EPS = 1e-05

        def act_quant(x):
            scale = 127.0 / jnp.clip(jnp.max(jnp.abs(x), axis=-1, keepdims=True), EPS, None)
            xq = jnp.clip(jnp.round(x * scale), -128.0, 127.0)
            return (xq, scale)

        def weight_quant(w):
            scale = 1.0 / jnp.clip(jnp.mean(jnp.abs(w)), EPS, None)
            wq = jnp.clip(jnp.round(w * scale), -1.0, 1.0)
            return (wq, scale)

        def qlinear(x, w, b):
            xq, sx = act_quant(x)
            wq, sw = weight_quant(w)
            y = jnp.einsum('bsd,hd->bsh', xq, wq) / (sx * sw)
            return y + b

        def layernorm(x, gamma, beta):
            mu = jnp.mean(x, axis=-1, keepdims=True)
            var = jnp.mean(jnp.square(x - mu), axis=-1, keepdims=True)
            return (x - mu) * jax.lax.rsqrt(var + EPS) * gamma + beta
        h = layernorm(x, gamma, beta)
        h = qlinear(h, w1, b1)
        h = jax.nn.gelu(h, approximate=False)
        out = qlinear(h, w2, b2)
        return out
    x = x + jnp.tanh(g_xattn[0]) * _L0_xattn_ref(_layernorm(x, axis=-1), ctx_1024, ctx_1024, L0_xattn_Q_weight, L0_xattn_K_weight, L0_xattn_V_weight, L0_xattn_Q_A, L0_xattn_Q_B, L0_xattn_K_A, L0_xattn_K_B, L0_xattn_V_A, L0_xattn_V_B, L0_xattn_O_weight)
    x = x + jnp.tanh(g_ffn[0]) * _L0_ffn_ref(_layernorm(x, axis=-1), L0_ffn_gate_w, L0_ffn_gate_b, L0_ffn_w1, L0_ffn_b1, L0_ffn_w2, L0_ffn_b2)
    x = x + jnp.tanh(g_xattn[1]) * _L1_xattn_ref(_layernorm(x, axis=-1), ctx_1024, ctx_1024)
    x = x + jnp.tanh(g_ffn[1]) * _L1_ffn_ref(_layernorm(x, axis=-1), L1_ffn_w1, L1_ffn_b1, L1_ffn_w2, L1_ffn_b2, L1_ffn_gamma, L1_ffn_beta)
    return x

_drawn_inputs = setup_inputs


def setup_inputs(seed=0):
    import zlib

    import numpy as np

    out = dict(_drawn_inputs(seed))
    spreads = {'g_ffn': (-1.0, 0.6),
     'L0_ffn_gate_b': (0.0, 0.1),
     'L0_ffn_b1': (0.0, 0.276),
     'L0_ffn_b2': (0.0, 0.1),
     'L1_ffn_b1': (0.0, 0.8),
     'L1_ffn_b2': (0.0, 0.8),
     'L1_ffn_gamma': (1.0, 0.6),
     'L1_ffn_beta': (0.0, 0.8)}
    factors = {'L0_xattn_Q_A': 7.679,
     'L0_xattn_Q_B': 8.0,
     'L0_xattn_K_A': 8.0,
     'L0_xattn_K_B': 7.329,
     'L0_xattn_V_A': 4.071,
     'L0_xattn_V_B': 3.924,
     'L0_ffn_w1': 3.165,
     'L1_ffn_w1': 4.416,
     'L1_ffn_w2': 4.112}
    for name, (base, spread) in spreads.items():
        noise = np.random.default_rng([zlib.crc32(name.encode()), seed]).standard_normal(out[name].shape)
        drawn = base * np.exp(spread * noise) if base else spread * noise
        out[name] = jnp.asarray(drawn.astype(out[name].dtype))
    for name, factor in factors.items():
        out[name] = (out[name] * factor).astype(out[name].dtype)
    return out
```

```python
from contextlib import ExitStack

import concourse.bass as bass
from concourse import mybir

F32 = mybir.dt.float32
BF16 = mybir.dt.bfloat16
I32 = mybir.dt.int32
U32 = mybir.dt.uint32
ALU = mybir.AluOpType
ACT = mybir.ActivationFunctionType
AX = mybir.AxisListType.X

P = 128
B, S, D = 32, 100, 256
SK = 361
R = 16
E, HID = 8, 1024
KC = D // P
HC = HID // P
KEYS = [(0, 128), (128, 128), (256, SK - 256)]
TAIL = KEYS[2][1]
NTOK = B * S
SLOTS = 32
ROW = D + 1
U = 4
NG = B // U
CTX = KC * SK + 2 * D + D
EPS = 1e-5
MAGIC = 12582912.0
FLOOR = 1.0 / 256 - 0.5


def flamingo_kernel(nc, x, ctx_pack, ctx_tail, g_x, g_f, wq, wk, wv, woT, qa, ka, va, qbT, kbT, vbT,
                    gateT, gate_b, w1m, b1m, w2m, b2m, w1l, b1l, w2l, b2l, gamma, beta, out):
    rows_dram = nc.dram_tensor("token_rows", [NTOK, ROW], F32, kind="Internal").ap()
    y_dram = nc.dram_tensor("slot_outputs", [SLOTS * P, D], F32, kind="Internal").ap()
    rows_by_batch = rows_dram.rearrange("(b p) c -> p b c", p=S)

    with ExitStack() as stack:
        def sb(name, shape, dt=F32):
            return stack.enter_context(nc.sbuf_tensor(name, shape, dt))

        def sem(name):
            return stack.enter_context(nc.semaphore(name))

        def sems(name, n):
            return [sem(f"{name}{i}") for i in range(n)]

        X = sb("X", [P, B, D])
        W1A = sb("W1A", [P, E * KC * HID])
        W2A = sb("W2A", [P, E * HC * D])
        W1 = W1A[:, :].rearrange("p (e k h) -> p e k h", e=E, k=KC)
        W2 = W2A[:, :].rearrange("p (e c d) -> p e c d", e=E, c=HC)
        WK = sb("WK", [P, 4096])

        def view(base, at, *shape, dt=F32):
            n = 1
            for d in shape:
                n *= d
            words = n if dt == F32 else n // 2
            v = base[:, at:at + words]
            if dt != F32:
                v = v.bitcast(dt)
            if len(shape) == 2:
                v = v.rearrange("p (a b) -> p a b", a=shape[0])
            if len(shape) == 3:
                v = v.rearrange("p (a b c) -> p a b c", a=shape[0], b=shape[1])
            return v

        M = sb("M", [P, KC, D])
        N = sb("N", [P, KC, D])
        w1q = sb("w1q", [P, KC, HID], BF16)
        w2q = sb("w2q", [P, HC, D], BF16)
        gate_sb = sb("gate_sb", [P, KC, E])
        gate_bc = sb("gate_bc", [P, E])
        b1_tab = sb("b1_tab", [P, E, HC])
        b2_bc = sb("b2_bc", [P, E, D])
        ident = sb("ident", [P, P])
        tri = sb("tri", [P, P], BF16)
        ones_b = sb("ones_b", [P, P], BF16)
        ones_f = sb("ones_f", [P, P])
        iota_row = sb("iota_row", [P, P])
        part_no = sb("part_no", [P, 1])
        rev = sb("rev", [P, E])
        zeros = sb("zeros", [P, 256])
        gates = sb("gates", [P, 4])
        tg = sb("tg", [P, 4])
        nhalf = sb("nhalf", [P, 1])
        eps_t = sb("eps_t", [P, 1])
        eps2_t = sb("eps2_t", [P, 1])
        opeps_t = sb("opeps_t", [P, 1])
        nmagic = sb("nmagic", [P, 1])
        wstat = sb("wstat", [P, 2])
        wmean = sb("wmean", [P, 2])
        wscale = sb("wscale", [P, 2])
        wdq = sb("wdq", [P, 2])
        st = sb("st", [P, 2, 6])
        mvA = sb("mvA", [P, U, 2])
        mvB = sb("mvB", [P, U, 2])
        veA = sb("veA", [P, U])
        veB = sb("veB", [P, U])
        rsA = sb("rsA", [P, U])
        rsB = sb("rsB", [P, U])
        negmax = sb("negmax", [P, U])
        rowsum = sb("rowsum", [P, U])
        coef = sb("coef", [P, 2])
        logit = sb("logit", [P, U, E])
        rt = sb("rt", [P, 6, U * E])
        rv = sb("rv", [P, 10, U])
        w_tab = sb("w_tab", [P, B])
        OH = sb("OH", [P, E, B], BF16)
        cum = sb("cum", [P, E * B])
        cex = sb("cex", [P, E * B])
        acc = sb("acc", [P, E * B])
        ce = sb("ce", [P, E + 1])
        sl = sb("sl", [P, 6, E])
        pos = sb("pos", [P, B])
        pos_u = sb("pos_u", [P, B], U32)
        slot_f = sb("slot_f", [P, B])
        r_f = sb("r_f", [P, B])
        le = sb("le", [1, SLOTS, E])
        ex_f = sb("ex_f", [1, 2, SLOTS])
        expert_of = sb("expert_of", [1, SLOTS], I32)
        id_b = sb("id_b", [P, SLOTS])
        tok_u = sb("tok_u", [P, SLOTS], U32)
        idx_c = sb("idx_c", [P, 2], U32)
        am = sb("am", [P, 2, 4])
        inv1 = sb("inv1", [P, 2])
        inv2 = sb("inv2", [P, 2])

        RING1 = E * HC * D - U * CTX
        ring1 = [W2A[:, RING1 + r * CTX:RING1 + (r + 1) * CTX] for r in range(U)]
        W2_EARLY = RING1 // (HC * D)
        xn = view(WK, 0, D)
        xnT = view(WK, 256, KC, S)
        qT = view(WK, 456, KC, S)
        probs = view(WK, 656, SK)
        pT = view(WK, 1024, 3, S)
        tT = view(WK, 1324, KC, S)
        xn2 = view(WK, 1536, 2, ROW)
        xn2T = view(WK, 2060, KC, S)
        EW = KC * HID
        raw_q, raw_k, raw_v, raw_o, eff_q, eff_k, eff_v = [
            view(W1A, 4 * EW + i * KC * D, KC, D) for i in range(7)]
        lowA = W1A[0:R, 3 * EW:3 * EW + 3 * D].rearrange("p (a b) -> p a b", a=3)
        lowB = W1A[0:R, 3 * EW + 3 * D:3 * EW + 6 * D].rearrange("p (a b) -> p a b", a=3)
        raw_w1 = view(W1A, 6 * EW, KC * HID)
        raw_w2 = view(W1A, 7 * EW, HC * D)
        qtmp = view(WK, 0, 2048)
        place = view(WK, 0, B, P, dt=BF16)
        carry = view(WK, 2048, B, 2 * SLOTS, dt=BF16)
        xs = view(WK, 0, 2, ROW)
        xsw = view(WK, 516, D)
        xsT = view(WK, 772, KC, P)
        hs = view(WK, 1028, HID)
        hT = view(WK, 2052, HC, P)
        ysb = view(WK, 3076, 2, D)
        b1s = view(WK, 3588, 2, HC)
        ring3 = [W1A[:, r * CTX:(r + 1) * CTX] for r in range(U)]
        at = [0]

        def work3(*shape, dt=F32):
            n = 1
            for d in shape:
                n *= d
            v = view(W2A, at[0], *shape, dt=dt)
            at[0] += (n if dt == F32 else n // 2) + 7 & ~7
            return v
        yg = work3(2, D)
        xn3 = work3(D)
        xn3T = work3(KC, S)
        s1T = work3(3, S)
        h0 = work3(D)
        xq = work3(D)
        xqT = work3(KC, S, dt=BF16)
        hb = work3(HID)
        hg = work3(HID)
        hq = work3(HID)
        hqT = work3(HC, S, dt=BF16)
        xb = work3(D)
        osb = work3(2, D)
        gamma_bc = work3(D)
        beta_bc = work3(D)
        b1_bc = work3(HID)
        b2raw_bc = work3(D)
        gb2_bc = work3(D)

        PS = stack.enter_context(nc.psum_tensor("PS", [P, 8, 512], F32))

        def bank(i, n):
            return PS[:, i, 0:n]

        consts_set = sem("consts_set")
        pool_seq = sem("pool_seq")
        setup_in = sem("setup_in")
        small_in = sem("small_in")
        lraw_in = sem("lraw_in")
        x_in0, x_in = sem("x_in0"), sem("x_in")
        ctx_in = sems("ctx_in", U)
        w_in = sem("w_in")
        low_done, eff_done, prod_done, mn_ready = sem("low_done"), sem("eff_done"), sem("prod_done"), sem("mn_ready")
        tanh_done = sem("tanh_done")
        wsum_ready, wsum_done, dve_w, quant_done = sem("wsum_ready"), sem("wsum_done"), sem("dve_w"), sem("quant_done")
        mv1_ready, mv2_ready, rstd1_ready, rstd2_ready = sem("mv1_ready"), sem("mv2_ready"), sem("rstd1_ready"), sem("rstd2_ready")
        pool_v1, pool_v2 = sem("pool_v1"), sem("pool_v2")
        stat1_seq, stat2_seq, res_seq = sem("stat1_seq"), sem("stat2_seq"), sem("res_seq")
        xn_ready, t1_done, xnT_ready = sem("xn_ready"), sem("t1_done"), sem("xnT_ready")
        q_done, q_ready, s_done, max_done, exp_done = sem("q_done"), sem("q_ready"), sem("s_done"), sem("max_done"), sem("exp_done")
        t2_done, pT_ready, tt_done, tt_ready, o_done, res_done = sem("t2_done"), sem("pT_ready"), sem("tt_done"), sem("tt_ready"), sem("o_done"), sem("res_done")
        xn2_ready, t3_done, xn2T_ready, l_done, logit_done = sem("xn2_ready"), sem("t3_done"), sem("xn2T_ready"), sem("l_done"), sem("logit_done")
        xn2_stored = sems("xn2_stored", 2)
        shifted, rexp_done, route_seq, route_done, w_stored = sem("shifted"), sem("rexp_done"), sem("route_seq"), sem("route_done"), sem("w_stored")
        count_done, plan_seq, slots_ready, place_ready, inv_done, tok_ready = sem("count_done"), sem("plan_seq"), sem("slots_ready"), sem("place_ready"), sem("inv_done"), sem("tok_ready")
        idx_set, xs_in = sem("idx_set"), sems("xs_in", 2)
        xsw_ready, x_done, xsT_ready = sem("xsw_ready"), sem("x_done"), sem("xsT_ready")
        h0_done, h1_done, h0_ready, h1_ready = sem("h0_done"), sem("h1_done"), sem("h0_ready"), sem("h1_ready")
        b1_ready, ht_done, htA_ready, htB_ready = sem("b1_ready"), sem("ht_done"), sem("htA_ready"), sem("htB_ready")
        y_done, y_ready, y_stored = sem("y_done"), sem("y_ready"), sems("y_stored", 2)
        ctx3_in, bc_in, gb2_seq = sems("ctx3_in", U), sem("bc_in"), sem("gb2_seq")
        pos_set, yg_in = sem("pos_set"), sems("yg_in", 2)
        x2_seq, mv3_ready, rstd3_ready, xn3_ready, t31_done, xn3T_ready = sem("x2_seq"), sem("mv3_ready"), sem("rstd3_ready"), sem("xn3_ready"), sem("t31_done"), sem("xn3T_ready")
        s1_done, s1T_ready, o1_done, x3_seq, mv4_ready, rstd4_ready, xb_ready = sem("s1_done"), sem("s1T_ready"), sem("o1_done"), sem("x3_seq"), sem("mv4_ready"), sem("rstd4_ready"), sem("xb_ready")
        pool_v3, pool_v4 = sem("pool_v3"), sem("pool_v4")
        xq_seq, xq_ready, tq_done, xqT_ready, f1_done, hb_ready, gelu_done = sem("xq_seq"), sem("xq_ready"), sem("tq_done"), sem("xqT_ready"), sem("f1_done"), sem("hb_ready"), sem("gelu_done")
        hq_seq, hq_ready, th_done, hqT_ready, f2_done, out_ready = sem("hq_seq"), sem("hq_ready"), sem("th_done"), sem("hqT_ready"), sem("f2_done"), sem("out_ready")
        out_stored = sems("out_stored", 2)

        carrier = {mybir.EngineType.DVE: sem("dve_carrier"), mybir.EngineType.PE: sem("pe_carrier"),
                   mybir.EngineType.Pool: sem("pool_carrier")}

        def ge(eng, s, v):
            if not (isinstance(v, int) and v <= 0):
                eng.wait_ge(s, v)

        def ge_alone(eng, s, v):
            ge(eng, s, v)
            if not isinstance(v, int):
                eng.sem_inc(carrier[eng.engine], 1)

        def behind(g, j, lag, unroll, total):
            q, r = divmod(j - lag, unroll)
            g = g + q
            if isinstance(g, int) and not 0 <= g < total // unroll:
                return None
            return g, r

        def steps(eng, step, unroll, total):
            for j in range(unroll):
                step(0, j)
            with eng.Fori(1, total // unroll) as g:
                for j in range(unroll):
                    step(g, j)
            for j in range(unroll):
                step(total // unroll, j)

        block = stack.enter_context(nc.Block())

        @block.sync
        def _(sp):
            for v, src in ((raw_q, wq), (raw_k, wk), (raw_v, wv), (raw_o, woT)):
                sp.dma_start(v, src).then_inc(setup_in, 16)
            for i, (a, b) in enumerate(((qa, qbT), (ka, kbT), (va, vbT))):
                sp.dma_start(lowA[:, i, :], a).then_inc(setup_in, 16)
                sp.dma_start(lowB[:, i, :], b).then_inc(setup_in, 16)
            sp.dma_start(X[0:S, 0:U, :], x[0:U].rearrange("b p d -> p b d")).then_inc(x_in0, 16)

            def load_ctx(buf, s_in, b):
                sp.dma_start(buf[:, 0:CTX - D], ctx_pack[b]).then_inc(s_in, 16)
                sp.dma_start(buf[0:TAIL, CTX - D:CTX], ctx_tail[b]).then_inc(s_in, 16)

            def step(g, j):
                b = 4 * g + j
                if not (isinstance(g, int) and g == NG):
                    ge(sp, tt_done, b - U + 1)
                    load_ctx(ring1[j], ctx_in[j], b)
                    if j == 0:
                        if isinstance(g, int):
                            sp.dma_start(W1A[:, 0:EW], w1m[:, 0:EW]).then_inc(w_in, 16)
                        else:
                            sp.dma_start(W1A[:, bass.ds(g * EW, EW)], w1m[:, bass.ds(g * EW, EW)]).then_inc(w_in, 16)
                it = behind(g, j, 4, U, B)
                if it:
                    bg, r = it
                    bb = 4 * bg + r
                    ge(sp, xn2_ready, bb + 1)
                    sp.dma_start(rows_by_batch[:, bb, 0:D], xn2[0:S, r % 2, 0:D]).then_inc(xn2_stored[r % 2], 16)
                    if r == U - 1:
                        ge(sp, route_done, bg + 1)
                        sp.dma_start(rows_by_batch[:, bass.ds(4 * bg, U), D:ROW],
                                     w_tab[0:S, bass.ds(4 * bg, U)].unsqueeze(2),
                                     allow_slow_non_contiguous=True).then_inc(w_stored, 16)

            for j in range(U):
                step(0, j)
                if j == 0:
                    sp.dma_start(gate_sb[:, :, :], gateT).then_inc(small_in, 16)
                    sp.dma_start(gate_bc[:, :], gate_b.partition_broadcast(P)).then_inc(small_in, 16)
                    sp.dma_start(gates[:, 0:2], g_x.partition_broadcast(P)).then_inc(small_in, 16)
                    sp.dma_start(gates[:, 2:4], g_f.partition_broadcast(P)).then_inc(small_in, 16)
                    sp.dma_start(raw_w1, w1l).then_inc(lraw_in, 16)
                    sp.dma_start(raw_w2, w2l).then_inc(lraw_in, 16)
                if j == 1:
                    sp.dma_start(X[0:S, U:B, :], x[U:B].rearrange("b p d -> p b d")).then_inc(x_in, 16)
            sp.dma_start(b1_tab[:, :, :], b1m).then_inc(w_in, 16)
            sp.dma_start(b2_bc[:, :, :], b2m.partition_broadcast(P)).then_inc(w_in, 16)
            sp.wait_ge(prod_done, 2)
            sp.wait_ge(quant_done, 1)
            for e in range(W2_EARLY):
                sp.dma_start(W2A[:, e * HC * D:(e + 1) * HC * D], w2m[:, e * HC * D:(e + 1) * HC * D]).then_inc(w_in, 16)
            with sp.Fori(1, NG) as g:
                for j in range(U):
                    step(g, j)
            sp.wait_ge(tt_done, B)
            sp.dma_start(W2A[:, W2_EARLY * HC * D:], w2m[:, W2_EARLY * HC * D:]).then_inc(w_in, 16)
            for j in range(U):
                step(NG, j)

            def store_y(g, j):
                it = behind(g, j, 2, 2, SLOTS)
                if it:
                    s = 2 * it[0] + it[1]
                    ge(sp, y_ready, s + 1)
                    sp.dma_start(y_dram[bass.ds(s * P, P), :], ysb[:, it[1], :]).then_inc(y_stored[it[1]], 16)
            steps(sp, store_y, 2, SLOTS)

            sp.wait_ge(h1_done, SLOTS)
            sp.wait_ge(y_done, SLOTS)
            for v, src in ((gamma_bc, gamma), (beta_bc, beta), (b1_bc, b1l), (b2raw_bc, b2l)):
                sp.dma_start(v, src.partition_broadcast(P)).then_inc(bc_in, 16)

            def step3(g, j):
                if not (isinstance(g, int) and g == NG):
                    b = 4 * g + j
                    ge(sp, o1_done, b - U + 1)
                    load_ctx(ring3[j], ctx3_in[j], b)
                it = behind(g, j, 4, U, B)
                if it:
                    bb = 4 * it[0] + it[1]
                    ge(sp, out_ready, bb + 1)
                    sp.dma_start(out[bb], osb[0:S, it[1] % 2, :]).then_inc(out_stored[it[1] % 2], 16)
            steps(sp, step3, U, B)
            for s in out_stored:
                sp.wait_ge(s, 16 * B // 2)
            for s in xn2_stored:
                sp.wait_ge(s, 16 * B // 2)
            for s in y_stored:
                sp.wait_ge(s, 16 * SLOTS // 2)
            sp.wait_ge(w_stored, 16 * NG)

        @block.gpsimd
        def _(pool):
            gp = nc.gpsimd
            gp.memset(ident[:, :], 0.0).then_inc(pool_seq, 1)
            gp.memset(tri[:, :], 1.0).then_inc(pool_seq, 1)
            gp.memset(ones_b[:, :], 1.0).then_inc(consts_set, 1)
            gp.memset(ones_f[:, :], 1.0).then_inc(consts_set, 1)
            gp.memset(nhalf[:, :], -0.5).then_inc(consts_set, 1)
            gp.memset(eps_t[:, :], EPS).then_inc(consts_set, 1)
            gp.memset(eps2_t[:, :], EPS * EPS).then_inc(consts_set, 1)
            gp.memset(opeps_t[:, :], 1.0 + EPS).then_inc(consts_set, 1)
            gp.memset(nmagic[:, :], -MAGIC).then_inc(consts_set, 1)
            gp.memset(zeros[:, :], 0.0).then_inc(consts_set, 1)
            gp.iota(iota_row[:, :], [[1, P]], base=0, channel_multiplier=0,
                    allow_small_or_imprecise_dtypes=True).then_inc(consts_set, 1)
            gp.iota(part_no[:, :], [[0, 1]], base=0, channel_multiplier=1,
                    allow_small_or_imprecise_dtypes=True).then_inc(consts_set, 1)
            gp.iota(rev[:, :], [[-1, E]], base=E, channel_multiplier=0,
                    allow_small_or_imprecise_dtypes=True).then_inc(consts_set, 1)
            pool.wait_ge(pool_seq, 2)
            gp.affine_select(out=ident[:, :], in_=ident[:, :], compare_op=ALU.not_equal, fill=1.0, base=0,
                             pattern=[[-1, P]], channel_multiplier=1).then_inc(consts_set, 1)
            gp.affine_select(out=tri[:, :], in_=tri[:, :], compare_op=ALU.is_gt, fill=0.0, base=0,
                             pattern=[[1, P]], channel_multiplier=-1).then_inc(consts_set, 1)
            pool.wait_ge(consts_set, CONSTS)

            def rstd(b, r, mv_ready, mv, ve, rs, ve_done, ready):
                ge(pool, mv_ready, b + 1)
                gp.tensor_tensor(ve[0:S, r:r + 1], mv[0:S, r, 1:2], eps_t[0:S, :], ALU.add).then_inc(ve_done, 1)
                ge(pool, ve_done, b + 1)
                gp.tensor_tensor(rs[0:S, r:r + 1], ve[0:S, r:r + 1], nhalf[0:S, :], ALU.pow).then_inc(ready, 1)

            def step1(g, j):
                it = behind(g, j, 3, U, B)
                if it:
                    rstd(4 * it[0] + it[1], it[1], mv2_ready, mvB, veB, rsB, pool_v2, rstd2_ready)
                it = behind(g, j, 0, U, B)
                if it:
                    rstd(4 * it[0] + it[1], it[1], mv1_ready, mvA, veA, rsA, pool_v1, rstd1_ready)
            steps(pool, step1, U, B)

            pool.wait_ge(tok_ready, 1)
            for s in xn2_stored:
                pool.wait_ge(s, 16 * B // 2)
            pool.wait_ge(w_stored, 16 * NG)

            def gather_rows(g, j):
                it = behind(g, j, 0, 2, SLOTS)
                if it:
                    s = 2 * g + j
                    ge(pool, xsw_ready, s - 1)
                    gp.tensor_copy(idx_c[:, j:j + 1], tok_u[:, bass.ds(s, 1)]).then_inc(idx_set, 1)
                    ge_alone(pool, idx_set, s + 1)
                    gp.indirect_dma_start(xs[:, j, :], None, rows_dram,
                                          bass.IndirectOffsetOnAxis(idx_c[:, j:j + 1], 0)).then_inc(xs_in[j], 16)
            steps(pool, gather_rows, 2, SLOTS)

            for s in y_stored:
                pool.wait_ge(s, 16 * SLOTS // 2)
            pool.wait_ge(gb2_seq, 1)

            def step3(g, j):
                it = behind(g, j, 0, U, B)
                if it:
                    b, r = 4 * it[0] + it[1], it[1]
                    ge(pool, x2_seq, 2 * (b - 1))
                    gp.tensor_copy(idx_c[0:S, r % 2:r % 2 + 1], pos_u[0:S, bass.ds(b, 1)]).then_inc(pos_set, 1)
                    ge_alone(pool, pos_set, b + 1)
                    gp.indirect_dma_start(yg[0:S, r % 2, :], None, y_dram,
                                          bass.IndirectOffsetOnAxis(idx_c[0:S, r % 2:r % 2 + 1], 0)).then_inc(yg_in[r % 2], 16)
                it = behind(g, j, 2, U, B)
                if it:
                    b, r = 4 * it[0] + it[1], it[1]
                    ge(pool, mv4_ready, b + 1)
                    gp.tensor_tensor(veB[0:S, r:r + 1], mvB[0:S, r, 1:2], opeps_t[0:S, :], ALU.mult).then_inc(pool_v4, 1)
                    ge(pool, pool_v4, 2 * b + 1)
                    gp.tensor_tensor(veB[0:S, r:r + 1], veB[0:S, r:r + 1], eps2_t[0:S, :], ALU.add).then_inc(pool_v4, 1)
                    ge(pool, pool_v4, 2 * b + 2)
                    gp.tensor_tensor(rsB[0:S, r:r + 1], veB[0:S, r:r + 1], nhalf[0:S, :], ALU.pow).then_inc(rstd4_ready, 1)
                it = behind(g, j, 0, U, B)
                if it:
                    rstd(4 * it[0] + it[1], it[1], mv3_ready, mvA, veA, rsA, pool_v3, rstd3_ready)
                it = behind(g, j, 3, U, B)
                if it:
                    b, r = 4 * it[0] + it[1], it[1]
                    ge(pool, out_ready, b)
                    gp.tensor_tensor(xb[0:S, :], X[0:S, b, :], gb2_bc[0:S, :], ALU.add).then_inc(xb_ready, 1)
            steps(pool, step3, U, B)

        @block.tensor
        def _(pe):
            mm = nc.tensor.matmul

            pe.wait_ge(setup_in, 16 * 10)
            for i in range(3):
                for f in range(KC):
                    last = mm(PS[:, i, f * D:(f + 1) * D], lowB[:, i, f * P:(f + 1) * P], lowA[:, i, :],
                              start=(f == 0), stop=(f == KC - 1), skip_group_check=True)
                last.then_inc(low_done, 1)
            for i, (a, b) in enumerate(((eff_q, eff_k), (eff_v, raw_o))):
                pe.wait_ge(eff_done, 2 + i)
                for c in range(KC):
                    for f in range(KC):
                        last = mm(bank(4 + 2 * i + c, D), a[:, f, c * P:(c + 1) * P], b[:, f, :], start=(f == 0), stop=(f == KC - 1))
                last.then_inc(prod_done, 1)
            pe.wait_ge(consts_set, CONSTS)
            pe.wait_ge(wsum_ready, 2)
            mm(PS[:, 3, 0:2], ones_f[:, :], wstat[:, :], start=True, stop=True).then_inc(wsum_done, 1)
            pe.wait_ge(mn_ready, 4)
            pe.wait_ge(dve_w, 1)
            pe.wait_ge(small_in, 16 * 4)

            def transposes(b_, src, n_rows, n, width=P):
                for c in range(n):
                    last = nc.tensor.transpose(PS[0:width, b_, c * n_rows:(c + 1) * n_rows],
                                               src[0:n_rows, c * P:c * P + width], ident[0:n_rows, 0:n_rows])
                return last

            def step1(g, j):
                it = behind(g, j, 2, U, B)
                if it:
                    b, r = 4 * it[0] + it[1], it[1]
                    ge(pe, xnT_ready, b + 1)
                    ge(pe, q_ready, b)
                    for c in range(KC):
                        for k in range(KC):
                            last = mm(PS[:, 1, c * S:(c + 1) * S], M[:, k, c * P:(c + 1) * P], xnT[:, k, :], start=(k == 0), stop=(k == KC - 1))
                    last.then_inc(q_done, 1)
                it = behind(g, j, 3, U, B)
                if it:
                    b, r = 4 * it[0] + it[1], it[1]
                    ge(pe, pT_ready, b + 1)
                    ge(pe, tt_ready, b)
                    for c in range(KC):
                        for k, (k0, kn) in enumerate(KEYS):
                            rows = ring1[r][0:kn, KC * SK + k * D + c * P:KC * SK + k * D + (c + 1) * P]
                            last = mm(PS[:, 4, c * S:(c + 1) * S], rows, pT[0:kn, k, :], start=(k == 0), stop=(k == 2))
                    last.then_inc(tt_done, 1)
                it = behind(g, j, 2, U, B)
                if it:
                    bg, r = it
                    b = 4 * bg + r
                    ge(pe, q_ready, b + 1)
                    ge(pe, ctx_in[r], 32 * (bg + 1))
                    ge(pe, exp_done, b)
                    for k in range(KC):
                        last = mm(PS[0:S, 2, 0:SK], qT[:, k, :], ring1[r][:, k * SK:(k + 1) * SK], start=(k == 0), stop=(k == KC - 1))
                    last.then_inc(s_done, 1)
                it = behind(g, j, 3, U, B)
                if it:
                    b, r = 4 * it[0] + it[1], it[1]
                    ge(pe, tt_ready, b + 1)
                    ge(pe, res_done, b)
                    for k in range(KC):
                        last = mm(PS[0:S, 5, 0:D], tT[:, k, :], N[:, k, :], start=(k == 0), stop=(k == KC - 1))
                    last.then_inc(o_done, 1)
                it = behind(g, j, 1, U, B)
                if it:
                    b, r = 4 * it[0] + it[1], it[1]
                    ge(pe, xn_ready, b + 1)
                    ge(pe, xnT_ready, b)
                    transposes(0, xn, S, KC).then_inc(t1_done, 1)
                it = behind(g, j, 4, U, B)
                if it:
                    b, r = 4 * it[0] + it[1], it[1]
                    ge(pe, xn2_ready, b + 1)
                    ge(pe, xn2T_ready, b)
                    transposes(6, xn2[:, r % 2, :], S, KC).then_inc(t3_done, 1)
                it = behind(g, j, 2, U, B)
                if it:
                    b, r = 4 * it[0] + it[1], it[1]
                    ge(pe, exp_done, b + 1)
                    ge(pe, pT_ready, b)
                    for k, (k0, kn) in enumerate(KEYS):
                        last = nc.tensor.transpose(PS[0:kn, 3, k * S:(k + 1) * S], probs[0:S, k0:k0 + kn], ident[0:S, 0:S])
                    last.then_inc(t2_done, 1)
                it = behind(g, j, 4, U, B)
                if it:
                    b, r = 4 * it[0] + it[1], it[1]
                    ge(pe, xn2T_ready, b + 1)
                    ge(pe, logit_done, b)
                    for k in range(KC):
                        last = mm(PS[0:S, 7, 0:E], xn2T[:, k, :], gate_sb[:, k, :], start=(k == 0), stop=(k == KC - 1))
                    last.then_inc(l_done, 1)
            steps(pe, step1, U, B)

            pe.wait_ge(route_done, NG)
            oh = OH[0:S, :, :].rearrange("p e b -> p (e b)")
            mm(PS[0:S, 0, 0:E * B], tri[0:S, 0:S], oh, start=True, stop=True)
            mm(PS[:, 1, 0:E * B], ones_b[0:S, :], oh, start=True, stop=True).then_inc(count_done, 1)
            for b in range(B):
                if b % 8 == 0:
                    pe.wait_ge(place_ready, 1 + b // 8)
                last = mm(PS[:, 2, 0:2 * SLOTS], place[0:S, b, :], carry[0:S, b, :], start=(b == 0), stop=(b == B - 1))
            last.then_inc(inv_done, 1)
            pe.wait_ge(slots_ready, 1)
            pe.wait_ge(w_in, 16 * W_DMAS)

            def step2(g, j):
                it = behind(g, j, 1, 2, SLOTS)
                if it:
                    s = 2 * it[0] + it[1]
                    ge_alone(pe, xsT_ready, s + 1)
                    e = pe.value_load(expert_of[0:1, bass.ds(s, 1)], min_val=0, max_val=E - 1)
                    for half, (ready, done) in enumerate(((h0_ready, h0_done), (h1_ready, h1_done))):
                        ge(pe, ready, s)
                        for k in range(KC):
                            last = mm(PS[:, half, :], xsT[:, k, :], W1[:, e, k, half * 512:(half + 1) * 512],
                                      start=(k == 0), stop=(k == KC - 1))
                        last.then_inc(done, 1)
                it = behind(g, j, 2, 2, SLOTS)
                if it:
                    s = 2 * it[0] + it[1]
                    ge(pe, htA_ready, s + 1)
                    ge(pe, htB_ready, s + 1)
                    ge_alone(pe, y_ready, s)
                    e = pe.value_load(expert_of[0:1, bass.ds(s, 1)], min_val=0, max_val=E - 1)
                    for c in range(HC):
                        last = mm(PS[:, 4, 0:D], hT[:, c, :], W2[:, e, c, :], start=(c == 0), stop=(c == HC - 1))
                    last.then_inc(y_done, 1)
                it = behind(g, j, 0, 2, SLOTS)
                if it:
                    s = 2 * it[0] + it[1]
                    ge(pe, xsw_ready, s + 1)
                    ge(pe, xsT_ready, s)
                    transposes(5, xsw, P, KC).then_inc(x_done, 1)
                it = behind(g, j, 1, 2, SLOTS)
                if it:
                    s = 2 * it[0] + it[1]
                    ge(pe, h0_ready, s + 1)
                    ge(pe, h1_ready, s + 1)
                    for c in range(HC):
                        last = nc.tensor.transpose(PS[:, 2 + c // 4, c % 4 * P:(c % 4 + 1) * P], hs[:, c * P:(c + 1) * P], ident[:, :])
                    last.then_inc(ht_done, 1)
            steps(pe, step2, 2, SLOTS)

            def step3(g, j):
                it = behind(g, j, 2, U, B)
                if it:
                    bg, r = it
                    b = 4 * bg + r
                    ge(pe, xn3T_ready, b + 1)
                    ge(pe, ctx3_in[r], 32 * (bg + 1))
                    ge(pe, s1T_ready, b)
                    for k, (k0, kn) in enumerate(KEYS):
                        for c in range(KC):
                            last = mm(PS[0:kn, 1, k * S:(k + 1) * S], ring3[r][:, c * SK + k0:c * SK + k0 + kn], xn3T[:, c, :],
                                      start=(c == 0), stop=(c == KC - 1))
                    last.then_inc(s1_done, 1)
                it = behind(g, j, 4, U, B)
                if it:
                    b, r = 4 * it[0] + it[1], it[1]
                    ge(pe, hq_ready, b + 1)
                    ge(pe, hqT_ready, b)
                    for c in range(HC):
                        last = nc.tensor.transpose(PS[:, 6 + c // 4, c % 4 * S:(c % 4 + 1) * S], hq[0:S, c * P:(c + 1) * P], ident[0:S, 0:S])
                    last.then_inc(th_done, 1)
                it = behind(g, j, 2, U, B)
                if it:
                    b, r = 4 * it[0] + it[1], it[1]
                    ge(pe, s1T_ready, b + 1)
                    ge(pe, x3_seq, 2 * b)
                    for k, (k0, kn) in enumerate(KEYS):
                        last = mm(PS[0:S, 2, 0:D], s1T[0:kn, k, :], ring3[r][0:kn, KC * SK + k * D:KC * SK + (k + 1) * D],
                                  start=(k == 0), stop=(k == 2))
                    last.then_inc(o1_done, 1)
                it = behind(g, j, 3, U, B)
                if it:
                    b, r = 4 * it[0] + it[1], it[1]
                    ge(pe, xq_ready, b + 1)
                    ge(pe, xn3T_ready, min(b + 2, B) if isinstance(b, int) else b + 2)
                    transposes(0, xq, S, KC).then_inc(tq_done, 1)
                it = behind(g, j, 4, U, B)
                if it:
                    b, r = 4 * it[0] + it[1], it[1]
                    ge(pe, hqT_ready, b + 1)
                    ge(pe, out_ready, b)
                    for c in range(HC):
                        last = mm(PS[0:S, 3, 0:D], hqT[:, c, :], w2q[:, c, :], start=(c == 0), stop=(c == HC - 1))
                    last.then_inc(f2_done, 1)
                it = behind(g, j, 1, U, B)
                if it:
                    b, r = 4 * it[0] + it[1], it[1]
                    ge(pe, xn3_ready, b + 1)
                    ge(pe, xqT_ready, b - 1)
                    transposes(0, xn3, S, KC).then_inc(t31_done, 1)
                it = behind(g, j, 3, U, B)
                if it:
                    b, r = 4 * it[0] + it[1], it[1]
                    ge(pe, xqT_ready, b + 1)
                    ge(pe, hb_ready, b)
                    for half in range(2):
                        for k in range(KC):
                            last = mm(PS[0:S, 4 + half, :], xqT[:, k, :], w1q[:, k, half * 512:(half + 1) * 512],
                                      start=(k == 0), stop=(k == KC - 1))
                    last.then_inc(f1_done, 1)
            steps(pe, step3, U, B)

        @block.scalar
        def _(act):
            def copy(dst, src, **kw):
                return nc.scalar.activation(dst, src, ACT.Copy, **kw)

            act.wait_ge(small_in, 16 * 4)
            nc.scalar.activation(tg[:, :], gates[:, :], ACT.Tanh).then_inc(tanh_done, 1)
            for i, (dst, scale) in enumerate(((M, D ** -0.5), (N, 1.0))):
                act.wait_ge(prod_done, i + 1)
                for c in range(KC):
                    copy(dst[:, c, :], bank(4 + 2 * i + c, D), scale=scale).then_inc(mn_ready, 1)

            def step1(g, j):
                it = behind(g, j, 2, U, B)
                if it:
                    ge(act, q_done, 4 * it[0] + it[1] + 1)
                    copy(qT[:, :, :].rearrange("p a b -> p (a b)"), bank(1, KC * S)).then_inc(q_ready, 1)
                it = behind(g, j, 3, U, B)
                if it:
                    ge(act, tt_done, 4 * it[0] + it[1] + 1)
                    copy(tT[:, :, :].rearrange("p a b -> p (a b)"), bank(4, KC * S)).then_inc(tt_ready, 1)
                it = behind(g, j, 2, U, B)
                if it:
                    r = it[1]
                    ge(act, max_done, 4 * it[0] + r + 1)
                    nc.scalar.activation(probs[0:S, :], PS[0:S, 2, 0:SK], ACT.Exp, bias=negmax[0:S, r:r + 1],
                                         accum_out=rowsum[0:S, r:r + 1]).then_inc(exp_done, 1)
                it = behind(g, j, 1, U, B)
                if it:
                    ge(act, t1_done, 4 * it[0] + it[1] + 1)
                    copy(xnT[:, :, :].rearrange("p a b -> p (a b)"), bank(0, KC * S)).then_inc(xnT_ready, 1)
                it = behind(g, j, 4, U, B)
                if it:
                    ge(act, t3_done, 4 * it[0] + it[1] + 1)
                    copy(xn2T[:, :, :].rearrange("p a b -> p (a b)"), bank(6, KC * S)).then_inc(xn2T_ready, 1)
                it = behind(g, j, 2, U, B)
                if it:
                    ge(act, t2_done, 4 * it[0] + it[1] + 1)
                    copy(pT[:, 0:2, :].rearrange("p a b -> p (a b)"), bank(3, 2 * S))
                    copy(pT[0:TAIL, 2, :], PS[0:TAIL, 3, 2 * S:3 * S]).then_inc(pT_ready, 1)
                it = behind(g, j, 4, U, B)
                if it and it[1] == U - 1:
                    ge(act, shifted, it[0] + 1)
                    nc.scalar.activation(rt[0:S, 1, :], rt[0:S, 0, :], ACT.Exp).then_inc(rexp_done, 1)
            steps(act, step1, U, B)

            def step2(g, j):
                it = behind(g, j, 1, 2, SLOTS)
                if it:
                    s = 2 * it[0] + it[1]
                    ge(act, h0_done, s + 1)
                    copy(hs[:, 0:512], bank(0, 512)).then_inc(h0_ready, 1)
                it = behind(g, j, 0, 2, SLOTS)
                if it:
                    s = 2 * it[0] + it[1]
                    ge(act, x_done, s + 1)
                    copy(xsT[:, :, :].rearrange("p a b -> p (a b)"), bank(5, D)).then_inc(xsT_ready, 1)
                it = behind(g, j, 1, 2, SLOTS)
                if it:
                    s = 2 * it[0] + it[1]
                    ge(act, ht_done, s + 1)
                    ge(act, b1_ready, s + 1)
                    for c in range(HC // 2):
                        last = nc.scalar.activation(hT[:, c, :], PS[:, 2, c * P:(c + 1) * P], ACT.Relu, bias=b1s[:, it[1], c:c + 1])
                    last.then_inc(htA_ready, 1)
            steps(act, step2, 2, SLOTS)

            def step3(g, j):
                it = behind(g, j, 2, U, B)
                if it:
                    ge(act, s1_done, 4 * it[0] + it[1] + 1)
                    copy(s1T[:, 0:2, :].rearrange("p a b -> p (a b)"), bank(1, 2 * S), scale=1.0 / S)
                    copy(s1T[0:TAIL, 2, :], PS[0:TAIL, 1, 2 * S:3 * S], scale=1.0 / S).then_inc(s1T_ready, 1)
                it = behind(g, j, 4, U, B)
                if it:
                    ge(act, th_done, 4 * it[0] + it[1] + 1)
                    nc.scalar.activation(hqT[:, :, :].rearrange("p (u c) b -> p u (c b)", u=2), PS[:, 6:8, 0:4 * S],
                                         ACT.Identity, bias=nmagic[:, :]).then_inc(hqT_ready, 1)
                it = behind(g, j, 3, U, B)
                if it:
                    ge(act, tq_done, 4 * it[0] + it[1] + 1)
                    nc.scalar.activation(xqT[:, :, :].rearrange("p a b -> p (a b)"), bank(0, KC * S),
                                         ACT.Identity, bias=nmagic[:, :]).then_inc(xqT_ready, 1)
                it = behind(g, j, 1, U, B)
                if it:
                    ge(act, t31_done, 4 * it[0] + it[1] + 1)
                    copy(xn3T[:, :, :].rearrange("p a b -> p (a b)"), bank(0, KC * S)).then_inc(xn3T_ready, 1)
                it = behind(g, j, 3, U, B)
                if it:
                    b = 4 * it[0] + it[1]
                    ge(act, hb_ready, b + 1)
                    ge(act, hq_ready, b)
                    nc.scalar.activation(hg[0:S, :], hb[0:S, :], ACT.Gelu).then_inc(gelu_done, 1)
            steps(act, step3, U, B)

        @block.vector
        def _(dve):
            v = nc.vector

            def link(ins, s, value):
                ins.then_inc(s, 1)
                dve.wait_ge(s, value)

            dve.wait_ge(setup_in, 16 * 10)
            for i, (raw, eff) in enumerate(((raw_q, eff_q), (raw_k, eff_k), (raw_v, eff_v))):
                dve.wait_ge(low_done, i + 1)
                v.tensor_tensor(eff[:, :, :].rearrange("p a b -> p (a b)"), PS[:, i, :],
                                raw[:, :, :].rearrange("p a b -> p (a b)"), ALU.add).then_inc(eff_done, 1)

            def stats(b, r, slot, mv, seq, ready):
                v.bn_stats(st[0:S, slot, :], X[0:S, b, :]).then_inc(seq, 1)
                ge_alone(dve, seq, b + 1)
                v.bn_aggr(mv[0:S, r, :], st[0:S, slot, :]).then_inc(ready, 1)

            def norm(dst, b, r, mv, rs):
                return v.tensor_scalar(dst, X[0:S, b, :], mv[0:S, r, 0:1], rs[0:S, r:r + 1], ALU.subtract, ALU.mult)

            dve.wait_ge(lraw_in, 32)
            for i, raw in enumerate((raw_w1, raw_w2)):
                v.tensor_reduce(wstat[:, i:i + 1], raw, AX, ALU.add, apply_absolute_value=True).then_inc(wsum_ready, 1)
            dve.wait_ge(wsum_done, 1)
            link(v.tensor_scalar(wmean[:, :], PS[:, 3, 0:2], 1.0 / (HID * D), EPS, ALU.mult, ALU.max), dve_w, 1)
            link(v.reciprocal(wscale[:, :], wmean[:, :]), dve_w, 2)
            n = 2
            for i, (raw, dst) in enumerate(((raw_w1, w1q[:, :, :].rearrange("p a b -> p (a b)")),
                                            (raw_w2, w2q[:, :, :].rearrange("p a b -> p (a b)")))):
                link(v.tensor_scalar(qtmp, raw, wscale[:, i:i + 1], MAGIC, ALU.mult, ALU.add), dve_w, n + 1)
                link(v.tensor_scalar(qtmp, qtmp, MAGIC + 1.0, MAGIC - 1.0, ALU.min, ALU.max), dve_w, n + 2)
                link(v.tensor_scalar(dst, qtmp, MAGIC, None, ALU.subtract), dve_w, n + 3)
                n += 3
            v.tensor_scalar(wdq[:, 0:1], wmean[:, 0:1], 1.0 / 127, None, ALU.mult)
            dve.wait_ge(tanh_done, 1)
            v.tensor_scalar(wdq[:, 1:2], wmean[:, 1:2], tg[:, 3:4], 1.0 / 127, ALU.mult, ALU.mult).then_inc(quant_done, 1)
            dve.wait_ge(small_in, 16 * 4)
            dve.wait_ge(consts_set, CONSTS)

            def bc(ap, n_):
                return ap.unsqueeze(2).broadcast_to([ap.shape[0], ap.shape[1], n_])

            def route(g):
                at_ = lambda i: g * ROUTE_LINKS + i
                L = logit[0:S, :, :]
                T = [rt[0:S, i, :].rearrange("p (b e) -> p b e", b=U) for i in range(6)]
                V = [rv[0:S, i, :] for i in range(10)]
                rev_b = rev[0:S, :].unsqueeze(1).broadcast_to([S, U, E])
                link(v.tensor_reduce(V[0], L, AX, ALU.max), route_seq, at_(1))
                v.tensor_tensor(T[0], L, bc(V[0], E), ALU.subtract).then_inc(shifted, 1)
                dve.wait_ge(rexp_done, g + 1)
                link(v.tensor_reduce(V[1], T[1], AX, ALU.add), route_seq, at_(2))
                link(v.reciprocal(V[2], V[1]), route_seq, at_(3))
                link(v.tensor_tensor(T[2], T[1], bc(V[2], E), ALU.mult), route_seq, at_(4))
                link(v.tensor_reduce(V[3], T[2], AX, ALU.max), route_seq, at_(5))
                link(v.tensor_tensor(T[3], T[2], bc(V[3], E), ALU.is_ge), route_seq, at_(6))
                link(v.tensor_tensor(T[3], T[3], rev_b, ALU.mult), route_seq, at_(7))
                link(v.tensor_reduce(V[4], T[3], AX, ALU.max), route_seq, at_(8))
                link(v.tensor_tensor(T[4], rev_b, bc(V[4], E), ALU.is_equal), route_seq, at_(9))
                link(v.scalar_tensor_tensor(T[4], T[4], -2.0, T[2], ALU.mult, ALU.add), route_seq, at_(10))
                link(v.tensor_reduce(V[5], T[4], AX, ALU.max), route_seq, at_(11))
                link(v.tensor_tensor(T[5], T[4], bc(V[5], E), ALU.is_ge), route_seq, at_(12))
                link(v.tensor_tensor(T[5], T[5], rev_b, ALU.mult), route_seq, at_(13))
                link(v.tensor_reduce(V[6], T[5], AX, ALU.max), route_seq, at_(14))
                link(v.tensor_tensor(V[7], V[6], V[4], ALU.subtract), route_seq, at_(15))
                link(v.tensor_scalar(V[8], V[5], 0.0, None, ALU.is_gt), route_seq, at_(16))
                link(v.scalar_tensor_tensor(V[7], V[7], 0.0, V[8], ALU.min, ALU.mult), route_seq, at_(17))
                link(v.tensor_tensor(V[9], V[4], V[7], ALU.add), route_seq, at_(18))
                link(v.tensor_tensor(T[5], rev_b, bc(V[9], E), ALU.is_equal), route_seq, at_(19))
                link(v.tensor_tensor(T[4], T[5], T[2], ALU.mult), route_seq, at_(20))
                v.tensor_copy(OH[0:S, :, bass.ds(U * g, U)].rearrange("p e b -> p b e"), T[5])
                v.tensor_reduce(w_tab[0:S, bass.ds(U * g, U)], T[4], AX, ALU.add).then_inc(route_done, 1)
            ROUTE_LINKS = 20

            dve.wait_ge(x_in0, 16)

            def step1(g, j):
                it = behind(g, j, 1, U, B)
                if it:
                    b, r = 4 * it[0] + it[1], it[1]
                    ge(dve, rstd1_ready, b + 1)
                    ge(dve, t1_done, b)
                    norm(xn[0:S, :], b, r, mvA, rsA).then_inc(xn_ready, 1)
                it = behind(g, j, 2, U, B)
                if it:
                    b, r = 4 * it[0] + it[1], it[1]
                    ge(dve, s_done, b + 1)
                    v.tensor_reduce(negmax[0:S, r:r + 1], PS[0:S, 2, 0:SK], AX, ALU.max, negate=True).then_inc(max_done, 1)
                it = behind(g, j, 4, U, B)
                if it:
                    bg, r = it
                    b = 4 * bg + r
                    ge(dve, rstd2_ready, b + 1)
                    ge(dve, t3_done, b)
                    ge(dve, xn2_stored[r % 2], 16 * (2 * bg + r // 2))
                    norm(xn2[0:S, r % 2, 0:D], b, r, mvB, rsB).then_inc(xn2_ready, 1)
                it = behind(g, j, 3, U, B)
                if it:
                    b, r = 4 * it[0] + it[1], it[1]
                    ge(dve, exp_done, b + 1)
                    link(v.reciprocal(coef[0:S, 0:1], rowsum[0:S, r:r + 1]), res_seq, 2 * b + 1)
                    link(v.tensor_tensor(coef[0:S, 1:2], coef[0:S, 0:1], tg[0:S, 0:1], ALU.mult), res_seq, 2 * b + 2)
                    ge(dve, o_done, b + 1)
                    v.scalar_tensor_tensor(X[0:S, b, :], PS[0:S, 5, 0:D], coef[0:S, 1:2], X[0:S, b, :],
                                           ALU.mult, ALU.add).then_inc(res_done, 1)
                    ge_alone(dve, res_done, b + 1)
                    stats(b, r, 1, mvB, stat2_seq, mv2_ready)
                it = behind(g, j, 0, U, B)
                if it:
                    b, r = 4 * it[0] + it[1], it[1]
                    stats(b, r, 0, mvA, stat1_seq, mv1_ready)
                it = behind(g, j, 4, U, B)
                if it:
                    bg, r = it
                    b = 4 * bg + r
                    ge(dve, l_done, b + 1)
                    v.tensor_tensor(logit[0:S, r, :], PS[0:S, 7, 0:E], gate_bc[0:S, :], ALU.add).then_inc(logit_done, 1)
                    if r == U - 1:
                        ge(dve, logit_done, b + 1)
                        route(bg)

            for j in range(U):
                step1(0, j)
            dve.wait_ge(x_in, 16)
            with dve.Fori(1, NG) as g:
                for j in range(U):
                    step1(g, j)
            for j in range(U):
                step1(NG, j)

            n = 0

            def then(ins):
                nonlocal n
                n += 1
                link(ins, plan_seq, n)
            EB = E * B
            dve.wait_ge(count_done, 1)
            then(v.tensor_tensor_scan(cum[:, :], PS[:, 1, 0:EB], zeros[:, 0:EB], 0.0, ALU.add, ALU.add))
            v.tensor_tensor(cex[:, :], cum[:, :], PS[:, 1, 0:EB], ALU.subtract)
            v.memset(ce[:, 0:1], 0.0)
            then(v.tensor_copy(ce[:, 1:E + 1], cum[:, B - 1:EB:B]))
            then(v.tensor_tensor(sl[:, 0, :], ce[:, 1:E + 1], ce[:, 0:E], ALU.subtract))
            then(v.tensor_scalar(sl[:, 1, :], sl[:, 0, :], 1.0 / P, (P - 1.0) / P + FLOOR, ALU.mult, ALU.add))
            then(v.tensor_scalar(sl[:, 2, :], sl[:, 1, :], MAGIC, MAGIC, ALU.add, ALU.subtract))
            then(v.tensor_tensor_scan(sl[:, 3, :], sl[:, 2, :], zeros[:, 0:E], 0.0, ALU.add, ALU.add))
            then(v.tensor_tensor(sl[:, 4, :], sl[:, 3, :], sl[:, 2, :], ALU.subtract))
            then(v.scalar_tensor_tensor(sl[:, 5, :], sl[:, 4, :], float(P), ce[:, 0:E], ALU.mult, ALU.subtract))
            then(v.tensor_tensor(acc[0:S, :], PS[0:S, 0, 0:EB], cex[0:S, :], ALU.add))
            acc3 = acc[0:S, :].rearrange("p (e b) -> p e b", e=E)
            then(v.tensor_tensor(acc3, acc3, bc(sl[0:S, 5, :], B), ALU.add))
            then(v.tensor_tensor(acc3, acc3, OH[0:S, :, :], ALU.mult))
            then(v.tensor_reduce(pos[0:S, :], acc3.rearrange("p e b -> p b e"), AX, ALU.add))
            then(v.tensor_scalar(slot_f[0:S, :], pos[0:S, :], 1.0 / P, FLOOR, ALU.mult, ALU.add))
            then(v.tensor_scalar(slot_f[0:S, :], slot_f[0:S, :], MAGIC, MAGIC, ALU.add, ALU.subtract))
            then(v.scalar_tensor_tensor(r_f[0:S, :], slot_f[0:S, :], -float(P), pos[0:S, :], ALU.mult, ALU.add))
            for s in xn2_stored:
                dve.wait_ge(s, 16 * B // 2)
            iota_s = iota_row[0:S, 0:SLOTS].unsqueeze(1).broadcast_to([S, B, SLOTS])
            then(v.tensor_tensor(carry[0:S, :, SLOTS:], bc(slot_f[0:S, :], SLOTS), iota_s, ALU.is_equal))
            then(v.tensor_scalar(carry[0:S, :, 0:SLOTS], carry[0:S, :, SLOTS:], part_no[0:S, :], None, ALU.mult))
            then(v.tensor_tensor(carry[0:S, :, SLOTS:], carry[0:S, :, SLOTS:], bc(iota_row[0:S, 0:B], SLOTS), ALU.mult))
            for c in range(4):
                v.tensor_tensor(place[0:S, 8 * c:8 * c + 8, :], bc(r_f[0:S, 8 * c:8 * c + 8], P),
                                iota_row[0:S, :].unsqueeze(1).broadcast_to([S, 8, P]), ALU.is_equal).then_inc(place_ready, 1)
            v.tensor_copy(pos_u[0:S, :], pos[0:S, :])
            then(v.tensor_tensor(le[0:1, :, :], sl[0:1, 3, :].unsqueeze(1).broadcast_to([1, SLOTS, E]),
                                 bc(iota_row[0:1, 0:SLOTS], E), ALU.is_le))
            then(v.tensor_reduce(ex_f[0:1, 0, :], le[0:1, :, :], AX, ALU.add))
            v.tensor_scalar(expert_of[0:1, :], ex_f[0:1, 0, :], E - 1.0, None, ALU.min).then_inc(slots_ready, 1)
            dve.wait_ge(inv_done, 1)
            then(v.tensor_copy(id_b[:, :], PS[:, 2, SLOTS:2 * SLOTS]))
            v.scalar_tensor_tensor(tok_u[:, :], id_b[:, :], float(S), PS[:, 2, 0:SLOTS], ALU.mult, ALU.add).then_inc(tok_ready, 1)
            dve.wait_ge(slots_ready, 1)
            dve.wait_ge(w_in, 16 * W_DMAS)

            def step2(g, j):
                it = behind(g, j, 0, 2, SLOTS)
                if it:
                    sg, r = it
                    s = 2 * sg + r
                    ge(dve, xs_in[r], 16 * (sg + 1))
                    ge(dve, x_done, s)
                    v.tensor_scalar(xsw, xs[:, r, 0:D], xs[:, r, D:ROW], None, ALU.mult).then_inc(xsw_ready, 1)
                it = behind(g, j, 1, 2, SLOTS)
                if it:
                    s = 2 * it[0] + it[1]
                    e = dve.value_load(expert_of[0:1, bass.ds(s, 1)], min_val=0, max_val=E - 1)
                    ge(dve, htA_ready, s - 1)
                    v.tensor_copy(b1s[:, it[1], :], b1_tab[:, e, :]).then_inc(b1_ready, 1)
                    ge(dve, h1_done, s + 1)
                    v.tensor_copy(hs[:, 512:1024], bank(1, 512)).then_inc(h1_ready, 1)
                it = behind(g, j, 2, 2, SLOTS)
                if it:
                    sg, r = it
                    s = 2 * sg + r
                    e = dve.value_load(expert_of[0:1, bass.ds(s, 1)], min_val=0, max_val=E - 1)
                    ge(dve, y_done, s + 1)
                    ge(dve, y_stored[r], 16 * sg)
                    v.tensor_tensor(ysb[:, r, :], PS[:, 4, 0:D], b2_bc[:, e, :], ALU.add).then_inc(y_ready, 1)
                it = behind(g, j, 1, 2, SLOTS)
                if it:
                    s = 2 * it[0] + it[1]
                    ge(dve, ht_done, s + 1)
                    ge(dve, b1_ready, s + 1)
                    for c in range(HC // 2, HC):
                        last = v.tensor_scalar(hT[:, c, :], PS[:, 3, (c - 4) * P:(c - 3) * P], b1s[:, it[1], c:c + 1], 0.0, ALU.add, ALU.max)
                    last.then_inc(htB_ready, 1)
            steps(dve, step2, 2, SLOTS)

            dve.wait_ge(bc_in, 16 * 4)
            v.tensor_scalar(gb2_bc, b2raw_bc, tg[:, 3:4], None, ALU.mult).then_inc(gb2_seq, 1)

            def quantise(src, width, r, a, b, links, done, seq, dst, ready):
                link(v.tensor_reduce(a[:, 0:1], src, AX, ALU.max, apply_absolute_value=True), seq, b * links + done + 1)
                link(v.tensor_scalar(a[:, 3:4], a[:, 0:1], EPS, None, ALU.max), seq, b * links + done + 2)
                link(v.reciprocal(a[:, 1:2], a[:, 3:4]), seq, b * links + done + 3)
                link(v.tensor_scalar(a[:, 2:3], a[:, 1:2], 127.0, None, ALU.mult), seq, b * links + done + 4)
                v.tensor_scalar(dst, src, a[:, 2:3], MAGIC, ALU.mult, ALU.add).then_inc(ready, 1)

            def step3(g, j):
                it = behind(g, j, 4, U, B)
                if it:
                    b, r = 4 * it[0] + it[1], it[1]
                    ge(dve, gelu_done, b + 1)
                    ge(dve, th_done, b)
                    quantise(hg[0:S, :], HID, r, am[0:S, 0, :], b, 5, 0, hq_seq, hq[0:S, :], hq_ready)
                    link(v.tensor_scalar(inv2[0:S, 0:1], am[0:S, 0, 3:4], wdq[0:S, 1:2], None, ALU.mult), hq_seq, 5 * b + 5)
                it = behind(g, j, 3, U, B)
                if it:
                    b, r = 4 * it[0] + it[1], it[1]
                    ge(dve, rstd4_ready, b + 1)
                    link(v.scalar_tensor_tensor(h0[0:S, :], X[0:S, b, :], mvB[0:S, r, 0:1], gamma_bc[0:S, :], ALU.subtract, ALU.mult),
                         xq_seq, 7 * b + 1)
                    link(v.scalar_tensor_tensor(h0[0:S, :], h0[0:S, :], rsB[0:S, r:r + 1], beta_bc[0:S, :], ALU.mult, ALU.add),
                         xq_seq, 7 * b + 2)
                    ge(dve, tq_done, b)
                    quantise(h0[0:S, :], D, r, am[0:S, 1, :], b, 7, 2, xq_seq, xq[0:S, :], xq_ready)
                    link(v.tensor_scalar(inv1[0:S, 0:1], am[0:S, 1, 3:4], wdq[0:S, 0:1], None, ALU.mult), xq_seq, 7 * b + 7)
                it = behind(g, j, 2, U, B)
                if it:
                    b, r = 4 * it[0] + it[1], it[1]
                    ge(dve, o1_done, b + 1)
                    v.scalar_tensor_tensor(X[0:S, b, :], PS[0:S, 2, 0:D], tg[0:S, 1:2], X[0:S, b, :], ALU.mult, ALU.add).then_inc(x3_seq, 1)
                    ge_alone(dve, x3_seq, 2 * b + 1)
                    v.bn_stats(st[0:S, 1, :], X[0:S, b, :]).then_inc(x3_seq, 1)
                    ge_alone(dve, x3_seq, 2 * b + 2)
                    v.bn_aggr(mvB[0:S, r, :], st[0:S, 1, :]).then_inc(mv4_ready, 1)
                it = behind(g, j, 1, U, B)
                if it:
                    b, r = 4 * it[0] + it[1], it[1]
                    ge(dve, rstd3_ready, b + 1)
                    ge(dve, t31_done, b)
                    norm(xn3[0:S, :], b, r, mvA, rsA).then_inc(xn3_ready, 1)
                it = behind(g, j, 0, U, B)
                if it:
                    bg, r = it
                    b = 4 * bg + r
                    ge(dve, yg_in[r % 2], 16 * (2 * bg + r // 2 + 1))
                    v.scalar_tensor_tensor(X[0:S, b, :], yg[0:S, r % 2, :], tg[0:S, 2:3], X[0:S, b, :], ALU.mult, ALU.add).then_inc(x2_seq, 1)
                    ge_alone(dve, x2_seq, 2 * b + 1)
                    v.bn_stats(st[0:S, 0, :], X[0:S, b, :]).then_inc(x2_seq, 1)
                    ge_alone(dve, x2_seq, 2 * b + 2)
                    v.bn_aggr(mvA[0:S, r, :], st[0:S, 0, :]).then_inc(mv3_ready, 1)
                it = behind(g, j, 4, U, B)
                if it:
                    bg, r = it
                    b = 4 * bg + r
                    ge(dve, f2_done, b + 1)
                    ge(dve, xb_ready, b + 1)
                    ge(dve, out_stored[r % 2], 16 * (2 * bg + r // 2))
                    v.scalar_tensor_tensor(osb[0:S, r % 2, :], PS[0:S, 3, 0:D], inv2[0:S, 0:1], xb[0:S, :],
                                           ALU.mult, ALU.add).then_inc(out_ready, 1)
                it = behind(g, j, 3, U, B)
                if it:
                    b, r = 4 * it[0] + it[1], it[1]
                    ge(dve, f1_done, b + 1)
                    ge(dve, gelu_done, b)
                    v.scalar_tensor_tensor(hb[0:S, :], PS[0:S, 4:6, :].rearrange("p a b -> p (a b)"), inv1[0:S, 0:1],
                                           b1_bc[0:S, :], ALU.mult, ALU.add).then_inc(hb_ready, 1)
            steps(dve, step3, U, B)


CONSTS = 13
W_DMAS = 2 + NG + (E * HC * D - U * CTX) // (HC * D) + 1


_OUTS = [((B, S, D), "float32")]


def kernel(**inputs):
    import numpy as np
    import concourse.bacc as bacc
    from concourse.bass_utils import run_bass_kernel_spmd

    a = {k: np.asarray(v) for k, v in inputs.items()}

    def chunked(w):
        return w.reshape(w.shape[0] // P, P, w.shape[1]).transpose(1, 0, 2)

    ctx = a["ctx_1024"]
    ctxT = ctx.transpose(0, 2, 1).reshape(B, KC, P, SK).transpose(0, 2, 1, 3).reshape(B, P, KC * SK)
    rows = ctx[:, 0:2 * P].reshape(B, 2, P, D).transpose(0, 2, 1, 3).reshape(B, P, 2 * D)
    arrays = [
        ("x", a["x"]),
        ("ctx_pack", np.concatenate([ctxT, rows], axis=2)),
        ("ctx_tail", ctx[:, 2 * P:]),
        ("g_x", a["g_xattn"]), ("g_f", a["g_ffn"]),
        ("wq", chunked(a["L0_xattn_Q_weight"])), ("wk", chunked(a["L0_xattn_K_weight"])), ("wv", chunked(a["L0_xattn_V_weight"])),
        ("woT", chunked(a["L0_xattn_O_weight"].T)),
        ("qa", a["L0_xattn_Q_A"]), ("ka", a["L0_xattn_K_A"]), ("va", a["L0_xattn_V_A"]),
        ("qbT", a["L0_xattn_Q_B"].T), ("kbT", a["L0_xattn_K_B"].T), ("vbT", a["L0_xattn_V_B"].T),
        ("gateT", chunked(a["L0_ffn_gate_w"].T)), ("gate_b", a["L0_ffn_gate_b"]),
        ("w1m", a["L0_ffn_w1"].transpose(2, 0, 1).reshape(KC, P, E, HID).transpose(1, 2, 0, 3).reshape(P, -1)),
        ("b1m", a["L0_ffn_b1"].reshape(E, HC, P).transpose(2, 0, 1)),
        ("w2m", a["L0_ffn_w2"].transpose(2, 0, 1).reshape(HC, P, E, D).transpose(1, 2, 0, 3).reshape(P, -1)),
        ("b2m", a["L0_ffn_b2"]),
        ("w1l", chunked(a["L1_ffn_w1"].T).reshape(P, -1)), ("b1l", a["L1_ffn_b1"]),
        ("w2l", chunked(a["L1_ffn_w2"].T).reshape(P, -1)), ("b2l", a["L1_ffn_b2"]),
        ("gamma", a["L1_ffn_gamma"]), ("beta", a["L1_ffn_beta"]),
    ]
    nc = bacc.Bacc("TRN2", target_bir_lowering=False, num_devices=1)
    feeds, args = {}, []
    for name, arr in arrays:
        arr = np.ascontiguousarray(arr)
        feeds[f"in_{name}"] = arr
        args.append(nc.dram_tensor(f"in_{name}", arr.shape, mybir.dt.from_np(arr.dtype), kind="ExternalInput").ap())
    for i, (shape, dtype) in enumerate(_OUTS):
        args.append(nc.dram_tensor(f"out_{i}", shape, mybir.dt.from_np(np.dtype(dtype)), kind="ExternalOutput").ap())
    flamingo_kernel(nc, *args)
    r = run_bass_kernel_spmd(nc, [feeds], core_ids=[0])
    return r.results[0]["out_0"]
```

```python
from contextlib import ExitStack

import concourse.bass as bass
from concourse import mybir

F32 = mybir.dt.float32
BF16 = mybir.dt.bfloat16
I32 = mybir.dt.int32
U32 = mybir.dt.uint32
ALU = mybir.AluOpType
ACT = mybir.ActivationFunctionType
AX = mybir.AxisListType.X

P = 128
B, S, D = 32, 100, 256
SK = 361
R = 16
E, HID = 8, 1024
KC = D // P
HC = HID // P
KEYS = [(0, 128), (128, 128), (256, SK - 256)]
TAIL = KEYS[2][1]
NTOK = B * S
SLOTS = 32
ROW = D + 1
U = 4
NG = B // U
CTX = KC * SK + 2 * D + D
EPS = 1e-5
MAGIC = 12582912.0
FLOOR = 1.0 / 256 - 0.5


def flamingo_kernel(nc, x, ctx_pack, ctx_tail, g_x, g_f, wq, wk, wv, woT, qa, ka, va, qbT, kbT, vbT,
                    gateT, gate_b, w1m, b1m, w2m, b2m, w1l, b1l, w2l, b2l, gamma, beta, out):
    rows_dram = nc.dram_tensor("token_rows", [NTOK, ROW], F32, kind="Internal").ap()
    y_dram = nc.dram_tensor("slot_outputs", [SLOTS * P, D], F32, kind="Internal").ap()
    rows_by_batch = rows_dram.rearrange("(b p) c -> p b c", p=S)

    with ExitStack() as stack:
        def sb(name, shape, dt=F32):
            return stack.enter_context(nc.sbuf_tensor(name, shape, dt))

        def sem(name):
            return stack.enter_context(nc.semaphore(name))

        def sems(name, n):
            return [sem(f"{name}{i}") for i in range(n)]

        X = sb("X", [P, B, D])
        W1A = sb("W1A", [P, E * KC * HID])
        W2A = sb("W2A", [P, E * HC * D])
        W1 = W1A[:, :].rearrange("p (e k h) -> p e k h", e=E, k=KC)
        W2 = W2A[:, :].rearrange("p (e c d) -> p e c d", e=E, c=HC)
        WK = sb("WK", [P, 4096])

        def view(base, at, *shape, dt=F32):
            n = 1
            for d in shape:
                n *= d
            words = n if dt == F32 else n // 2
            v = base[:, at:at + words]
            if dt != F32:
                v = v.bitcast(dt)
            if len(shape) == 2:
                v = v.rearrange("p (a b) -> p a b", a=shape[0])
            if len(shape) == 3:
                v = v.rearrange("p (a b c) -> p a b c", a=shape[0], b=shape[1])
            return v

        M = sb("M", [P, KC, D])
        N = sb("N", [P, KC, D])
        w1q = sb("w1q", [P, KC, HID], BF16)
        w2q = sb("w2q", [P, HC, D], BF16)
        gate_sb = sb("gate_sb", [P, KC, E])
        gate_bc = sb("gate_bc", [P, E])
        b1_tab = sb("b1_tab", [P, E, HC])
        b2_bc = sb("b2_bc", [P, E, D])
        ident = sb("ident", [P, P])
        tri = sb("tri", [P, P], BF16)
        ones_b = sb("ones_b", [P, P], BF16)
        ones_f = sb("ones_f", [P, P])
        iota_row = sb("iota_row", [P, P])
        part_no = sb("part_no", [P, 1])
        batch_no = sb("batch_no", [P, B, SLOTS], BF16)
        rev = sb("rev", [P, E])
        zeros = sb("zeros", [P, 256])
        gates = sb("gates", [P, 4])
        tg = sb("tg", [P, 4])
        nhalf = sb("nhalf", [P, 1])
        eps_t = sb("eps_t", [P, 1])
        nmagic = sb("nmagic", [P, 1])
        pmagic = sb("pmagic", [P, 1])
        wstat = sb("wstat", [P, 2])
        wmean = sb("wmean", [P, 2])
        wscale = sb("wscale", [P, 2])
        wdq = sb("wdq", [P, 2])
        st = sb("st", [P, 2, 6])
        mvA = sb("mvA", [P, U, 2])
        mvB = sb("mvB", [P, U, 2])
        veA = sb("veA", [P, U])
        veB = sb("veB", [P, U])
        rsA = sb("rsA", [P, U])
        rsB = sb("rsB", [P, U])
        negmax = sb("negmax", [P, U])
        rowsum = sb("rowsum", [P, U])
        rsum_inv = sb("rsum_inv", [P, U])
        coef = sb("coef", [P, U])
        logit = sb("logit", [P, U, E])
        rt = sb("rt", [P, 6, U * E])
        rv = sb("rv", [P, 10, U])
        w_tab = sb("w_tab", [P, B])
        OH = sb("OH", [P, E, B], BF16)
        ce = sb("ce", [P, E + 1])
        sl = sb("sl", [P, 6, E])
        pos = sb("pos", [P, B])
        pos_u = sb("pos_u", [P, B], U32)
        slot_f = sb("slot_f", [P, B])
        r_f = sb("r_f", [P, B])
        ex_f = sb("ex_f", [1, 2, SLOTS])
        expert_of = sb("expert_of", [1, SLOTS], I32)
        id_b = sb("id_b", [P, SLOTS])
        tok_u = sb("tok_u", [P, SLOTS], U32)
        idx_c = sb("idx_c", [P, 2], U32)
        nbA = sb("nbA", [P, U])
        amh = sb("amh", [P, U, 3])
        amx = sb("amx", [P, U, 3])
        inv1 = sb("inv1", [P, U])
        inv2 = sb("inv2", [P, U])

        RING1 = E * HC * D - U * CTX
        ring1 = [W2A[:, RING1 + r * CTX:RING1 + (r + 1) * CTX] for r in range(U)]
        W2_EARLY = RING1 // (HC * D)
        xn = view(WK, 0, D)
        xnT = view(WK, 256, KC, S)
        qT = view(WK, 456, KC, S)
        probs = view(WK, 656, SK)
        pT = view(WK, 1024, 3, S)
        tT = view(WK, 1324, KC, S)
        xn2 = view(WK, 1536, 2, ROW)
        xn2T = view(WK, 2060, KC, S)
        EW = KC * HID
        raw_q, raw_k, raw_v, raw_o, eff_q, eff_k, eff_v = [
            view(W1A, 4 * EW + i * KC * D, KC, D) for i in range(7)]
        lowA = W1A[0:R, 3 * EW:3 * EW + 3 * D].rearrange("p (a b) -> p a b", a=3)
        lowB = W1A[0:R, 3 * EW + 3 * D:3 * EW + 6 * D].rearrange("p (a b) -> p a b", a=3)
        raw_w1 = view(W1A, 6 * EW, KC * HID)
        raw_w2 = view(W1A, 7 * EW, HC * D)
        place = view(WK, 0, B, P, dt=BF16)
        carry = view(WK, 2048, B, 2 * SLOTS, dt=BF16)
        cum, cex, acc = [view(WK, 3072 + i * E * B, E * B) for i in range(3)]
        le = view(WK, 3072 + 3 * E * B, SLOTS, E)
        xs = view(WK, 0, 2, ROW)
        xsw = view(WK, 516, D)
        xsT = view(WK, 772, KC, P)
        hs = view(WK, 1028, HID)
        hT = view(WK, 2052, HC, P)
        ysb = view(WK, 3076, 2, D)
        b1s = view(WK, 3588, 2, HC)
        ring3 = [W1A[:, r * CTX:(r + 1) * CTX] for r in range(U)]
        at = [0]

        def work3(*shape, dt=F32):
            n = 1
            for d in shape:
                n *= d
            v = view(W2A, at[0], *shape, dt=dt)
            at[0] += (n if dt == F32 else n // 2) + 7 & ~7
            return v
        yg = work3(2, D)
        xn3 = work3(D)
        xn3T = work3(KC, S)
        s1T = work3(3, S)
        h0 = work3(D)
        xq = work3(D)
        xqT = work3(KC, S, dt=BF16)
        hb = work3(HID)
        hg = work3(2, HID)
        hq = work3(HID)
        hqT = work3(HC, S, dt=BF16)
        osb = work3(2, D)
        gamma_bc = work3(D)
        beta_bc = work3(D)
        b1_bc = work3(HID)
        b2raw_bc = work3(D)
        gb2_bc = work3(D)

        PS = stack.enter_context(nc.psum_tensor("PS", [P, 8, 512], F32))

        def bank(i, n):
            return PS[:, i, 0:n]

        consts_set = sem("consts_set")
        pool_seq = sem("pool_seq")
        setup_in, low_in, b2_in = sem("setup_in"), sem("low_in"), sem("b2_in")
        small_in = sem("small_in")
        lraw_in = sem("lraw_in")
        x_in0, x_in = sem("x_in0"), sem("x_in")
        ctx_in = sems("ctx_in", U)
        w_in = sem("w_in")
        low_done, eff_done, prod_done, mn_ready = sem("low_done"), sem("eff_done"), sem("prod_done"), sem("mn_ready")
        tanh_done = sem("tanh_done")
        wsum_ready, wsum_done, wround_done = sem("wsum_ready"), sem("wsum_done"), sem("wround_done")
        dve_w, quant_done, b2_scaled = sem("dve_w"), sem("quant_done"), sem("b2_scaled")
        mv1_ready, mv2_ready, rstd1_ready, rstd2_ready = sem("mv1_ready"), sem("mv2_ready"), sem("rstd1_ready"), sem("rstd2_ready")
        pool_v1, pool_v2 = sem("pool_v1"), sem("pool_v2")
        stat1_seq, stat2_seq, coef_seq = sem("stat1_seq"), sem("stat2_seq"), sem("coef_seq")
        xn_ready, t1_done, xnT_ready = sem("xn_ready"), sem("t1_done"), sem("xnT_ready")
        q_done, q_ready, s_done, max_done, exp_done = sem("q_done"), sem("q_ready"), sem("s_done"), sem("max_done"), sem("exp_done")
        t2_done, pT_ready, tt_done, tt_ready, o_done, res_done = sem("t2_done"), sem("pT_ready"), sem("tt_done"), sem("tt_ready"), sem("o_done"), sem("res_done")
        xn2_ready, t3_done, xn2T_ready, l_done, logit_done = sem("xn2_ready"), sem("t3_done"), sem("xn2T_ready"), sem("l_done"), sem("logit_done")
        xn2_stored = sems("xn2_stored", 2)
        rexp_done, route_seq, route_done, w_stored = sem("rexp_done"), sem("route_seq"), sem("route_done"), sem("w_stored")
        count_done, plan_seq, slots_ready, place_ready, inv_done, tok_ready = sem("count_done"), sem("plan_seq"), sem("slots_ready"), sem("place_ready"), sem("inv_done"), sem("tok_ready")
        idx_set, xs_in = sem("idx_set"), sems("xs_in", 2)
        xsw_ready, x_done, xsT_ready = sem("xsw_ready"), sem("x_done"), sem("xsT_ready")
        h0_done, h1_done, h_ready = sem("h0_done"), sem("h1_done"), sem("h_ready")
        b1_ready, ht_done, hT_ready = sem("b1_ready"), sem("ht_done"), sem("hT_ready")
        y_done, y_ready, y_stored = sem("y_done"), sem("y_ready"), sems("y_stored", 2)
        ctx3_in, bc_in, gb2_seq = sems("ctx3_in", U), sem("bc_in"), sem("gb2_seq")
        pos_set, yg_in = sem("pos_set"), sems("yg_in", 2)
        x2_ready, stat3_seq, mv3_ready, rstd3_ready, nb3_ready = sem("x2_ready"), sem("stat3_seq"), sem("mv3_ready"), sem("rstd3_ready"), sem("nb3_ready")
        xn3_ready, t31_done, xn3T_ready = sem("xn3_ready"), sem("t31_done"), sem("xn3T_ready")
        s1_done, s1T_ready, o1_done, x3_seq, mv4_ready, rstd4_ready, xb_ready = sem("s1_done"), sem("s1T_ready"), sem("o1_done"), sem("x3_seq"), sem("mv4_ready"), sem("rstd4_ready"), sem("xb_ready")
        pool_v3, pool_v4 = sem("pool_v3"), sem("pool_v4")
        x_seq, h_seq = sem("x_seq"), sem("h_seq")
        xq_ready, tq_done, xqT_ready, f1_done, hb_ready, gelu_done = sem("xq_ready"), sem("tq_done"), sem("xqT_ready"), sem("f1_done"), sem("hb_ready"), sem("gelu_done")
        hq_ready, th_done, hqT_ready, f2_done, out_ready = sem("hq_ready"), sem("th_done"), sem("hqT_ready"), sem("f2_done"), sem("out_ready")
        out_stored = sems("out_stored", 2)

        carrier = {mybir.EngineType.DVE: sem("dve_carrier"), mybir.EngineType.PE: sem("pe_carrier"),
                   mybir.EngineType.Pool: sem("pool_carrier"), mybir.EngineType.Activation: sem("act_carrier")}

        def ge(eng, s, v):
            if not (isinstance(v, int) and v <= 0):
                eng.wait_ge(s, v)

        def ge_alone(eng, s, v):
            ge(eng, s, v)
            if not isinstance(v, int):
                eng.sem_inc(carrier[eng.engine], 1)

        def behind(g, j, lag, unroll, total):
            q, r = divmod(j - lag, unroll)
            g = g + q
            if isinstance(g, int) and not 0 <= g < total // unroll:
                return None
            return unroll * g + r, g, r

        def steps(eng, step, unroll, total, ends=1):
            for g in range(ends):
                for j in range(unroll):
                    step(g, j)
            with eng.Fori(ends, total // unroll) as g:
                for j in range(unroll):
                    step(g, j)
            for g in range(total // unroll, total // unroll + ends):
                for j in range(unroll):
                    step(g, j)

        block = stack.enter_context(nc.Block())

        @block.sync
        def _(sp):
            for v, src in ((raw_q, wq), (raw_k, wk), (raw_v, wv), (raw_o, woT)):
                sp.dma_start(v, src).then_inc(setup_in, 16)
            sp.dma_start(X[0:S, 0:U, :], x[0:U].rearrange("b p d -> p b d")).then_inc(x_in0, 16)

            def load_ctx(buf, s_in, b):
                sp.dma_start(buf[:, 0:CTX - D], ctx_pack[b]).then_inc(s_in, 16)
                sp.dma_start(buf[0:TAIL, CTX - D:CTX], ctx_tail[b]).then_inc(s_in, 16)

            def step(g, j):
                if it := behind(g, j, 0, U, B):
                    b, _, r = it
                    ge(sp, tt_done, b - U + 1)
                    load_ctx(ring1[r], ctx_in[r], b)
                    if j == 0:
                        sp.dma_start(W1A[:, bass.ds(g * EW, EW)], w1m[:, bass.ds(g * EW, EW)]).then_inc(w_in, 16)
                if it := behind(g, j, 4, U, B):
                    b, bg, r = it
                    ge(sp, xn2_ready, b + 1)
                    sp.dma_start(rows_by_batch[:, b, 0:D], xn2[0:S, r % 2, 0:D]).then_inc(xn2_stored[r % 2], 16)
                if it := behind(g, j, 8, U, B):
                    if it[2] == U - 1:
                        store_weights(it[1])

            def store_weights(bg):
                ge(sp, route_done, bg + 1)
                sp.dma_start(rows_by_batch[:, bass.ds(U * bg, U), D:ROW], w_tab[0:S, bass.ds(U * bg, U)].unsqueeze(2),
                             allow_slow_non_contiguous=True).then_inc(w_stored, 16)

            for g in range(2):
                for j in range(U):
                    step(g, j)
                    if (g, j) == (0, 1):
                        sp.dma_start(X[0:S, U:B, :], x[U:B].rearrange("b p d -> p b d")).then_inc(x_in, 16)
                    if (g, j) == (0, 2):
                        sp.dma_start(raw_w1, w1l).then_inc(lraw_in, 16)
                        sp.dma_start(raw_w2, w2l).then_inc(lraw_in, 16)
            sp.dma_start(b1_tab[:, :, :], b1m).then_inc(w_in, 16)
            sp.wait_ge(prod_done, 2)
            sp.wait_ge(quant_done, 1)
            for e in range(W2_EARLY):
                sp.dma_start(W2A[:, e * HC * D:(e + 1) * HC * D], w2m[:, e * HC * D:(e + 1) * HC * D]).then_inc(w_in, 16)
            with sp.Fori(2, NG) as g:
                for j in range(U):
                    step(g, j)
            for j in range(U):
                step(NG, j)
            sp.wait_ge(tt_done, B)
            sp.dma_start(W2A[:, W2_EARLY * HC * D:], w2m[:, W2_EARLY * HC * D:]).then_inc(w_in, 16)
            step(NG + 1, 0)
            store_weights(NG - 1)

            def store_y(g, j):
                if it := behind(g, j, 2, 2, SLOTS):
                    s, _, r = it
                    ge(sp, y_ready, s + 1)
                    sp.dma_start(y_dram[bass.ds(s * P, P), :], ysb[:, r, :]).then_inc(y_stored[r], 16)
            steps(sp, store_y, 2, SLOTS)

            sp.wait_ge(h1_done, SLOTS)

            def step3(g, j):
                if it := behind(g, j, 0, U, B):
                    b, _, r = it
                    ge(sp, o1_done, b - U + 1)
                    load_ctx(ring3[r], ctx3_in[r], b)
                if it := behind(g, j, 6, U, B):
                    b, _, r = it
                    ge(sp, out_ready, b + 1)
                    sp.dma_start(out[b], osb[0:S, r % 2, :]).then_inc(out_stored[r % 2], 16)
                if isinstance(g, int) and (g, j) == (0, U - 1):
                    sp.wait_ge(y_done, SLOTS)
                    for v, src in ((gamma_bc, gamma), (beta_bc, beta), (b1_bc, b1l), (b2raw_bc, b2l)):
                        sp.dma_start(v, src.partition_broadcast(P)).then_inc(bc_in, 16)
            steps(sp, step3, U, B, ends=2)
            for s in out_stored:
                sp.wait_ge(s, 16 * B // 2)
            for s in xn2_stored:
                sp.wait_ge(s, 16 * B // 2)
            for s in y_stored:
                sp.wait_ge(s, 16 * SLOTS // 2)
            sp.wait_ge(w_stored, 16 * NG)

        @block.gpsimd
        def _(pool):
            gp = nc.gpsimd
            gp.memset(ident[:, :], 0.0).then_inc(pool_seq, 1)
            gp.memset(tri[:, :], 1.0).then_inc(pool_seq, 1)
            gp.memset(nhalf[:, :], -0.5).then_inc(consts_set, 1)
            gp.memset(eps_t[:, :], EPS).then_inc(consts_set, 1)
            pool.wait_ge(pool_seq, 2)
            gp.affine_select(out=ident[:, :], in_=ident[:, :], compare_op=ALU.not_equal, fill=1.0, base=0,
                             pattern=[[-1, P]], channel_multiplier=1).then_inc(consts_set, 1)
            gp.affine_select(out=tri[:, :], in_=tri[:, :], compare_op=ALU.is_gt, fill=0.0, base=0,
                             pattern=[[1, P]], channel_multiplier=-1).then_inc(consts_set, 1)
            gp.memset(ones_b[:, :], 1.0).then_inc(consts_set, 1)
            gp.memset(ones_f[:, :], 1.0).then_inc(consts_set, 1)
            gp.memset(nmagic[:, :], -MAGIC).then_inc(consts_set, 1)
            gp.memset(pmagic[:, :], MAGIC).then_inc(consts_set, 1)
            gp.memset(zeros[:, :], 0.0).then_inc(consts_set, 1)
            gp.iota(iota_row[:, :], [[1, P]], base=0, channel_multiplier=0,
                    allow_small_or_imprecise_dtypes=True).then_inc(consts_set, 1)
            gp.iota(batch_no[:, :, :], [[1, B], [0, SLOTS]], base=0, channel_multiplier=0,
                    allow_small_or_imprecise_dtypes=True).then_inc(consts_set, 1)
            gp.iota(part_no[:, :], [[0, 1]], base=0, channel_multiplier=1,
                    allow_small_or_imprecise_dtypes=True).then_inc(consts_set, 1)
            gp.iota(rev[:, :], [[-1, E]], base=E, channel_multiplier=0,
                    allow_small_or_imprecise_dtypes=True).then_inc(consts_set, 1)
            pool.wait_ge(consts_set, CONSTS)

            def rstd(b, r, mv_ready, mv, ve, rs, ve_done, ready):
                ge(pool, mv_ready, b + 1)
                gp.tensor_tensor(ve[0:S, r:r + 1], mv[0:S, r, 1:2], eps_t[0:S, :], ALU.add).then_inc(ve_done, 1)
                ge(pool, ve_done, b + 1)
                gp.tensor_tensor(rs[0:S, r:r + 1], ve[0:S, r:r + 1], nhalf[0:S, :], ALU.pow).then_inc(ready, 1)

            def step1(g, j):
                if it := behind(g, j, 0, U, B):
                    rstd(it[0], it[2], mv1_ready, mvA, veA, rsA, pool_v1, rstd1_ready)
                if it := behind(g, j, 3, U, B):
                    rstd(it[0], it[2], mv2_ready, mvB, veB, rsB, pool_v2, rstd2_ready)
            steps(pool, step1, U, B)

            pool.wait_ge(tok_ready, 1)
            for s in xn2_stored:
                pool.wait_ge(s, 16 * B // 2)
            pool.wait_ge(w_stored, 16 * NG)

            def gather_rows(g, j):
                if it := behind(g, j, 0, 2, SLOTS):
                    s, _, r = it
                    ge(pool, xsw_ready, s - 1)
                    gp.tensor_copy(idx_c[:, r:r + 1], tok_u[:, bass.ds(s, 1)]).then_inc(idx_set, 1)
                    ge_alone(pool, idx_set, s + 1)
                    gp.indirect_dma_start(xs[:, r, :], None, rows_dram,
                                          bass.IndirectOffsetOnAxis(idx_c[:, r:r + 1], 0)).then_inc(xs_in[r], 16)
            steps(pool, gather_rows, 2, SLOTS)

            for s in y_stored:
                pool.wait_ge(s, 16 * SLOTS // 2)

            def step3(g, j):
                if it := behind(g, j, 0, U, B):
                    b, _, r = it
                    ge(pool, x2_ready, b - 1)
                    gp.tensor_copy(idx_c[0:S, r % 2:r % 2 + 1], pos_u[0:S, bass.ds(b, 1)]).then_inc(pos_set, 1)
                    ge_alone(pool, pos_set, b + 1)
                    gp.indirect_dma_start(yg[0:S, r % 2, :], None, y_dram,
                                          bass.IndirectOffsetOnAxis(idx_c[0:S, r % 2:r % 2 + 1], 0)).then_inc(yg_in[r % 2], 16)
                if it := behind(g, j, 2, U, B):
                    b, _, r = it
                    ge_alone(pool, mv4_ready, b + 1)
                    gp.tensor_scalar(veB[0:S, r:r + 1], mvB[0:S, r, 1:2], 1.0 + EPS, EPS * EPS, ALU.mult, ALU.add).then_inc(pool_v4, 1)
                    ge(pool, pool_v4, b + 1)
                    gp.tensor_tensor(rsB[0:S, r:r + 1], veB[0:S, r:r + 1], nhalf[0:S, :], ALU.pow).then_inc(rstd4_ready, 1)
                    if isinstance(b, int) and b == 0:
                        pool.wait_ge(gb2_seq, 1)
                    ge_alone(pool, x_seq, 6 * b + 1)
                    gp.tensor_tensor(X[0:S, b, :], X[0:S, b, :], gb2_bc[0:S, :], ALU.add).then_inc(xb_ready, 1)
                if it := behind(g, j, 0, U, B):
                    b, bg, r = it
                    ge_alone(pool, yg_in[r % 2], 16 * (2 * bg + r // 2 + 1))
                    gp.tensor_tensor(X[0:S, b, :], X[0:S, b, :], yg[0:S, r % 2, :], ALU.add).then_inc(x2_ready, 1)
                    rstd(b, r, mv3_ready, mvA, veA, rsA, pool_v3, rstd3_ready)
                    ge_alone(pool, rstd3_ready, b + 1)
                    gp.tensor_scalar(nbA[0:S, r:r + 1], rsA[0:S, r:r + 1], mvA[0:S, r, 0:1], -1.0, ALU.mult, ALU.mult).then_inc(nb3_ready, 1)
            steps(pool, step3, U, B, ends=2)

        @block.tensor
        def _(pe):
            mm = nc.tensor.matmul

            pe.wait_ge(low_in, 16 * 6)
            for i in range(3):
                for f in range(KC):
                    last = mm(PS[:, i, f * D:(f + 1) * D], lowB[:, i, f * P:(f + 1) * P], lowA[:, i, :],
                              start=(f == 0), stop=(f == KC - 1), skip_group_check=True)
                last.then_inc(low_done, 1)
            pe.wait_ge(setup_in, 16 * 4)
            for i, (a, b) in enumerate(((eff_q, eff_k), (eff_v, raw_o))):
                pe.wait_ge(eff_done, 2 + i)
                for c in range(KC):
                    for f in range(KC):
                        last = mm(bank(4 + 2 * i + c, D), a[:, f, c * P:(c + 1) * P], b[:, f, :], start=(f == 0), stop=(f == KC - 1))
                last.then_inc(prod_done, 1)
            pe.wait_ge(consts_set, CONSTS)
            pe.wait_ge(mn_ready, 4)
            pe.wait_ge(small_in, 16 * 4)

            def transposes(b_, src, n_rows, n):
                for c in range(n):
                    last = nc.tensor.transpose(PS[:, b_, c * n_rows:(c + 1) * n_rows],
                                               src[0:n_rows, c * P:(c + 1) * P], ident[0:n_rows, 0:n_rows])
                return last

            def step1(g, j):
                if it := behind(g, j, 1, U, B):
                    b, _, r = it
                    ge(pe, xnT_ready, b + 1)
                    for c in range(KC):
                        for k in range(KC):
                            last = mm(PS[:, 1, c * S:(c + 1) * S], M[:, k, c * P:(c + 1) * P], xnT[:, k, :], start=(k == 0), stop=(k == KC - 1))
                    last.then_inc(q_done, 1)
                if it := behind(g, j, 2, U, B):
                    b, _, r = it
                    ge(pe, exp_done, b + 1)
                    for k, (k0, kn) in enumerate(KEYS):
                        last = nc.tensor.transpose(PS[0:kn, 3, k * S:(k + 1) * S], probs[0:S, k0:k0 + kn], ident[0:S, 0:S])
                    last.then_inc(t2_done, 1)
                if it := behind(g, j, 3, U, B):
                    b, _, r = it
                    ge(pe, tt_ready, b + 1)
                    ge(pe, res_done, b)
                    for k in range(KC):
                        last = mm(PS[0:S, 5, 0:D], tT[:, k, :], N[:, k, :], start=(k == 0), stop=(k == KC - 1))
                    last.then_inc(o_done, 1)
                if it := behind(g, j, 4, U, B):
                    b, _, r = it
                    ge(pe, xn2T_ready, b + 1)
                    if isinstance(b, int) and b == 3:
                        pe.wait_ge(dve_w, 1)
                    for k in range(KC):
                        last = mm(PS[0:S, 7, 0:E], xn2T[:, k, :], gate_sb[:, k, :], start=(k == 0), stop=(k == KC - 1))
                    last.then_inc(l_done, 1)
                if it := behind(g, j, 0, U, B):
                    b, _, r = it
                    ge(pe, xn_ready, b + 1)
                    transposes(0, xn, S, KC).then_inc(t1_done, 1)
                if it := behind(g, j, 1, U, B):
                    b, bg, r = it
                    ge(pe, q_ready, b + 1)
                    ge(pe, ctx_in[r], 32 * (bg + 1))
                    for k in range(KC):
                        last = mm(PS[0:S, 2, 0:SK], qT[:, k, :], ring1[r][:, k * SK:(k + 1) * SK], start=(k == 0), stop=(k == KC - 1))
                    last.then_inc(s_done, 1)
                if it := behind(g, j, 2, U, B):
                    b, _, r = it
                    ge(pe, pT_ready, b + 1)
                    for c in range(KC):
                        for k, (k0, kn) in enumerate(KEYS):
                            rows = ring1[r][0:kn, KC * SK + k * D + c * P:KC * SK + k * D + (c + 1) * P]
                            last = mm(PS[:, 4, c * S:(c + 1) * S], rows, pT[0:kn, k, :], start=(k == 0), stop=(k == 2))
                    last.then_inc(tt_done, 1)
                if it := behind(g, j, 3, U, B):
                    b, _, r = it
                    ge(pe, xn2_ready, b + 1)
                    transposes(6, xn2[:, r % 2, :], S, KC).then_inc(t3_done, 1)
                if isinstance(g, int) and (g, j) == (1, 2):
                    pe.wait_ge(wsum_ready, 2)
                    pe.wait_ge(logit_done, 3)
                    mm(PS[:, 7, 64:66], ones_f[:, :], wstat[:, :], start=True, stop=True).then_inc(wsum_done, 1)
            for g in range(2):
                for j in range(U):
                    step1(g, j)
            with pe.Fori(2, NG) as g:
                for j in range(U):
                    step1(g, j)
            for g in range(NG, NG + 2):
                for j in range(U):
                    step1(g, j)

            pe.wait_ge(route_done, NG)
            oh = OH[0:S, :, :].rearrange("p e b -> p (e b)")
            mm(PS[:, 1, 0:E * B], ones_b[0:S, :], oh, start=True, stop=True).then_inc(count_done, 1)
            mm(PS[0:S, 0, 0:E * B], tri[0:S, 0:S], oh, start=True, stop=True).then_inc(count_done, 1)
            for b in range(B):
                if b % 8 == 0:
                    pe.wait_ge(place_ready, 1 + b // 8)
                last = mm(PS[:, 2, 0:2 * SLOTS], place[0:S, b, :], carry[0:S, b, :], start=(b == 0), stop=(b == B - 1))
            last.then_inc(inv_done, 1)
            pe.wait_ge(slots_ready, 1)
            pe.wait_ge(w_in, 16 * W_DMAS)

            def step2(g, j):
                if it := behind(g, j, 1, 2, SLOTS):
                    s, _, r = it
                    e = pe.value_load(expert_of[0:1, bass.ds(s, 1)], min_val=0, max_val=E - 1)
                    ge(pe, xsT_ready, s + 1)
                    for half, done in enumerate((h0_done, h1_done)):
                        for k in range(KC):
                            last = mm(PS[:, half, :], xsT[:, k, :], W1[:, e, k, half * 512:(half + 1) * 512],
                                      start=(k == 0), stop=(k == KC - 1))
                        last.then_inc(done, 1)
                if it := behind(g, j, 2, 2, SLOTS):
                    s, _, r = it
                    e = pe.value_load(expert_of[0:1, bass.ds(s, 1)], min_val=0, max_val=E - 1)
                    ge(pe, hT_ready, 2 * (s + 1))
                    for c in range(HC):
                        last = mm(PS[:, 4, 0:D], hT[:, c, :], W2[:, e, c, :], start=(c == 0), stop=(c == HC - 1))
                    last.then_inc(y_done, 1)
                if it := behind(g, j, 0, 2, SLOTS):
                    s, _, r = it
                    ge(pe, xsw_ready, s + 1)
                    transposes(5, xsw, P, KC).then_inc(x_done, 1)
                if it := behind(g, j, 1, 2, SLOTS):
                    s, _, r = it
                    ge(pe, h_ready, 2 * (s + 1))
                    for c in range(HC):
                        last = nc.tensor.transpose(PS[:, 2 + c // 4, c % 4 * P:(c % 4 + 1) * P], hs[:, c * P:(c + 1) * P], ident[:, :])
                    last.then_inc(ht_done, 1)
            steps(pe, step2, 2, SLOTS)

            def step3(g, j):
                if it := behind(g, j, 1, U, B):
                    b, _, r = it
                    ge(pe, xn3_ready, b + 1)
                    transposes(0, xn3, S, KC).then_inc(t31_done, 1)
                if it := behind(g, j, 3, U, B):
                    b, _, r = it
                    ge(pe, xq_ready, b + 1)
                    ge(pe, x3_seq, min(2 * b + 3, 2 * B) if isinstance(b, int) else 2 * b + 3)
                    transposes(2, xq, S, KC).then_inc(tq_done, 1)
                if it := behind(g, j, 1, U, B):
                    b, bg, r = it
                    ge(pe, xn3T_ready, b + 1)
                    ge(pe, ctx3_in[r], 32 * (bg + 1))
                    for k, (k0, kn) in enumerate(KEYS):
                        for c in range(KC):
                            last = mm(PS[0:kn, 1, k * S:(k + 1) * S], ring3[r][:, c * SK + k0:c * SK + k0 + kn], xn3T[:, c, :],
                                      start=(c == 0), stop=(c == KC - 1))
                    last.then_inc(s1_done, 1)
                if it := behind(g, j, 6, U, B):
                    b, _, r = it
                    ge(pe, hqT_ready, b + 1)
                    ge(pe, out_ready, b)
                    for c in range(HC):
                        last = mm(PS[0:S, 3, 0:D], hqT[:, c, :], w2q[:, c, :], start=(c == 0), stop=(c == HC - 1))
                    last.then_inc(f2_done, 1)
                if it := behind(g, j, 1, U, B):
                    b, _, r = it
                    ge(pe, s1T_ready, b + 1)
                    ge(pe, x3_seq, 2 * b - 1)
                    for k, (k0, kn) in enumerate(KEYS):
                        last = mm(PS[0:S, 2, 0:D], s1T[0:kn, k, :], ring3[r][0:kn, KC * SK + k * D:KC * SK + (k + 1) * D],
                                  start=(k == 0), stop=(k == 2))
                    last.then_inc(o1_done, 1)
                if it := behind(g, j, 3, U, B):
                    b, _, r = it
                    ge(pe, xqT_ready, b + 1)
                    ge(pe, hb_ready, b)
                    for half in range(2):
                        for k in range(KC):
                            last = mm(PS[0:S, 4 + half, :], xqT[:, k, :], w1q[:, k, half * 512:(half + 1) * 512],
                                      start=(k == 0), stop=(k == KC - 1))
                    last.then_inc(f1_done, 1)
                if it := behind(g, j, 5, U, B):
                    b, _, r = it
                    ge(pe, hq_ready, b + 1)
                    for c in range(HC):
                        last = nc.tensor.transpose(PS[:, 6 + c // 4, c % 4 * S:(c % 4 + 1) * S], hq[0:S, c * P:(c + 1) * P], ident[0:S, 0:S])
                    last.then_inc(th_done, 1)
            steps(pe, step3, U, B, ends=2)

        @block.scalar
        def _(act):
            def copy(dst, src, **kw):
                return nc.scalar.activation(dst, src, ACT.Copy, **kw)

            def flat(ap):
                return ap.rearrange("p a b -> p (a b)")

            for i, (a, b) in enumerate(((qa, qbT), (ka, kbT), (va, vbT))):
                act.dma_start(lowA[:, i, :], a).then_inc(low_in, 16)
                act.dma_start(lowB[:, i, :], b).then_inc(low_in, 16)
            act.dma_start(gates[:, 0:2], g_x.partition_broadcast(P)).then_inc(small_in, 16)
            act.dma_start(gates[:, 2:4], g_f.partition_broadcast(P)).then_inc(small_in, 16)
            act.dma_start(gate_sb[:, :, :], gateT).then_inc(small_in, 16)
            act.dma_start(gate_bc[:, :], gate_b.partition_broadcast(P)).then_inc(small_in, 16)
            act.dma_start(b2_bc[:, :, :], b2m.partition_broadcast(P)).then_inc(b2_in, 16)
            act.wait_ge(small_in, 16 * 4)
            nc.scalar.activation(tg[:, :], gates[:, :], ACT.Tanh).then_inc(tanh_done, 1)
            for i, (dst, scale) in enumerate(((M, D ** -0.5), (N, 1.0))):
                act.wait_ge(prod_done, i + 1)
                for c in range(KC):
                    copy(dst[:, c, :], bank(4 + 2 * i + c, D), scale=scale).then_inc(mn_ready, 1)

            def step1(g, j):
                if it := behind(g, j, 3, U, B):
                    ge(act, tt_done, it[0] + 1)
                    copy(flat(tT[:, :, :]), bank(4, KC * S)).then_inc(tt_ready, 1)
                if it := behind(g, j, 4, U, B):
                    ge(act, t3_done, it[0] + 1)
                    copy(flat(xn2T[:, :, :]), bank(6, KC * S)).then_inc(xn2T_ready, 1)
                if it := behind(g, j, 1, U, B):
                    ge(act, q_done, it[0] + 1)
                    copy(flat(qT[:, :, :]), bank(1, KC * S)).then_inc(q_ready, 1)
                if it := behind(g, j, 2, U, B):
                    ge(act, t2_done, it[0] + 1)
                    copy(flat(pT[:, 0:2, :]), bank(3, 2 * S))
                    copy(pT[0:TAIL, 2, :], PS[0:TAIL, 3, 2 * S:3 * S]).then_inc(pT_ready, 1)
                if it := behind(g, j, 8, U, B + U):
                    if it[2] == 0:
                        ge(act, route_seq, LINKS * it[1] + 2)
                        nc.scalar.activation(rt[0:S, 1, :], rt[0:S, 0, :], ACT.Exp).then_inc(rexp_done, 1)
                if it := behind(g, j, 0, U, B):
                    ge(act, t1_done, it[0] + 1)
                    copy(flat(xnT[:, :, :]), bank(0, KC * S)).then_inc(xnT_ready, 1)
                if it := behind(g, j, 1, U, B):
                    b, _, r = it
                    ge(act, max_done, b + 1)
                    nc.scalar.activation(probs[0:S, :], PS[0:S, 2, 0:SK], ACT.Exp, bias=negmax[0:S, r:r + 1],
                                         accum_out=rowsum[0:S, r:r + 1]).then_inc(exp_done, 1)
                if isinstance(g, int) and g == 1:
                    pair = ((raw_w1, flat(w1q[:, :, :])), (raw_w2, flat(w2q[:, :, :])))
                    if j < 2:
                        act.wait_ge(lraw_in, 32)
                        nc.scalar.activation(pair[j][1], pair[j][0], ACT.Abs, accum_out=wstat[:, j:j + 1]).then_inc(wsum_ready, 1)
                    else:
                        act.wait_ge(dve_w, 2)
                        nc.scalar.activation(pair[j - 2][0], pair[j - 2][0], ACT.Identity, bias=pmagic[:, :],
                                             scale=wscale[:, j - 2:j - 1]).then_inc(wround_done, 1)
            for g in range(2):
                for j in range(U):
                    step1(g, j)
            with act.Fori(2, NG) as g:
                for j in range(U):
                    step1(g, j)
            for g in range(NG, NG + 2):
                for j in range(U):
                    step1(g, j)

            def step2(g, j):
                if it := behind(g, j, 1, 2, SLOTS):
                    ge(act, h0_done, it[0] + 1)
                    copy(hs[:, 0:512], bank(0, 512)).then_inc(h_ready, 1)
                if it := behind(g, j, 0, 2, SLOTS):
                    ge(act, x_done, it[0] + 1)
                    copy(flat(xsT[:, :, :]), bank(5, D)).then_inc(xsT_ready, 1)
                if it := behind(g, j, 1, 2, SLOTS):
                    s, _, r = it
                    ge(act, b1_ready, s + 1)
                    ge(act, ht_done, s + 1)
                    for c in range(HC // 2):
                        last = nc.scalar.activation(hT[:, c, :], PS[:, 2, c * P:(c + 1) * P], ACT.Relu, bias=b1s[:, r, c:c + 1])
                    last.then_inc(hT_ready, 1)
            steps(act, step2, 2, SLOTS)

            def step3(g, j):
                if it := behind(g, j, 1, U, B):
                    b, _, r = it
                    ge(act, t31_done, b)
                    ge_alone(act, nb3_ready, b + 1)
                    nc.scalar.activation(xn3[0:S, :], X[0:S, b, :], ACT.Identity, bias=nbA[0:S, r:r + 1],
                                         scale=rsA[0:S, r:r + 1]).then_inc(xn3_ready, 1)
                if it := behind(g, j, 3, U, B):
                    b, _, r = it
                    ge(act, x_seq, 6 * b + 5)
                    nc.scalar.activation(xq[0:S, :], h0[0:S, :], ACT.Identity, bias=pmagic[0:S, :],
                                         scale=amx[0:S, r, 2:3]).then_inc(xq_ready, 1)
                if it := behind(g, j, 1, U, B):
                    ge(act, t31_done, it[0] + 1)
                    copy(flat(xn3T[:, :, :]), bank(0, KC * S)).then_inc(xn3T_ready, 1)
                if it := behind(g, j, 6, U, B):
                    b, _, r = it
                    ge(act, th_done, b + 1)
                    nc.scalar.activation(hqT[:, :, :].rearrange("p (u c) b -> p u (c b)", u=2), PS[:, 6:8, 0:4 * S],
                                         ACT.Identity, bias=nmagic[:, :]).then_inc(hqT_ready, 1)
                if it := behind(g, j, 3, U, B):
                    b, _, r = it
                    ge(act, tq_done, b + 1)
                    nc.scalar.activation(flat(xqT[:, :, :]), bank(2, KC * S),
                                         ACT.Identity, bias=nmagic[:, :]).then_inc(xqT_ready, 1)
                if it := behind(g, j, 1, U, B):
                    ge(act, s1_done, it[0] + 1)
                    copy(flat(s1T[:, 0:2, :]), bank(1, 2 * S), scale=1.0 / S)
                    copy(s1T[0:TAIL, 2, :], PS[0:TAIL, 1, 2 * S:3 * S], scale=1.0 / S).then_inc(s1T_ready, 1)
                if it := behind(g, j, 4, U, B):
                    b, _, r = it
                    ge(act, hb_ready, b + 1)
                    nc.scalar.activation(hg[0:S, r % 2, :], hb[0:S, :], ACT.Gelu).then_inc(gelu_done, 1)
                if it := behind(g, j, 5, U, B):
                    b, _, r = it
                    ge(act, h_seq, 4 * b + 3)
                    nc.scalar.activation(hq[0:S, :], hg[0:S, r % 2, :], ACT.Identity, bias=pmagic[0:S, :],
                                         scale=amh[0:S, r, 2:3]).then_inc(hq_ready, 1)
            steps(act, step3, U, B, ends=2)

        @block.vector
        def _(dve):
            v = nc.vector

            def link(ins, s, value):
                ins.then_inc(s, 1)
                dve.wait_ge(s, value)

            def flat(ap):
                return ap.rearrange("p a b -> p (a b)")

            dve.wait_ge(setup_in, 16 * 4)
            for i, (raw, eff) in enumerate(((raw_q, eff_q), (raw_k, eff_k), (raw_v, eff_v))):
                dve.wait_ge(low_done, i + 1)
                v.tensor_tensor(flat(eff[:, :, :]), PS[:, i, :], flat(raw[:, :, :]), ALU.add).then_inc(eff_done, 1)

            def norm(dst, b, r, mv, rs):
                return v.tensor_scalar(dst, X[0:S, b, :], mv[0:S, r, 0:1], rs[0:S, r:r + 1], ALU.subtract, ALU.mult)

            dve.wait_ge(small_in, 16 * 4)
            dve.wait_ge(tanh_done, 1)
            dve.wait_ge(consts_set, CONSTS)

            def bc(ap, n_):
                return ap.unsqueeze(2).broadcast_to([ap.shape[0], ap.shape[1], n_])

            def route(g, piece):
                if piece:
                    ge(dve, route_seq, LINKS * g + piece)
                else:
                    ge(dve, logit_done, U * (g + 1))
                if piece == 2:
                    ge(dve, rexp_done, g + 1)
                L = logit[0:S, :, :]
                T = [rt[0:S, i, :].rearrange("p (b e) -> p b e", b=U) for i in range(6)]
                V = [rv[0:S, i, :] for i in range(10)]
                rev_b = rev[0:S, :].unsqueeze(1).broadcast_to([S, U, E])
                if piece == 0:
                    ins = v.tensor_reduce(V[0], L, AX, ALU.max)
                elif piece == 1:
                    ins = v.tensor_tensor(T[0], L, bc(V[0], E), ALU.subtract)
                elif piece == 2:
                    ins = v.tensor_reduce(V[1], T[1], AX, ALU.add)
                elif piece == 3:
                    ins = v.reciprocal(V[2], V[1])
                elif piece == 4:
                    ins = v.tensor_tensor(T[2], T[1], bc(V[2], E), ALU.mult)
                elif piece == 5:
                    ins = v.tensor_reduce(V[3], T[2], AX, ALU.max)
                elif piece == 6:
                    ins = v.tensor_tensor(T[3], T[2], bc(V[3], E), ALU.is_ge)
                elif piece == 7:
                    ins = v.tensor_tensor(T[3], T[3], rev_b, ALU.mult)
                elif piece == 8:
                    ins = v.tensor_reduce(V[4], T[3], AX, ALU.max)
                elif piece == 9:
                    ins = v.tensor_tensor(T[4], rev_b, bc(V[4], E), ALU.is_equal)
                elif piece == 10:
                    ins = v.scalar_tensor_tensor(T[4], T[4], -2.0, T[2], ALU.mult, ALU.add)
                elif piece == 11:
                    ins = v.tensor_reduce(V[5], T[4], AX, ALU.max)
                elif piece == 12:
                    ins = v.tensor_tensor(T[5], T[4], bc(V[5], E), ALU.is_ge)
                elif piece == 13:
                    ins = v.tensor_tensor(T[5], T[5], rev_b, ALU.mult)
                elif piece == 14:
                    ins = v.tensor_reduce(V[6], T[5], AX, ALU.max)
                elif piece == 15:
                    ins = v.tensor_scalar(V[8], V[5], 0.0, None, ALU.is_gt)
                elif piece == 16:
                    ins = v.tensor_tensor(V[7], V[6], V[4], ALU.subtract)
                elif piece == 17:
                    ins = v.scalar_tensor_tensor(V[7], V[7], 0.0, V[8], ALU.min, ALU.mult)
                elif piece == 18:
                    ins = v.tensor_tensor(V[9], V[4], V[7], ALU.add)
                elif piece == 19:
                    ins = v.tensor_tensor(T[5], rev_b, bc(V[9], E), ALU.is_equal)
                elif piece == 20:
                    ins = v.tensor_copy(OH[0:S, :, bass.ds(U * g, U)].rearrange("p e b -> p b e"), T[5])
                elif piece == 21:
                    ins = v.tensor_tensor(T[4], T[5], T[2], ALU.mult)
                if piece < LINKS:
                    ins.then_inc(route_seq, 1)
                else:
                    v.tensor_reduce(w_tab[0:S, bass.ds(U * g, U)], T[4], AX, ALU.add).then_inc(route_done, 1)

            def route_slot(g, j, i):
                if it := behind(g, j, 8, U, B + U):
                    bg, slot = it[1], 6 * it[2] + i
                    if not isinstance(bg, int) or bg < NG - 1:
                        if slot != 2:
                            route(bg, slot - (slot > 2))
                    elif slot == 0:
                        for piece in range(LINKS + 1):
                            route(bg, piece)

            dve.wait_ge(x_in0, 16)

            def step1(g, j):
                if it := behind(g, j, 0, U, B):
                    b, _, r = it
                    v.bn_stats(st[0:S, 0, :], X[0:S, b, :]).then_inc(stat1_seq, 1)
                route_slot(g, j, 0)
                if it := behind(g, j, 2, U, B):
                    b, _, r = it
                    ge(dve, exp_done, b + 1)
                    v.reciprocal(rsum_inv[0:S, r:r + 1], rowsum[0:S, r:r + 1]).then_inc(coef_seq, 1)
                if it := behind(g, j, 0, U, B):
                    b, _, r = it
                    ge_alone(dve, stat1_seq, b + 1)
                    v.bn_aggr(mvA[0:S, r, :], st[0:S, 0, :]).then_inc(mv1_ready, 1)
                route_slot(g, j, 1)
                if it := behind(g, j, 2, U, B):
                    b, _, r = it
                    ge(dve, coef_seq, 2 * b + 1)
                    v.tensor_tensor(coef[0:S, r:r + 1], rsum_inv[0:S, r:r + 1], tg[0:S, 0:1], ALU.mult).then_inc(coef_seq, 1)
                route_slot(g, j, 2)
                if it := behind(g, j, 0, U, B):
                    b, _, r = it
                    ge(dve, t1_done, b)
                    ge(dve, rstd1_ready, b + 1)
                    norm(xn[0:S, :], b, r, mvA, rsA).then_inc(xn_ready, 1)
                if it := behind(g, j, 3, U, B):
                    b, _, r = it
                    ge(dve, coef_seq, 2 * (b + 1))
                    ge(dve, o_done, b + 1)
                    v.scalar_tensor_tensor(X[0:S, b, :], PS[0:S, 5, 0:D], coef[0:S, r:r + 1], X[0:S, b, :],
                                           ALU.mult, ALU.add).then_inc(res_done, 1)
                route_slot(g, j, 3)
                if it := behind(g, j, 3, U, B):
                    b, _, r = it
                    ge_alone(dve, res_done, b + 1)
                    v.bn_stats(st[0:S, 1, :], X[0:S, b, :]).then_inc(stat2_seq, 1)
                if it := behind(g, j, 4, U, B):
                    b, bg, r = it
                    ge(dve, l_done, b + 1)
                    v.tensor_tensor(logit[0:S, r, :], PS[0:S, 7, 0:E], gate_bc[0:S, :], ALU.add).then_inc(logit_done, 1)
                if it := behind(g, j, 3, U, B):
                    b, _, r = it
                    ge_alone(dve, stat2_seq, b + 1)
                    v.bn_aggr(mvB[0:S, r, :], st[0:S, 1, :]).then_inc(mv2_ready, 1)
                route_slot(g, j, 4)
                if it := behind(g, j, 1, U, B):
                    b, _, r = it
                    ge(dve, s_done, b + 1)
                    v.tensor_reduce(negmax[0:S, r:r + 1], PS[0:S, 2, 0:SK], AX, ALU.max, negate=True).then_inc(max_done, 1)
                route_slot(g, j, 5)
                if it := behind(g, j, 3, U, B):
                    b, bg, r = it
                    ge(dve, t3_done, b - 1)
                    ge(dve, xn2_stored[r % 2], 16 * (2 * bg + r // 2))
                    ge(dve, rstd2_ready, b + 1)
                    norm(xn2[0:S, r % 2, 0:D], b, r, mvB, rsB).then_inc(xn2_ready, 1)
                if isinstance(g, int) and g == 1:
                    if j == 2:
                        dve.wait_ge(wsum_done, 1)
                        link(v.tensor_scalar(wmean[:, :], PS[:, 7, 64:66], 1.0 / (HID * D), EPS, ALU.mult, ALU.max), dve_w, 1)
                        v.reciprocal(wscale[:, :], wmean[:, :]).then_inc(dve_w, 1)
                        v.tensor_copy(wdq[:, 0:1], wmean[:, 0:1])
                        v.tensor_tensor(wdq[:, 1:2], wmean[:, 1:2], tg[:, 3:4], ALU.mult)
                    if j == 3:
                        for i, (raw, dst) in enumerate(((raw_w1, w1q), (raw_w2, w2q))):
                            dve.wait_ge(wround_done, i + 1)
                            link(v.tensor_scalar(raw, raw, MAGIC + 1.0, MAGIC - 1.0, ALU.min, ALU.max), dve_w, 3 + i)
                            last = v.tensor_scalar(flat(dst[:, :, :]), raw, MAGIC, None, ALU.subtract)
                        last.then_inc(quant_done, 1)
                        dve.wait_ge(b2_in, 16)
                        v.tensor_scalar(flat(b2_bc[:, :, :]), flat(b2_bc[:, :, :]), tg[:, 2:3], None, ALU.mult).then_inc(b2_scaled, 1)

            for j in range(U):
                step1(0, j)
            dve.wait_ge(x_in, 16)
            for j in range(U):
                step1(1, j)
            with dve.Fori(2, NG) as g:
                for j in range(U):
                    step1(g, j)
            for g in range(NG, NG + 2):
                for j in range(U):
                    step1(g, j)

            n = 0

            def then(ins):
                nonlocal n
                n += 1
                link(ins, plan_seq, n)
            EB = E * B
            dve.wait_ge(count_done, 1)
            v.memset(ce[:, 0:1], 0.0)
            then(v.tensor_tensor_scan(cum[:, :], PS[:, 1, 0:EB], zeros[:, 0:EB], 0.0, ALU.add, ALU.add))
            then(v.tensor_copy(ce[:, 1:E + 1], cum[:, B - 1:EB:B]))
            v.tensor_tensor(cex[:, :], cum[:, :], PS[:, 1, 0:EB], ALU.subtract)
            then(v.tensor_tensor(sl[:, 0, :], ce[:, 1:E + 1], ce[:, 0:E], ALU.subtract))
            then(v.tensor_scalar(sl[:, 1, :], sl[:, 0, :], 1.0 / P, (P - 1.0) / P + FLOOR, ALU.mult, ALU.add))
            then(v.tensor_scalar(sl[:, 2, :], sl[:, 1, :], MAGIC, MAGIC, ALU.add, ALU.subtract))
            then(v.tensor_tensor_scan(sl[:, 3, :], sl[:, 2, :], zeros[:, 0:E], 0.0, ALU.add, ALU.add))
            then(v.tensor_tensor(sl[:, 4, :], sl[:, 3, :], sl[:, 2, :], ALU.subtract))
            then(v.scalar_tensor_tensor(sl[:, 5, :], sl[:, 4, :], float(P), ce[:, 0:E], ALU.mult, ALU.subtract))
            dve.wait_ge(count_done, 2)
            then(v.tensor_tensor(acc[0:S, :], PS[0:S, 0, 0:EB], cex[0:S, :], ALU.add))
            acc3 = acc[0:S, :].rearrange("p (e b) -> p e b", e=E)
            then(v.tensor_tensor(acc3, acc3, bc(sl[0:S, 5, :], B), ALU.add))
            then(v.tensor_tensor(acc3, acc3, OH[0:S, :, :], ALU.mult))
            then(v.tensor_reduce(pos[0:S, :], acc3.rearrange("p e b -> p b e"), AX, ALU.add))
            then(v.tensor_scalar(slot_f[0:S, :], pos[0:S, :], 1.0 / P, FLOOR, ALU.mult, ALU.add))
            then(v.tensor_scalar(slot_f[0:S, :], slot_f[0:S, :], MAGIC, MAGIC, ALU.add, ALU.subtract))
            then(v.scalar_tensor_tensor(r_f[0:S, :], slot_f[0:S, :], -float(P), pos[0:S, :], ALU.mult, ALU.add))
            for s in xn2_stored:
                dve.wait_ge(s, 16 * B // 2)
            iota_s = iota_row[0:S, 0:SLOTS].unsqueeze(1).broadcast_to([S, B, SLOTS])
            then(v.tensor_tensor(carry[0:S, :, SLOTS:], bc(slot_f[0:S, :], SLOTS), iota_s, ALU.is_equal))
            then(v.tensor_scalar(carry[0:S, :, 0:SLOTS], carry[0:S, :, SLOTS:], part_no[0:S, :], None, ALU.mult))
            then(v.tensor_tensor(carry[0:S, :, SLOTS:], carry[0:S, :, SLOTS:], batch_no[0:S, :, :], ALU.mult))
            for c in range(4):
                v.tensor_tensor(place[0:S, 8 * c:8 * c + 8, :], bc(r_f[0:S, 8 * c:8 * c + 8], P),
                                iota_row[0:S, :].unsqueeze(1).broadcast_to([S, 8, P]), ALU.is_equal).then_inc(place_ready, 1)
            v.tensor_copy(pos_u[0:S, :], pos[0:S, :])
            then(v.tensor_tensor(le[0:1, :, :], sl[0:1, 3, :].unsqueeze(1).broadcast_to([1, SLOTS, E]),
                                 bc(iota_row[0:1, 0:SLOTS], E), ALU.is_le))
            then(v.tensor_reduce(ex_f[0:1, 0, :], le[0:1, :, :], AX, ALU.add))
            v.tensor_scalar(expert_of[0:1, :], ex_f[0:1, 0, :], E - 1.0, None, ALU.min).then_inc(slots_ready, 1)
            dve.wait_ge(inv_done, 1)
            then(v.tensor_copy(id_b[:, :], PS[:, 2, SLOTS:2 * SLOTS]))
            v.scalar_tensor_tensor(tok_u[:, :], id_b[:, :], float(S), PS[:, 2, 0:SLOTS], ALU.mult, ALU.add).then_inc(tok_ready, 1)
            dve.wait_ge(slots_ready, 1)
            dve.wait_ge(b2_scaled, 1)
            dve.wait_ge(w_in, 16 * W_DMAS)

            def step2(g, j):
                if it := behind(g, j, 0, 2, SLOTS):
                    s, sg, r = it
                    ge(dve, x_done, s)
                    ge(dve, xs_in[r], 16 * (sg + 1))
                    v.tensor_scalar(xsw, xs[:, r, 0:D], xs[:, r, D:ROW], None, ALU.mult).then_inc(xsw_ready, 1)
                if it := behind(g, j, 1, 2, SLOTS):
                    s, _, r = it
                    e = dve.value_load(expert_of[0:1, bass.ds(s, 1)], min_val=0, max_val=E - 1)
                    v.tensor_copy(b1s[:, r, :], b1_tab[:, e, :]).then_inc(b1_ready, 1)
                    ge(dve, h1_done, s + 1)
                    v.tensor_copy(hs[:, 512:1024], bank(1, 512)).then_inc(h_ready, 1)
                if it := behind(g, j, 2, 2, SLOTS):
                    s, sg, r = it
                    e = dve.value_load(expert_of[0:1, bass.ds(s, 1)], min_val=0, max_val=E - 1)
                    ge(dve, y_stored[r], 16 * sg)
                    ge(dve, y_done, s + 1)
                    v.scalar_tensor_tensor(ysb[:, r, :], PS[:, 4, 0:D], tg[:, 2:3], b2_bc[:, e, :], ALU.mult, ALU.add).then_inc(y_ready, 1)
                if it := behind(g, j, 1, 2, SLOTS):
                    s, _, r = it
                    ge(dve, b1_ready, s + 1)
                    ge(dve, ht_done, s + 1)
                    for c in range(HC // 2, HC):
                        last = v.tensor_scalar(hT[:, c, :], PS[:, 3, (c - 4) * P:(c - 3) * P], b1s[:, r, c:c + 1], 0.0, ALU.add, ALU.max)
                    last.then_inc(hT_ready, 1)
            steps(dve, step2, 2, SLOTS, ends=2)

            def step3(g, j):
                H = lambda r, i: amh[0:S, r, i:i + 1]
                Q = lambda r, i: amx[0:S, r, i:i + 1]
                n3 = behind(g, j, 0, U, B)
                q = behind(g, j, 2, U, B)
                h = behind(g, j, 5, U, B)
                if q:
                    b, _, r = q
                    ge_alone(dve, x3_seq, 2 * b + 1)
                    v.bn_stats(st[0:S, 1, :], X[0:S, b, :]).then_inc(x3_seq, 1)
                if h:
                    b, _, r = h
                    ge(dve, h_seq, 4 * b + 1)
                    v.tensor_scalar(H(r, 1), H(r, 0), EPS, 1.0 / 127, ALU.max, ALU.mult).then_inc(h_seq, 1)
                if q:
                    b, _, r = q
                    ge_alone(dve, x3_seq, 2 * b + 2)
                    v.bn_aggr(mvB[0:S, r, :], st[0:S, 1, :]).then_inc(mv4_ready, 1)
                if h:
                    b, _, r = h
                    ge(dve, h_seq, 4 * b + 2)
                    v.reciprocal(H(r, 2), H(r, 1)).then_inc(h_seq, 1)
                if q:
                    b, _, r = q
                    if isinstance(b, int) and b == 0:
                        dve.wait_ge(bc_in, 16 * 4)
                        v.tensor_scalar(gb2_bc, b2raw_bc, tg[:, 3:4], None, ALU.mult).then_inc(gb2_seq, 1)
                    ge(dve, xq_ready, b)
                    ge(dve, mv4_ready, b + 1)
                    v.scalar_tensor_tensor(h0[0:S, :], X[0:S, b, :], mvB[0:S, r, 0:1], gamma_bc[0:S, :],
                                           ALU.subtract, ALU.mult).then_inc(x_seq, 1)
                if it := behind(g, j, 4, U, B):
                    b, _, r = it
                    ge(dve, x_seq, 6 * b + 6)
                    ge(dve, gelu_done, b)
                    ge(dve, f1_done, b + 1)
                    v.scalar_tensor_tensor(hb[0:S, :], flat(PS[0:S, 4:6, :]), inv1[0:S, r:r + 1],
                                           b1_bc[0:S, :], ALU.mult, ALU.add).then_inc(hb_ready, 1)
                if q:
                    b, _, r = q
                    ge(dve, rstd4_ready, b + 1)
                    ge(dve, x_seq, 6 * b + 1)
                    v.scalar_tensor_tensor(h0[0:S, :], h0[0:S, :], rsB[0:S, r:r + 1], beta_bc[0:S, :],
                                           ALU.mult, ALU.add).then_inc(x_seq, 1)
                    ge(dve, x_seq, 6 * b + 2)
                    v.tensor_reduce(Q(r, 0), h0[0:S, :], AX, ALU.max, apply_absolute_value=True).then_inc(x_seq, 1)
                if n3:
                    b, _, r = n3
                    ge_alone(dve, x2_ready, b + 1)
                    v.bn_stats(st[0:S, 0, :], X[0:S, b, :]).then_inc(stat3_seq, 1)
                if q:
                    b, _, r = q
                    ge(dve, x_seq, 6 * b + 3)
                    v.tensor_scalar(Q(r, 1), Q(r, 0), EPS, 1.0 / 127, ALU.max, ALU.mult).then_inc(x_seq, 1)
                if n3:
                    b, _, r = n3
                    ge_alone(dve, stat3_seq, b + 1)
                    v.bn_aggr(mvA[0:S, r, :], st[0:S, 0, :]).then_inc(mv3_ready, 1)
                if it := behind(g, j, 1, U, B):
                    b, _, r = it
                    ge(dve, o1_done, b + 1)
                    v.scalar_tensor_tensor(X[0:S, b, :], PS[0:S, 2, 0:D], tg[0:S, 1:2], X[0:S, b, :], ALU.mult, ALU.add).then_inc(x3_seq, 1)
                if h:
                    b, _, r = h
                    v.tensor_scalar(inv2[0:S, r:r + 1], H(r, 1), wdq[0:S, 1:2], None, ALU.mult).then_inc(h_seq, 1)
                if it := behind(g, j, 6, U, B):
                    b, bg, r = it
                    ge(dve, h_seq, 4 * b + 4)
                    ge(dve, out_stored[r % 2], 16 * (2 * bg + r // 2))
                    ge(dve, xb_ready, b + 1)
                    ge(dve, f2_done, b + 1)
                    v.scalar_tensor_tensor(osb[0:S, r % 2, :], PS[0:S, 3, 0:D], inv2[0:S, r:r + 1], X[0:S, b, :],
                                           ALU.mult, ALU.add).then_inc(out_ready, 1)
                if q:
                    b, _, r = q
                    ge(dve, x_seq, 6 * b + 4)
                    v.reciprocal(Q(r, 2), Q(r, 1)).then_inc(x_seq, 1)
                    v.tensor_scalar(inv1[0:S, r:r + 1], Q(r, 1), wdq[0:S, 0:1], None, ALU.mult).then_inc(x_seq, 1)
                if it := behind(g, j, 4, U, B):
                    b, _, r = it
                    ge(dve, gelu_done, b + 1)
                    v.tensor_reduce(H(r, 0), hg[0:S, r % 2, :], AX, ALU.max, apply_absolute_value=True).then_inc(h_seq, 1)
            steps(dve, step3, U, B, ends=2)


LINKS = 22
CONSTS = 13
W_DMAS = 1 + NG + (E * HC * D - U * CTX) // (HC * D) + 1


_OUTS = [((B, S, D), "float32")]


def kernel(**inputs):
    import numpy as np
    import concourse.bacc as bacc
    from concourse.bass_utils import run_bass_kernel_spmd

    a = {k: np.asarray(v) for k, v in inputs.items()}

    def chunked(w):
        return w.reshape(w.shape[0] // P, P, w.shape[1]).transpose(1, 0, 2)

    ctx = a["ctx_1024"]
    ctxT = ctx.transpose(0, 2, 1).reshape(B, KC, P, SK).transpose(0, 2, 1, 3).reshape(B, P, KC * SK)
    rows = ctx[:, 0:2 * P].reshape(B, 2, P, D).transpose(0, 2, 1, 3).reshape(B, P, 2 * D)
    arrays = [
        ("x", a["x"]),
        ("ctx_pack", np.concatenate([ctxT, rows], axis=2)),
        ("ctx_tail", ctx[:, 2 * P:]),
        ("g_x", a["g_xattn"]), ("g_f", a["g_ffn"]),
        ("wq", chunked(a["L0_xattn_Q_weight"])), ("wk", chunked(a["L0_xattn_K_weight"])), ("wv", chunked(a["L0_xattn_V_weight"])),
        ("woT", chunked(a["L0_xattn_O_weight"].T)),
        ("qa", a["L0_xattn_Q_A"]), ("ka", a["L0_xattn_K_A"]), ("va", a["L0_xattn_V_A"]),
        ("qbT", a["L0_xattn_Q_B"].T), ("kbT", a["L0_xattn_K_B"].T), ("vbT", a["L0_xattn_V_B"].T),
        ("gateT", chunked(a["L0_ffn_gate_w"].T)), ("gate_b", a["L0_ffn_gate_b"]),
        ("w1m", a["L0_ffn_w1"].transpose(2, 0, 1).reshape(KC, P, E, HID).transpose(1, 2, 0, 3).reshape(P, -1)),
        ("b1m", a["L0_ffn_b1"].reshape(E, HC, P).transpose(2, 0, 1)),
        ("w2m", a["L0_ffn_w2"].transpose(2, 0, 1).reshape(HC, P, E, D).transpose(1, 2, 0, 3).reshape(P, -1)),
        ("b2m", a["L0_ffn_b2"]),
        ("w1l", chunked(a["L1_ffn_w1"].T).reshape(P, -1)), ("b1l", a["L1_ffn_b1"]),
        ("w2l", chunked(a["L1_ffn_w2"].T).reshape(P, -1)), ("b2l", a["L1_ffn_b2"]),
        ("gamma", a["L1_ffn_gamma"]), ("beta", a["L1_ffn_beta"]),
    ]
    nc = bacc.Bacc("TRN2", target_bir_lowering=False, num_devices=1)
    feeds, args = {}, []
    for name, arr in arrays:
        arr = np.ascontiguousarray(arr)
        feeds[f"in_{name}"] = arr
        args.append(nc.dram_tensor(f"in_{name}", arr.shape, mybir.dt.from_np(arr.dtype), kind="ExternalInput").ap())
    for i, (shape, dtype) in enumerate(_OUTS):
        args.append(nc.dram_tensor(f"out_{i}", shape, mybir.dt.from_np(np.dtype(dtype)), kind="ExternalOutput").ap())
    flamingo_kernel(nc, *args)
    r = run_bass_kernel_spmd(nc, [feeds], core_ids=[0])
    return r.results[0]["out_0"]
```

```python
from contextlib import ExitStack

import concourse.bass as bass
from concourse import mybir

F32 = mybir.dt.float32
BF16 = mybir.dt.bfloat16
I32 = mybir.dt.int32
U32 = mybir.dt.uint32
ALU = mybir.AluOpType
ACT = mybir.ActivationFunctionType
AX = mybir.AxisListType.X

P = 128
B, S, D = 32, 100, 256
SK = 361
R = 16
E, HID = 8, 1024
KC = D // P
HC = HID // P
KEYS = [(0, 128), (128, 128), (256, SK - 256)]
TAIL = KEYS[2][1]
NTOK = B * S
SLOTS = 32
ROW = D + 1
QC = 4
QW = KC * HID // QC
U = 4
NG = B // U
CTX = KC * SK + 2 * D + D
EPS = 1e-5
MAGIC = 12582912.0
FLOOR = 1.0 / 256 - 0.5


def flamingo_kernel(nc, x, ctx_pack, ctx_tail, small, w_qk, w_vo, low, gateT, w1m, b1m, w2m, b2m, w1l, b1l, w2l, b2l, gamma, beta, out):
    rows_dram = nc.dram_tensor("token_rows", [NTOK, ROW], F32, kind="Internal").ap()
    y_dram = nc.dram_tensor("slot_outputs", [SLOTS * P, D], F32, kind="Internal").ap()
    rows_by_batch = rows_dram.rearrange("(b p) c -> p b c", p=S)

    with ExitStack() as stack:
        def sb(name, shape, dt=F32):
            return stack.enter_context(nc.sbuf_tensor(name, shape, dt))

        def sem(name):
            return stack.enter_context(nc.semaphore(name))

        def sems(name, n):
            return [sem(f"{name}{i}") for i in range(n)]

        X = sb("X", [P, B, D])
        W1A = sb("W1A", [P, E * KC * HID])
        W2A = sb("W2A", [P, E * HC * D])
        W1 = W1A[:, :].rearrange("p (e k h) -> p e k h", e=E, k=KC)
        W2 = W2A[:, :].rearrange("p (e c d) -> p e c d", e=E, c=HC)
        WK = sb("WK", [P, 4096])

        def view(base, at, *shape, dt=F32):
            n = 1
            for d in shape:
                n *= d
            words = n if dt == F32 else n // 2
            v = base[:, at:at + words]
            if dt != F32:
                v = v.bitcast(dt)
            if len(shape) == 2:
                v = v.rearrange("p (a b) -> p a b", a=shape[0])
            if len(shape) == 3:
                v = v.rearrange("p (a b c) -> p a b c", a=shape[0], b=shape[1])
            return v

        MN = sb("MN", [P, 2 * KC * D])
        w1q = sb("w1q", [P, KC, HID], BF16)
        w2q = sb("w2q", [P, HC, D], BF16)
        gate_sb = sb("gate_sb", [P, KC, E])
        b1_tab = sb("b1_tab", [P, E, HC])
        b2_bc = sb("b2_bc", [P, E, D])
        ident = sb("ident", [P, P])
        tri = sb("tri", [P, P], BF16)
        ones_b = sb("ones_b", [P, P], BF16)
        ones_f = sb("ones_f", [P, P])
        iota_row = sb("iota_row", [P, P])
        iota_b = sb("iota_b", [P, P], BF16)
        part_no = sb("part_no", [P, 1])
        batch_no = sb("batch_no", [P, B, SLOTS], BF16)
        rev = sb("rev", [P, E])
        zeros = sb("zeros", [P, 256])
        small_bc = sb("small_bc", [P, 4 + E])
        tg = sb("tg", [P, 4])
        nhalf = sb("nhalf", [P, 1])
        eps_t = sb("eps_t", [P, 1])
        nmagic = sb("nmagic", [P, 1])
        pmagic = sb("pmagic", [P, 1])
        wstat = sb("wstat", [P, 2 * QC])
        wmean = sb("wmean", [P, 2])
        wscale = sb("wscale", [P, 2])
        wdq = sb("wdq", [P, 2])
        st = sb("st", [P, 2, 6])
        mvA = sb("mvA", [P, U, 2])
        mvB = sb("mvB", [P, U, 2])
        veA = sb("veA", [P, U])
        veB = sb("veB", [P, U])
        rsA = sb("rsA", [P, U])
        rsB = sb("rsB", [P, U])
        negmax = sb("negmax", [P, U])
        rowsum = sb("rowsum", [P, U])
        rsum_inv = sb("rsum_inv", [P, U])
        coef = sb("coef", [P, U])
        logit = sb("logit", [P, U, E])
        rt = sb("rt", [P, 6, U * E])
        rv = sb("rv", [P, 10, U])
        w_tab = sb("w_tab", [P, B])
        OH = sb("OH", [P, E, B], BF16)
        ce = sb("ce", [P, E + 1])
        sl = sb("sl", [P, 6, E])
        pos = sb("pos", [P, B])
        pos_u = sb("pos_u", [P, B], U32)
        slot_f = sb("slot_f", [P, B])
        slot_b, r_b = sb("slot_b", [P, B], BF16), sb("r_b", [P, B], BF16)
        ex_f = sb("ex_f", [1, 2, SLOTS])
        expert_of = sb("expert_of", [1, SLOTS], I32)
        last_of = sb("last_of", [1, SLOTS], I32)
        id_b = sb("id_b", [P, SLOTS])
        tok_u = sb("tok_u", [P, SLOTS], U32)
        idx_c = sb("idx_c", [P, 2], U32)
        nbA = sb("nbA", [P, U])
        amh = sb("amh", [P, U, 3])
        amx = sb("amx", [P, U, 3])
        inv1 = sb("inv1", [P, U])
        inv2 = sb("inv2", [P, U])

        RING1 = E * HC * D - U * CTX
        ring1 = [W2A[:, RING1 + r * CTX:RING1 + (r + 1) * CTX] for r in range(U)]
        W2_PART = RING1 // (NG - 2) // 8 * 8
        xn = view(WK, 0, D)
        xnT = view(WK, 256, KC, S)
        qT = view(WK, 456, KC, S)
        probs = view(WK, 656, SK)
        pT = view(WK, 1024, 3, S)
        tT = view(WK, 1324, KC, S)
        xn2 = view(WK, 1536, 2, ROW)
        xn2T = view(WK, 2060, KC, S)
        EW = KC * HID
        raw_q, raw_k, raw_v, raw_o, eff_q, eff_k, eff_v = [
            view(W1A, 4 * EW + i * KC * D, KC, D) for i in range(7)]
        raw_qk, raw_vo = [W1A[:, 4 * EW + i * 2 * KC * D:4 * EW + (i + 1) * 2 * KC * D] for i in range(2)]
        low_sb = W1A[0:R, 3 * EW:3 * EW + 6 * D].rearrange("p (i h d) -> p i h d", i=3, h=2)
        raw_w1 = view(W1A, 6 * EW, KC * HID)
        raw_w2 = view(W1A, 7 * EW, HC * D)
        M, N = view(MN, 0, KC, D), view(MN, KC * D, KC, D)
        place = view(WK, 0, B, P, dt=BF16)
        carry = view(WK, 2048, B, 2 * SLOTS, dt=BF16)
        cum, cex, acc = [view(WK, 3072 + i * E * B, E * B) for i in range(3)]
        le = view(WK, 3072 + 3 * E * B, SLOTS, E)
        xs = view(WK, 0, 2, ROW)
        xsw = view(WK, 516, D)
        xsT = view(WK, 772, KC, P)
        w1s = [view(WK, 1028, HID), view(MN, 0, HID)]
        hT = view(WK, 2052, HC, P)
        ysb = view(WK, 3076, 2, D)
        b1s = view(WK, 3588, 2, HC)
        ring3 = [W1A[:, r * CTX:(r + 1) * CTX] for r in range(U)]
        at = [0]

        def work3(*shape, dt=F32):
            n = 1
            for d in shape:
                n *= d
            v = view(W2A, at[0], *shape, dt=dt)
            at[0] += (n if dt == F32 else n // 2) + 7 & ~7
            return v
        yg = work3(2, D)
        xn3 = work3(D)
        xn3T = work3(KC, S)
        s1T = work3(3, S)
        h0 = work3(2, D)
        xq = work3(D)
        xqT = work3(KC, S, dt=BF16)
        hb = work3(HID)
        hg = work3(2, HID)
        hq = work3(HID)
        hqT = work3(HC, S, dt=BF16)
        osb = work3(2, D)
        gamma_bc = work3(D)
        beta_bc = work3(D)
        b1_bc = work3(HID)
        b2raw_bc = work3(D)
        gb2_bc = work3(D)

        PS = stack.enter_context(nc.psum_tensor("PS", [P, 8, 512], F32))

        def bank(i, n):
            return PS[:, i, 0:n]

        consts_set, ones_set = sem("consts_set"), sem("ones_set")
        pool_seq = sem("pool_seq")
        qk_in, vo_in, low_in, b2_in = sem("qk_in"), sem("vo_in"), sem("low_in"), sem("b2_in")
        small_in = sem("small_in")
        lraw_in = sem("lraw_in")
        x_in0, x_in1, x_in2 = sem("x_in0"), sem("x_in1"), sem("x_in2")
        ctx_in = sems("ctx_in", U)
        w_in = sem("w_in")
        low_done, eff_done, prod_done, mn_ready = sem("low_done"), sem("eff_done"), sem("prod_done"), sem("mn_ready")
        tanh_done = sem("tanh_done")
        wsum_ready, wsum_done, wround_done = sem("wsum_ready"), sem("wsum_done"), sem("wround_done")
        dve_w, quant_done, b2_scaled = sem("dve_w"), sem("quant_done"), sem("b2_scaled")
        mv1_ready, mv2_ready, rstd1_ready, rstd2_ready = sem("mv1_ready"), sem("mv2_ready"), sem("rstd1_ready"), sem("rstd2_ready")
        pool_v1, pool_v2 = sem("pool_v1"), sem("pool_v2")
        stat1_seq, stat2_seq, coef_seq = sem("stat1_seq"), sem("stat2_seq"), sem("coef_seq")
        xn_ready, t1_done, xnT_ready = sem("xn_ready"), sem("t1_done"), sem("xnT_ready")
        q_done, q_ready, s_done, max_done, exp_done = sem("q_done"), sem("q_ready"), sem("s_done"), sem("max_done"), sem("exp_done")
        t2_done, pT_ready, tt_done, tt_ready, o_done, res_done = sem("t2_done"), sem("pT_ready"), sem("tt_done"), sem("tt_ready"), sem("o_done"), sem("res_done")
        xn2_ready, t3_done, xn2T_ready, l_done, logit_done = sem("xn2_ready"), sem("t3_done"), sem("xn2T_ready"), sem("l_done"), sem("logit_done")
        xn2_stored = sems("xn2_stored", 2)
        rexp_done, route_seq, route_done, w_stored = sem("rexp_done"), sem("route_seq"), sem("route_done"), sem("w_stored")
        count_done, plan_seq, slots_ready, place_ready, inv_done, tok_ready = sem("count_done"), sem("plan_seq"), sem("slots_ready"), sem("place_ready"), sem("inv_done"), sem("tok_ready")
        idx_set, xs_in = sem("idx_set"), sems("xs_in", 2)
        xsw_ready, x_done, xsT_ready = sem("xsw_ready"), sem("x_done"), sem("xsT_ready")
        w1_ready = sem("w1_ready")
        h0_done, h1_done, hT0_ready, hT1_ready, b1_ready = sem("h0_done"), sem("h1_done"), sem("hT0_ready"), sem("hT1_ready"), sem("b1_ready")
        y_done, y_ready, y_stored = sem("y_done"), sem("y_ready"), sems("y_stored", 2)
        ctx3_in, bc_in, gb2_seq = sems("ctx3_in", U), sem("bc_in"), sem("gb2_seq")
        pos_set, yg_in = sem("pos_set"), sems("yg_in", 2)
        x2_ready, stat3_seq, mv3_ready, rstd3_ready, nb3_ready = sem("x2_ready"), sem("stat3_seq"), sem("mv3_ready"), sem("rstd3_ready"), sem("nb3_ready")
        xn3_ready, t31_done, xn3T_ready = sem("xn3_ready"), sem("t31_done"), sem("xn3T_ready")
        s1_done, s1T_ready, o1_done, x3_seq, mv4_ready, rstd4_ready, xb_ready = sem("s1_done"), sem("s1T_ready"), sem("o1_done"), sem("x3_seq"), sem("mv4_ready"), sem("rstd4_ready"), sem("xb_ready")
        pool_v3, pool_v4 = sem("pool_v3"), sem("pool_v4")
        inv1_ready, inv2_ready = sem("inv1_ready"), sem("inv2_ready")
        x_seq, h_seq = sem("x_seq"), sem("h_seq")
        xq_ready, tq_done, xqT_ready, f1_done, hb_ready, gelu_done = sem("xq_ready"), sem("tq_done"), sem("xqT_ready"), sem("f1_done"), sem("hb_ready"), sem("gelu_done")
        hq_ready, th_done, hqT_ready, f2_done, out_ready = sem("hq_ready"), sem("th_done"), sem("hqT_ready"), sem("f2_done"), sem("out_ready")
        out_stored = sems("out_stored", 2)

        carrier = {mybir.EngineType.DVE: sem("dve_carrier"), mybir.EngineType.PE: sem("pe_carrier"),
                   mybir.EngineType.Pool: sem("pool_carrier"), mybir.EngineType.Activation: sem("act_carrier")}

        def ge(eng, s, v):
            if not (isinstance(v, int) and v <= 0):
                eng.wait_ge(s, v)

        def ge_alone(eng, s, v):
            ge(eng, s, v)
            if not isinstance(v, int):
                eng.sem_inc(carrier[eng.engine], 1)

        def behind(g, j, lag, unroll, total):
            q, r = divmod(j - lag, unroll)
            g = g + q
            if isinstance(g, int) and not 0 <= g < total // unroll:
                return None
            return unroll * g + r, g, r

        def steps(eng, step, unroll, total, ends=1):
            for g in range(ends):
                for j in range(unroll):
                    step(g, j)
            with eng.Fori(ends, total // unroll) as g:
                for j in range(unroll):
                    step(g, j)
            for g in range(total // unroll, total // unroll + ends):
                for j in range(unroll):
                    step(g, j)

        block = stack.enter_context(nc.Block())

        @block.sync
        def _(sp):
            def load_x(b0, b1, s_in):
                sp.dma_start(X[0:S, b0:b1, :], x[b0:b1].rearrange("b p d -> p b d")).then_inc(s_in, 16)

            sp.dma_start(raw_qk, w_qk).then_inc(qk_in, 16)
            load_x(0, U, x_in0)
            sp.dma_start(raw_vo, w_vo).then_inc(vo_in, 16)

            def load_ctx(buf, s_in, b):
                sp.dma_start(buf[:, 0:CTX - D], ctx_pack[b]).then_inc(s_in, 16)
                sp.dma_start(buf[0:TAIL, CTX - D:CTX], ctx_tail[b]).then_inc(s_in, 16)

            def step(g, j):
                if it := behind(g, j, 0, U, B):
                    b, _, r = it
                    ge(sp, tt_done, b - U + 1)
                    load_ctx(ring1[r], ctx_in[r], b)
                    if j == 2:
                        if not isinstance(g, int):
                            sp.wait_ge(quant_done, 2)
                        sp.dma_start(W1A[:, bass.ds(g * EW, EW)], w1m[:, bass.ds(g * EW, EW)]).then_inc(w_in, 16)
                        if not isinstance(g, int):
                            part = bass.ds((g - 2) * W2_PART, W2_PART)
                            sp.dma_start(W2A[:, part], w2m[:, part]).then_inc(w_in, 16)
                if it := behind(g, j, 4, U, B):
                    b, bg, r = it
                    ge(sp, xn2_ready, b + 1)
                    sp.dma_start(rows_by_batch[:, b, 0:D], xn2[0:S, r % 2, 0:D]).then_inc(xn2_stored[r % 2], 16)
                if it := behind(g, j, 8, U, B):
                    if it[2] == U - 1:
                        store_weights(it[1])

            def store_weights(bg):
                ge(sp, route_done, bg + 1)
                sp.dma_start(rows_by_batch[:, bass.ds(U * bg, U), D:ROW], w_tab[0:S, bass.ds(U * bg, U)].unsqueeze(2),
                             allow_slow_non_contiguous=True).then_inc(w_stored, 16)

            for g in range(2):
                for j in range(U):
                    step(g, j)
                    if (g, j) == (0, 1):
                        load_x(U, B // 2, x_in1)
                    if (g, j) == (0, 3):
                        sp.dma_start(raw_w1, w1l).then_inc(lraw_in, 16)
                        sp.dma_start(raw_w2, w2l).then_inc(lraw_in, 16)
                        load_x(B // 2, B, x_in2)
            sp.dma_start(b1_tab[:, :, :], b1m).then_inc(w_in, 16)
            sp.dma_start(b2_bc[:, :, :], b2m.partition_broadcast(P)).then_inc(b2_in, 16)
            sp.wait_ge(prod_done, 2)
            with sp.Fori(2, NG) as g:
                for j in range(U):
                    step(g, j)
            for j in range(U):
                step(NG, j)
            sp.wait_ge(tt_done, B)
            sp.dma_start(W2A[:, W2_PART * (NG - 2):], w2m[:, W2_PART * (NG - 2):]).then_inc(w_in, 16)
            step(NG + 1, 0)
            store_weights(NG - 1)

            def store_y(g, j):
                if it := behind(g, j, 1, 2, SLOTS):
                    s, _, r = it
                    ge(sp, y_ready, s + 1)
                    sp.dma_start(y_dram[bass.ds(s * P, P), :], ysb[:, r, :]).then_inc(y_stored[r], 16)
            steps(sp, store_y, 2, SLOTS)

            sp.wait_ge(h1_done, SLOTS)

            def step3(g, j):
                if it := behind(g, j, 0, U, B):
                    b, _, r = it
                    ge(sp, o1_done, b - U + 1)
                    load_ctx(ring3[r], ctx3_in[r], b)
                if it := behind(g, j, 8, U, B):
                    b, _, r = it
                    ge(sp, out_ready, b + 1)
                    sp.dma_start(out[b], osb[0:S, r % 2, :]).then_inc(out_stored[r % 2], 16)
                if isinstance(g, int) and (g, j) == (0, U - 1):
                    sp.wait_ge(y_done, SLOTS)
                    for v, src in ((gamma_bc, gamma), (beta_bc, beta), (b1_bc, b1l), (b2raw_bc, b2l)):
                        sp.dma_start(v, src.partition_broadcast(P)).then_inc(bc_in, 16)
            steps(sp, step3, U, B, ends=2)
            for s in out_stored:
                sp.wait_ge(s, 16 * B // 2)
            for s in xn2_stored:
                sp.wait_ge(s, 16 * B // 2)
            for s in y_stored:
                sp.wait_ge(s, 16 * SLOTS // 2)
            sp.wait_ge(w_stored, 16 * NG)

        @block.gpsimd
        def _(pool):
            gp = nc.gpsimd
            gp.memset(ones_b[:, :], 1.0).then_inc(ones_set, 1)
            gp.memset(ident[:, :], 0.0).then_inc(pool_seq, 1)
            gp.memset(tri[:, :], 1.0).then_inc(pool_seq, 1)
            gp.memset(nhalf[:, :], -0.5).then_inc(consts_set, 1)
            gp.memset(eps_t[:, :], EPS).then_inc(consts_set, 1)
            pool.wait_ge(pool_seq, 2)
            gp.affine_select(out=ident[:, :], in_=ident[:, :], compare_op=ALU.not_equal, fill=1.0, base=0,
                             pattern=[[-1, P]], channel_multiplier=1).then_inc(consts_set, 1)
            gp.affine_select(out=tri[:, :], in_=tri[:, :], compare_op=ALU.is_gt, fill=0.0, base=0,
                             pattern=[[1, P]], channel_multiplier=-1).then_inc(consts_set, 1)
            gp.memset(ones_f[:, :], 1.0).then_inc(consts_set, 1)
            gp.memset(nmagic[:, :], -MAGIC).then_inc(consts_set, 1)
            gp.memset(pmagic[:, :], MAGIC).then_inc(consts_set, 1)
            gp.memset(zeros[:, :], 0.0).then_inc(consts_set, 1)
            gp.iota(iota_row[:, :], [[1, P]], base=0, channel_multiplier=0,
                    allow_small_or_imprecise_dtypes=True).then_inc(consts_set, 1)
            gp.iota(iota_b[:, :], [[1, P]], base=0, channel_multiplier=0,
                    allow_small_or_imprecise_dtypes=True).then_inc(consts_set, 1)
            gp.iota(batch_no[:, :, :], [[1, B], [0, SLOTS]], base=0, channel_multiplier=0,
                    allow_small_or_imprecise_dtypes=True).then_inc(consts_set, 1)
            gp.iota(part_no[:, :], [[0, 1]], base=0, channel_multiplier=1,
                    allow_small_or_imprecise_dtypes=True).then_inc(consts_set, 1)
            gp.iota(rev[:, :], [[-1, E]], base=E, channel_multiplier=0,
                    allow_small_or_imprecise_dtypes=True).then_inc(consts_set, 1)
            pool.wait_ge(consts_set, CONSTS)

            def rstd(b, r, mv_ready, mv, ve, rs, ve_done, ready):
                ge(pool, mv_ready, b + 1)
                gp.tensor_tensor(ve[0:S, r:r + 1], mv[0:S, r, 1:2], eps_t[0:S, :], ALU.add).then_inc(ve_done, 1)
                ge(pool, ve_done, b + 1)
                gp.tensor_tensor(rs[0:S, r:r + 1], ve[0:S, r:r + 1], nhalf[0:S, :], ALU.pow).then_inc(ready, 1)

            def step1(g, j):
                if it := behind(g, j, 0, U, B):
                    rstd(it[0], it[2], mv1_ready, mvA, veA, rsA, pool_v1, rstd1_ready)
                if it := behind(g, j, 3, U, B):
                    rstd(it[0], it[2], mv2_ready, mvB, veB, rsB, pool_v2, rstd2_ready)
            steps(pool, step1, U, B)

            pool.wait_ge(tok_ready, 1)
            for s in xn2_stored:
                pool.wait_ge(s, 16 * B // 2)
            pool.wait_ge(w_stored, 16 * NG)

            def gather_rows(g, j):
                if it := behind(g, j, 0, 2, SLOTS):
                    s, _, r = it
                    ge(pool, xsw_ready, s - 1)
                    gp.tensor_copy(idx_c[:, r:r + 1], tok_u[:, bass.ds(s, 1)]).then_inc(idx_set, 1)
                    ge_alone(pool, idx_set, s + 1)
                    gp.indirect_dma_start(xs[:, r, :], None, rows_dram,
                                          bass.IndirectOffsetOnAxis(idx_c[:, r:r + 1], 0)).then_inc(xs_in[r], 16)
            steps(pool, gather_rows, 2, SLOTS)

            for s in y_stored:
                pool.wait_ge(s, 16 * SLOTS // 2)

            def step3(g, j):
                if it := behind(g, j, 5, U, B):
                    b, _, r = it
                    ge_alone(pool, mv4_ready, b + 1)
                    gp.tensor_scalar(veB[0:S, r:r + 1], mvB[0:S, r, 1:2], 1.0 + EPS, EPS * EPS, ALU.mult, ALU.add).then_inc(pool_v4, 1)
                    ge(pool, pool_v4, b + 1)
                    gp.tensor_tensor(rsB[0:S, r:r + 1], veB[0:S, r:r + 1], nhalf[0:S, :], ALU.pow).then_inc(rstd4_ready, 1)
                if it := behind(g, j, 6, U, B):
                    b, _, r = it
                    ge_alone(pool, x_seq, 5 * b + 4)
                    gp.tensor_scalar(inv1[0:S, r:r + 1], amx[0:S, r, 1:2], wdq[0:S, 0:1], 1.0, ALU.mult, ALU.mult).then_inc(inv1_ready, 1)
                if it := behind(g, j, 8, U, B):
                    b, _, _ = it
                    if isinstance(b, int) and b == 0:
                        pool.wait_ge(gb2_seq, 1)
                    ge_alone(pool, x_seq, 5 * b + 1)
                    gp.tensor_tensor(X[0:S, b, :], X[0:S, b, :], gb2_bc[0:S, :], ALU.add).then_inc(xb_ready, 1)
                if it := behind(g, j, 8, U, B):
                    b, _, r = it
                    ge_alone(pool, h_seq, 3 * b + 2)
                    gp.tensor_scalar(inv2[0:S, r:r + 1], amh[0:S, r, 1:2], wdq[0:S, 1:2], 1.0, ALU.mult, ALU.mult).then_inc(inv2_ready, 1)
                if it := behind(g, j, 0, U, B):
                    b, _, r = it
                    ge(pool, x2_ready, b - 1)
                    gp.tensor_copy(idx_c[0:S, r % 2:r % 2 + 1], pos_u[0:S, bass.ds(b, 1)]).then_inc(pos_set, 1)
                    ge_alone(pool, pos_set, b + 1)
                    gp.indirect_dma_start(yg[0:S, r % 2, :], None, y_dram,
                                          bass.IndirectOffsetOnAxis(idx_c[0:S, r % 2:r % 2 + 1], 0)).then_inc(yg_in[r % 2], 16)
                if it := behind(g, j, 2, U, B):
                    b, _, r = it
                    rstd(b, r, mv3_ready, mvA, veA, rsA, pool_v3, rstd3_ready)
                    ge_alone(pool, rstd3_ready, b + 1)
                    gp.tensor_scalar(nbA[0:S, r:r + 1], rsA[0:S, r:r + 1], mvA[0:S, r, 0:1], -1.0, ALU.mult, ALU.mult).then_inc(nb3_ready, 1)
                if it := behind(g, j, 1, U, B):
                    b, bg, r = it
                    ge_alone(pool, yg_in[r % 2], 16 * (2 * bg + r // 2 + 1))
                    gp.tensor_tensor(X[0:S, b, :], X[0:S, b, :], yg[0:S, r % 2, :], ALU.add).then_inc(x2_ready, 1)
            steps(pool, step3, U, B, ends=2)

        @block.tensor
        def _(pe):
            mm = nc.tensor.matmul

            def keep_busy(n):
                for _ in range(n):
                    mm(PS[:, 6, 0:P], ones_b[:, :], ones_b[:, :], start=True, stop=True)

            pe.wait_ge(ones_set, 1)
            pe.wait_ge(low_in, 16)
            for i in range(3):
                for f in range(KC):
                    last = mm(PS[:, i, f * D:(f + 1) * D], low_sb[:, i, 1, f * P:(f + 1) * P], low_sb[:, i, 0, :],
                              start=(f == 0), stop=(f == KC - 1), skip_group_check=True)
                last.then_inc(low_done, 1)
            def weight_product(i, a, b):
                pe.wait_ge(eff_done, 2 + i)
                for c in range(KC):
                    for f in range(KC):
                        last = mm(bank(4 + 2 * i + c, D), a[:, f, c * P:(c + 1) * P], b[:, f, :], start=(f == 0), stop=(f == KC - 1))
                last.then_inc(prod_done, 1)

            weight_product(0, eff_q, eff_k)
            pe.wait_ge(consts_set, CONSTS)

            def transposes(b_, src, n_rows, n):
                for c in range(n):
                    last = nc.tensor.transpose(PS[:, b_, c * n_rows:(c + 1) * n_rows],
                                               src[0:n_rows, c * P:(c + 1) * P], ident[0:n_rows, 0:n_rows])
                return last

            def step1(g, j):
                if it := behind(g, j, 1, U, B):
                    b, _, r = it
                    if isinstance(b, int) and b == 0:
                        pe.wait_ge(mn_ready, 2)
                    ge(pe, xnT_ready, b + 1)
                    for c in range(KC):
                        for k in range(KC):
                            last = mm(PS[:, 1, c * S:(c + 1) * S], M[:, k, c * P:(c + 1) * P], xnT[:, k, :], start=(k == 0), stop=(k == KC - 1))
                    last.then_inc(q_done, 1)
                if it := behind(g, j, 4, U, B):
                    b, _, r = it
                    ge(pe, xn2_ready, b + 1)
                    transposes(6, xn2[:, r % 2, :], S, KC).then_inc(t3_done, 1)
                if it := behind(g, j, 2, U, B):
                    b, _, r = it
                    ge(pe, exp_done, b + 1)
                    for k, (k0, kn) in enumerate(KEYS):
                        last = nc.tensor.transpose(PS[0:kn, 3, k * S:(k + 1) * S], probs[0:S, k0:k0 + kn], ident[0:S, 0:S])
                    last.then_inc(t2_done, 1)
                if it := behind(g, j, 3, U, B):
                    b, _, r = it
                    ge(pe, tt_ready, b + 1)
                    ge(pe, res_done, b)
                    for k in range(KC):
                        last = mm(PS[0:S, 5, 0:D], tT[:, k, :], N[:, k, :], start=(k == 0), stop=(k == KC - 1))
                    last.then_inc(o_done, 1)
                if it := behind(g, j, 0, U, B):
                    b, _, r = it
                    ge(pe, xn_ready, b + 1)
                    transposes(0, xn, S, KC).then_inc(t1_done, 1)
                if it := behind(g, j, 1, U, B):
                    b, bg, r = it
                    ge(pe, q_ready, b + 1)
                    ge(pe, ctx_in[r], 32 * (bg + 1))
                    for k in range(KC):
                        last = mm(PS[0:S, 2, 0:SK], qT[:, k, :], ring1[r][:, k * SK:(k + 1) * SK], start=(k == 0), stop=(k == KC - 1))
                    last.then_inc(s_done, 1)
                if it := behind(g, j, 4, U, B):
                    b, _, r = it
                    ge(pe, xn2T_ready, b + 1)
                    ge(pe, logit_done, b)
                    if isinstance(b, int) and b == 2:
                        pe.wait_ge(dve_w, 1)
                    for k in range(KC):
                        last = mm(PS[0:S, 7, 0:E], xn2T[:, k, :], gate_sb[:, k, :], start=(k == 0), stop=(k == KC - 1))
                    last.then_inc(l_done, 1)
                if it := behind(g, j, 2, U, B):
                    b, _, r = it
                    ge(pe, pT_ready, b + 1)
                    for c in range(KC):
                        for k, (k0, kn) in enumerate(KEYS):
                            rows = ring1[r][0:kn, KC * SK + k * D + c * P:KC * SK + k * D + (c + 1) * P]
                            last = mm(PS[:, 4, c * S:(c + 1) * S], rows, pT[0:kn, k, :], start=(k == 0), stop=(k == 2))
                    last.then_inc(tt_done, 1)
                if isinstance(g, int) and (g, j) == (0, 1):
                    pe.wait_ge(vo_in, 16)
                    weight_product(1, eff_v, raw_o)
                if isinstance(g, int) and (g, j) == (0, 2):
                    pe.wait_ge(mn_ready, 4)
                    pe.wait_ge(small_in, 16 * 2)
                if isinstance(g, int) and (g, j) == (1, 1):
                    pe.wait_ge(wsum_ready, 2 * QC)
                    pe.wait_ge(logit_done, 2)
                    mm(PS[:, 7, 64:64 + 2 * QC], ones_f[:, :], wstat[:, :], start=True, stop=True).then_inc(wsum_done, 1)
            for g in range(2):
                for j in range(U):
                    step1(g, j)
            with pe.Fori(2, NG) as g:
                for j in range(U):
                    step1(g, j)
            for g in range(NG, NG + 2):
                for j in range(U):
                    step1(g, j)

            pe.wait_ge(route_done, NG)
            oh = OH[0:S, :, :].rearrange("p e b -> p (e b)")
            mm(PS[:, 1, 0:E * B], ones_b[0:S, :], oh, start=True, stop=True).then_inc(count_done, 1)
            mm(PS[0:S, 0, 0:E * B], tri[0:S, 0:S], oh, start=True, stop=True).then_inc(count_done, 1)
            for b in range(B):
                if b % 8 == 0:
                    pe.wait_ge(place_ready, 1 + b // 8)
                last = mm(PS[:, 2, 0:2 * SLOTS], place[0:S, b, :], carry[0:S, b, :], start=(b == 0), stop=(b == B - 1))
            last.then_inc(inv_done, 1)
            pe.wait_ge(tok_ready, 1)
            keep_busy(45)
            pe.wait_ge(slots_ready, 2)
            pe.wait_ge(w_in, 16 * W_DMAS)

            def step2(g, j):
                if it := behind(g, j, 1, 2, SLOTS):
                    s, _, r = it
                    expert = pe.value_load(last_of[0:1, bass.ds(s, 1)], min_val=0, max_val=E)
                    with pe.If(expert < E):
                        ge(pe, xsT_ready, s + 1)
                        for half, done in enumerate((h0_done, h1_done)):
                            ge(pe, w1_ready, 2 * s + half + 1)
                            for c in range(HC // 2):
                                for k in range(KC):
                                    cols = slice((half * HC // 2 + c) * P, (half * HC // 2 + c + 1) * P)
                                    last = mm(PS[:, half, c * P:(c + 1) * P], w1s[k][:, cols], xsT[:, k, :], start=(k == 0), stop=(k == KC - 1))
                            last.then_inc(done, 1)
                    with pe.Else():
                        ge(pe, xsT_ready, s + 1)
                        ge(pe, w1_ready, 2 * s + 2)
                        ge(pe, y_done, s)
                        pe.sem_inc(h0_done, 1)
                        pe.sem_inc(h1_done, 1)
                if it := behind(g, j, 0, 2, SLOTS):
                    s, _, r = it
                    ge(pe, xsw_ready, s + 1)
                    transposes(5, xsw, P, KC).then_inc(x_done, 1)
                if it := behind(g, j, 1, 2, SLOTS):
                    s, _, r = it
                    e = pe.value_load(expert_of[0:1, bass.ds(s, 1)], min_val=0, max_val=E - 1)
                    with pe.If(expert < E):
                        ge(pe, y_ready, s)
                        for half, ready in enumerate((hT0_ready, hT1_ready)):
                            ge(pe, ready, s + 1)
                            for c in range(half * HC // 2, (half + 1) * HC // 2):
                                last = mm(PS[:, 4, 0:D], hT[:, c, :], W2[:, e, c, :], start=(c == 0), stop=(c == HC - 1))
                        last.then_inc(y_done, 1)
                    with pe.Else():
                        ge(pe, y_ready, s)
                        ge(pe, hT0_ready, s + 1)
                        ge(pe, hT1_ready, s + 1)
                        pe.sem_inc(y_done, 1)
            steps(pe, step2, 2, SLOTS)

            pe.wait_ge(mv3_ready, 1)
            keep_busy(18)
            def step3(g, j):
                if it := behind(g, j, 4, U, B):
                    b, _, _ = it
                    ge(pe, xqT_ready, b + 1)
                    ge(pe, hb_ready, b)
                    for half in range(2):
                        for k in range(KC):
                            last = mm(PS[0:S, 4 + half, :], xqT[:, k, :], w1q[:, k, half * 512:(half + 1) * 512],
                                      start=(k == 0), stop=(k == KC - 1))
                    last.then_inc(f1_done, 1)
                if it := behind(g, j, 1, U, B):
                    b, bg, r = it
                    ge(pe, xn3T_ready, b + 1)
                    ge(pe, ctx3_in[r], 32 * (bg + 1))
                    for k, (k0, kn) in enumerate(KEYS):
                        for c in range(KC):
                            last = mm(PS[0:kn, 1, k * S:(k + 1) * S], ring3[r][:, c * SK + k0:c * SK + k0 + kn], xn3T[:, c, :],
                                      start=(c == 0), stop=(c == KC - 1))
                    last.then_inc(s1_done, 1)
                if isinstance(g, int) and g == 0:
                    keep_busy(8)
                if it := behind(g, j, 3, U, B):
                    b, _, _ = it
                    ge(pe, xq_ready, b + 1)
                    ge(pe, x3_seq, min(2 * b + 3, 2 * B) if isinstance(b, int) else 2 * b + 3)
                    transposes(2, xq, S, KC).then_inc(tq_done, 1)
                if it := behind(g, j, 7, U, B):
                    b, _, _ = it
                    ge(pe, hqT_ready, b + 1)
                    ge(pe, out_ready, b)
                    for c in range(HC):
                        last = mm(PS[0:S, 3, 0:D], hqT[:, c, :], w2q[:, c, :], start=(c == 0), stop=(c == HC - 1))
                    last.then_inc(f2_done, 1)
                if it := behind(g, j, 6, U, B):
                    b, _, _ = it
                    ge(pe, hq_ready, b + 1)
                    for c in range(HC):
                        last = nc.tensor.transpose(PS[:, 6 + c // 4, c % 4 * S:(c % 4 + 1) * S], hq[0:S, c * P:(c + 1) * P], ident[0:S, 0:S])
                    last.then_inc(th_done, 1)
                if it := behind(g, j, 1, U, B):
                    b, _, r = it
                    ge(pe, s1T_ready, b + 1)
                    ge(pe, x3_seq, 2 * b - 1)
                    ge(pe, xqT_ready, b - 1)
                    for k, (k0, kn) in enumerate(KEYS):
                        last = mm(PS[0:S, 2, 0:D], s1T[0:kn, k, :], ring3[r][0:kn, KC * SK + k * D:KC * SK + (k + 1) * D],
                                  start=(k == 0), stop=(k == 2))
                    last.then_inc(o1_done, 1)
                if it := behind(g, j, 0, U, B):
                    b, _, _ = it
                    ge(pe, xn3_ready, b + 1)
                    transposes(0, xn3, S, KC).then_inc(t31_done, 1)
                if isinstance(g, int) and g == 0:
                    keep_busy(4)
            steps(pe, step3, U, B, ends=2)

        @block.scalar
        def _(act):
            def copy(dst, src, **kw):
                return nc.scalar.activation(dst, src, ACT.Copy, **kw)

            def flat(ap):
                return ap.rearrange("p a b -> p (a b)")

            def weight_chunk(g, j, i):
                if not (isinstance(g, int) and g == 1):
                    return
                n = (4 * j + i) % (2 * QC)
                raw, q = pair[n // QC]
                cols = slice(n % QC * QW, (n % QC + 1) * QW)
                if 4 * j + i < 2 * QC:
                    act.wait_ge(lraw_in, 32)
                    nc.scalar.activation(q[:, cols], raw[:, cols], ACT.Abs, accum_out=wstat[:, n:n + 1]).then_inc(wsum_ready, 1)
                else:
                    act.wait_ge(dve_w, 4)
                    nc.scalar.activation(raw[:, cols], raw[:, cols], ACT.Identity, bias=pmagic[:, :],
                                         scale=wscale[:, n // QC:n // QC + 1]).then_inc(wround_done, 1)

            pair = ((raw_w1, flat(w1q[:, :, :])), (raw_w2, flat(w2q[:, :, :])))
            act.dma_start(low_sb, low).then_inc(low_in, 16)
            act.dma_start(small_bc[:, :], small.partition_broadcast(P)).then_inc(small_in, 16)
            act.dma_start(gate_sb[:, :, :], gateT).then_inc(small_in, 16)
            act.wait_ge(small_in, 16 * 2)
            nc.scalar.activation(tg[:, :], small_bc[:, 0:4], ACT.Tanh).then_inc(tanh_done, 1)
            def product_out(i, dst, scale):
                act.wait_ge(prod_done, i + 1)
                for c in range(KC):
                    copy(dst[:, c, :], bank(4 + 2 * i + c, D), scale=scale).then_inc(mn_ready, 1)

            product_out(0, M, D ** -0.5)

            def step1(g, j):
                if it := behind(g, j, 3, U, B):
                    ge(act, tt_done, it[0] + 1)
                    copy(flat(tT[:, :, :]), bank(4, KC * S)).then_inc(tt_ready, 1)
                weight_chunk(g, j, 0)
                if it := behind(g, j, 1, U, B):
                    ge(act, q_done, it[0] + 1)
                    copy(flat(qT[:, :, :]), bank(1, KC * S)).then_inc(q_ready, 1)
                if it := behind(g, j, 2, U, B):
                    ge(act, t2_done, it[0] + 1)
                    copy(flat(pT[:, 0:2, :]), bank(3, 2 * S))
                    copy(pT[0:TAIL, 2, :], PS[0:TAIL, 3, 2 * S:3 * S]).then_inc(pT_ready, 1)
                weight_chunk(g, j, 1)
                if it := behind(g, j, 4, U, B):
                    ge(act, t3_done, it[0] + 1)
                    copy(flat(xn2T[:, :, :]), bank(6, KC * S)).then_inc(xn2T_ready, 1)
                if it := behind(g, j, 8, U, B + U):
                    if it[2] == 0:
                        ge(act, route_seq, LINKS * it[1] + 2)
                        nc.scalar.activation(rt[0:S, 1, :], rt[0:S, 0, :], ACT.Exp).then_inc(rexp_done, 1)
                if it := behind(g, j, 0, U, B):
                    ge(act, t1_done, it[0] + 1)
                    copy(flat(xnT[:, :, :]), bank(0, KC * S)).then_inc(xnT_ready, 1)
                weight_chunk(g, j, 2)
                if it := behind(g, j, 1, U, B):
                    b, _, r = it
                    ge(act, max_done, b + 1)
                    nc.scalar.activation(probs[0:S, :], PS[0:S, 2, 0:SK], ACT.Exp, bias=negmax[0:S, r:r + 1],
                                         accum_out=rowsum[0:S, r:r + 1]).then_inc(exp_done, 1)
                weight_chunk(g, j, 3)
                if isinstance(g, int) and (g, j) == (0, 1):
                    product_out(1, N, 1.0)
            for g in range(2):
                for j in range(U):
                    step1(g, j)
            with act.Fori(2, NG) as g:
                for j in range(U):
                    step1(g, j)
            for g in range(NG, NG + 2):
                for j in range(U):
                    step1(g, j)

            def step2(g, j):
                if it := behind(g, j, 1, 2, SLOTS):
                    s, _, r = it
                    ge(act, b1_ready, s + 1)
                    ge(act, h0_done, s + 1)
                    for c in range(HC // 2):
                        last = nc.scalar.activation(hT[:, c, :], PS[:, 0, c * P:(c + 1) * P], ACT.Relu, bias=b1s[:, r, c:c + 1])
                    last.then_inc(hT0_ready, 1)
                if it := behind(g, j, 0, 2, SLOTS):
                    ge(act, x_done, it[0] + 1)
                    copy(flat(xsT[:, :, :]), bank(5, D)).then_inc(xsT_ready, 1)
            steps(act, step2, 2, SLOTS)

            def step3(g, j):
                if it := behind(g, j, 1, U, B):
                    b, _, _ = it
                    ge(act, s1_done, b + 1)
                    copy(flat(s1T[:, 0:2, :]), bank(1, 2 * S), scale=1.0 / S)
                    copy(s1T[0:TAIL, 2, :], PS[0:TAIL, 1, 2 * S:3 * S], scale=1.0 / S).then_inc(s1T_ready, 1)
                if it := behind(g, j, 3, U, B):
                    b, _, _ = it
                    ge(act, tq_done, b + 1)
                    nc.scalar.activation(flat(xqT[:, :, :]), bank(2, KC * S),
                                         ACT.Identity, bias=nmagic[:, :]).then_inc(xqT_ready, 1)
                if it := behind(g, j, 0, U, B):
                    b, _, r = it
                    ge(act, t31_done, b)
                    ge_alone(act, nb3_ready, b + 1)
                    nc.scalar.activation(xn3[0:S, :], X[0:S, b, :], ACT.Identity, bias=nbA[0:S, r:r + 1],
                                         scale=rsA[0:S, r:r + 1]).then_inc(xn3_ready, 1)
                if it := behind(g, j, 4, U, B):
                    b, _, r = it
                    ge(act, hq_ready, b - 1)
                    ge(act, hb_ready, b + 1)
                    nc.scalar.activation(hg[0:S, r % 2, :], hb[0:S, :], ACT.Gelu).then_inc(gelu_done, 1)
                if it := behind(g, j, 6, U, B):
                    b, _, _ = it
                    ge(act, th_done, b + 1)
                    nc.scalar.activation(hqT[:, :, :].rearrange("p (u c) b -> p u (c b)", u=2), PS[:, 6:8, 0:4 * S],
                                         ACT.Identity, bias=nmagic[:, :]).then_inc(hqT_ready, 1)
                if it := behind(g, j, 0, U, B):
                    b, _, _ = it
                    ge(act, t31_done, b + 1)
                    copy(flat(xn3T[:, :, :]), bank(0, KC * S)).then_inc(xn3T_ready, 1)
                if it := behind(g, j, 2, U, B):
                    b, _, r = it
                    ge(act, x_seq, 5 * b + 5)
                    nc.scalar.activation(xq[0:S, :], h0[0:S, r % 2, :], ACT.Identity, bias=pmagic[0:S, :],
                                         scale=amx[0:S, r, 2:3]).then_inc(xq_ready, 1)
                if it := behind(g, j, 5, U, B):
                    b, _, r = it
                    ge(act, h_seq, 3 * b + 3)
                    nc.scalar.activation(hq[0:S, :], hg[0:S, r % 2, :], ACT.Identity, bias=pmagic[0:S, :],
                                         scale=amh[0:S, r, 2:3]).then_inc(hq_ready, 1)
            steps(act, step3, U, B, ends=2)

        @block.vector
        def _(dve):
            v = nc.vector

            def link(ins, s, value):
                ins.then_inc(s, 1)
                dve.wait_ge(s, value)

            def flat(ap):
                return ap.rearrange("p a b -> p (a b)")

            dve.wait_ge(qk_in, 16)
            for i, (raw, eff) in enumerate(((raw_q, eff_q), (raw_k, eff_k), (raw_v, eff_v))):
                if i == 2:
                    dve.wait_ge(vo_in, 16)
                dve.wait_ge(low_done, i + 1)
                v.tensor_tensor(flat(eff[:, :, :]), PS[:, i, :], flat(raw[:, :, :]), ALU.add).then_inc(eff_done, 1)

            def norm(dst, b, r, mv, rs):
                return v.tensor_scalar(dst, X[0:S, b, :], mv[0:S, r, 0:1], rs[0:S, r:r + 1], ALU.subtract, ALU.mult)


            def bc(ap, n_):
                return ap.unsqueeze(2).broadcast_to([ap.shape[0], ap.shape[1], n_])

            def route(g, piece):
                if piece:
                    ge(dve, route_seq, LINKS * g + piece)
                else:
                    ge(dve, logit_done, U * (g + 1))
                if piece == 2:
                    ge(dve, rexp_done, g + 1)
                L = logit[0:S, :, :]
                T = [rt[0:S, i, :].rearrange("p (b e) -> p b e", b=U) for i in range(6)]
                V = [rv[0:S, i, :] for i in range(10)]
                rev_b = rev[0:S, :].unsqueeze(1).broadcast_to([S, U, E])
                if piece == 0:
                    ins = v.tensor_reduce(V[0], L, AX, ALU.max)
                elif piece == 1:
                    ins = v.tensor_tensor(T[0], L, bc(V[0], E), ALU.subtract)
                elif piece == 2:
                    ins = v.tensor_reduce(V[1], T[1], AX, ALU.add)
                elif piece == 3:
                    ins = v.reciprocal(V[2], V[1])
                elif piece == 4:
                    ins = v.tensor_tensor(T[2], T[1], bc(V[2], E), ALU.mult)
                elif piece == 5:
                    ins = v.tensor_reduce(V[3], T[2], AX, ALU.max)
                elif piece == 6:
                    ins = v.tensor_tensor(T[3], T[2], bc(V[3], E), ALU.is_ge)
                elif piece == 7:
                    ins = v.tensor_tensor(T[3], T[3], rev_b, ALU.mult)
                elif piece == 8:
                    ins = v.tensor_reduce(V[4], T[3], AX, ALU.max)
                elif piece == 9:
                    ins = v.tensor_tensor(T[4], rev_b, bc(V[4], E), ALU.is_equal)
                elif piece == 10:
                    ins = v.scalar_tensor_tensor(T[4], T[4], -2.0, T[2], ALU.mult, ALU.add)
                elif piece == 11:
                    ins = v.tensor_reduce(V[5], T[4], AX, ALU.max)
                elif piece == 12:
                    ins = v.tensor_tensor(T[5], T[4], bc(V[5], E), ALU.is_ge)
                elif piece == 13:
                    ins = v.tensor_tensor(T[5], T[5], rev_b, ALU.mult)
                elif piece == 14:
                    ins = v.tensor_reduce(V[6], T[5], AX, ALU.max)
                elif piece == 15:
                    ins = v.tensor_scalar(V[8], V[5], 0.0, None, ALU.is_gt)
                elif piece == 16:
                    ins = v.tensor_tensor(V[7], V[6], V[4], ALU.subtract)
                elif piece == 17:
                    ins = v.scalar_tensor_tensor(V[7], V[7], 0.0, V[8], ALU.min, ALU.mult)
                elif piece == 18:
                    ins = v.tensor_tensor(V[9], V[4], V[7], ALU.add)
                elif piece == 19:
                    ins = v.tensor_tensor(T[5], rev_b, bc(V[9], E), ALU.is_equal)
                elif piece == 20:
                    ins = v.tensor_copy(OH[0:S, :, bass.ds(U * g, U)].rearrange("p e b -> p b e"), T[5])
                elif piece == 21:
                    ins = v.tensor_tensor(T[4], T[5], T[2], ALU.mult)
                if piece < LINKS:
                    ins.then_inc(route_seq, 1)
                else:
                    v.tensor_reduce(w_tab[0:S, bass.ds(U * g, U)], T[4], AX, ALU.add).then_inc(route_done, 1)

            def weights_slot(j, i):
                pair = ((raw_w1, flat(w1q[:, :, :])), (raw_w2, flat(w2q[:, :, :])))
                if (j, i) == (2, 0):
                    dve.wait_ge(wsum_done, 1)
                    v.tensor_reduce(wmean[:, :], PS[:, 7, 64:64 + 2 * QC].rearrange("p (w c) -> p w c", w=2), AX, ALU.add).then_inc(dve_w, 1)
                if (j, i) == (2, 1):
                    dve.wait_ge(dve_w, 1)
                    v.tensor_scalar(wmean[:, :], wmean[:, :], 1.0 / (HID * D), EPS, ALU.mult, ALU.max).then_inc(dve_w, 1)
                if (j, i) == (2, 2):
                    dve.wait_ge(dve_w, 2)
                    v.reciprocal(wscale[:, :], wmean[:, :]).then_inc(dve_w, 1)
                    v.tensor_copy(wdq[:, 0:1], wmean[:, 0:1])
                    dve.wait_ge(tanh_done, 1)
                    v.tensor_tensor(wdq[:, 1:2], wmean[:, 1:2], tg[:, 3:4], ALU.mult).then_inc(dve_w, 1)
                n = {(2, 3): (0,), (2, 4): (1,), (2, 5): (2,), (3, 0): (3,), (3, 2): (4,), (3, 3): (5,), (3, 4): (6,), (3, 5): (7,)}.get((j, i), ())
                for c in n:
                    raw, q = pair[c // QC]
                    cols = slice(c % QC * QW, (c % QC + 1) * QW)
                    dve.wait_ge(wround_done, c + 1)
                    v.tensor_scalar(q[:, cols], raw[:, cols], MAGIC, 1.0, ALU.subtract, ALU.min).then_inc(dve_w, 1)
                if (j, i) in ((3, 1), (3, 5)):
                    w = i // 5
                    dve.wait_ge(dve_w, 4 + QC * (w + 1))
                    v.tensor_scalar(pair[w][1], pair[w][1], -1.0, None, ALU.max).then_inc(quant_done, 1)

            def route_slot(g, j, i):
                if isinstance(g, int) and g == 1:
                    weights_slot(j, i)
                if it := behind(g, j, 8, U, B + U):
                    bg, slot = it[1], 6 * it[2] + i
                    if not isinstance(bg, int) or bg < NG - 1:
                        if slot != 2:
                            route(bg, slot - (slot > 2))
                    elif slot == 0:
                        for piece in range(LINKS + 1):
                            route(bg, piece)

            dve.wait_ge(x_in0, 16)

            def step1(g, j):
                if it := behind(g, j, 0, U, B):
                    b, _, r = it
                    v.bn_stats(st[0:S, 0, :], X[0:S, b, :]).then_inc(stat1_seq, 1)
                route_slot(g, j, 0)
                if it := behind(g, j, 2, U, B):
                    b, _, r = it
                    ge(dve, exp_done, b + 1)
                    v.reciprocal(rsum_inv[0:S, r:r + 1], rowsum[0:S, r:r + 1]).then_inc(coef_seq, 1)
                if it := behind(g, j, 0, U, B):
                    b, _, r = it
                    ge_alone(dve, stat1_seq, b + 1)
                    v.bn_aggr(mvA[0:S, r, :], st[0:S, 0, :]).then_inc(mv1_ready, 1)
                route_slot(g, j, 1)
                if it := behind(g, j, 2, U, B):
                    b, _, r = it
                    if isinstance(b, int) and b == 0:
                        dve.wait_ge(tanh_done, 1)
                    ge(dve, coef_seq, 2 * b + 1)
                    v.tensor_tensor(coef[0:S, r:r + 1], rsum_inv[0:S, r:r + 1], tg[0:S, 0:1], ALU.mult).then_inc(coef_seq, 1)
                route_slot(g, j, 2)
                if it := behind(g, j, 0, U, B):
                    b, _, r = it
                    ge(dve, t1_done, b)
                    ge(dve, rstd1_ready, b + 1)
                    norm(xn[0:S, :], b, r, mvA, rsA).then_inc(xn_ready, 1)
                if it := behind(g, j, 3, U, B):
                    b, _, r = it
                    ge(dve, coef_seq, 2 * (b + 1))
                    ge(dve, o_done, b + 1)
                    v.scalar_tensor_tensor(X[0:S, b, :], PS[0:S, 5, 0:D], coef[0:S, r:r + 1], X[0:S, b, :],
                                           ALU.mult, ALU.add).then_inc(res_done, 1)
                route_slot(g, j, 3)
                if it := behind(g, j, 3, U, B):
                    b, _, r = it
                    ge_alone(dve, res_done, b + 1)
                    v.bn_stats(st[0:S, 1, :], X[0:S, b, :]).then_inc(stat2_seq, 1)
                if it := behind(g, j, 3, U, B):
                    b, _, r = it
                    ge_alone(dve, stat2_seq, b + 1)
                    v.bn_aggr(mvB[0:S, r, :], st[0:S, 1, :]).then_inc(mv2_ready, 1)
                route_slot(g, j, 4)
                if it := behind(g, j, 1, U, B):
                    b, _, r = it
                    ge(dve, s_done, b + 1)
                    v.tensor_reduce(negmax[0:S, r:r + 1], PS[0:S, 2, 0:SK], AX, ALU.max, negate=True).then_inc(max_done, 1)
                if it := behind(g, j, 3, U, B):
                    b, bg, r = it
                    ge(dve, t3_done, b - 1)
                    ge(dve, xn2_stored[r % 2], 16 * (2 * bg + r // 2))
                    ge(dve, rstd2_ready, b + 1)
                    norm(xn2[0:S, r % 2, 0:D], b, r, mvB, rsB).then_inc(xn2_ready, 1)
                if it := behind(g, j, 4, U, B):
                    b, bg, r = it
                    if isinstance(b, int) and b == 0:
                        dve.wait_ge(consts_set, CONSTS)
                    ge(dve, l_done, b + 1)
                    v.tensor_tensor(logit[0:S, r, :], PS[0:S, 7, 0:E], small_bc[0:S, 4:4 + E], ALU.add).then_inc(logit_done, 1)
                route_slot(g, j, 5)
            for j in range(U):
                step1(0, j)
            dve.wait_ge(x_in1, 16)
            for j in range(U):
                step1(1, j)
            dve.wait_ge(x_in2, 16)
            with dve.Fori(2, NG) as g:
                for j in range(U):
                    step1(g, j)
            for g in range(NG, NG + 2):
                for j in range(U):
                    step1(g, j)

            n = 0

            def then(ins):
                nonlocal n
                n += 1
                link(ins, plan_seq, n)
            EB = E * B
            dve.wait_ge(count_done, 1)
            v.memset(ce[:, 0:1], 0.0)
            then(v.tensor_tensor_scan(cum[:, :], PS[:, 1, 0:EB], zeros[:, 0:EB], 0.0, ALU.add, ALU.add))
            then(v.tensor_copy(ce[:, 1:E + 1], cum[:, B - 1:EB:B]))
            v.tensor_tensor(cex[:, :], cum[:, :], PS[:, 1, 0:EB], ALU.subtract)
            then(v.tensor_tensor(sl[:, 0, :], ce[:, 1:E + 1], ce[:, 0:E], ALU.subtract))
            then(v.tensor_scalar(sl[:, 1, :], sl[:, 0, :], 1.0 / P, (P - 1.0) / P + FLOOR, ALU.mult, ALU.add))
            then(v.tensor_scalar(sl[:, 2, :], sl[:, 1, :], MAGIC, MAGIC, ALU.add, ALU.subtract))
            then(v.tensor_tensor_scan(sl[:, 3, :], sl[:, 2, :], zeros[:, 0:E], 0.0, ALU.add, ALU.add))
            then(v.tensor_tensor(sl[:, 4, :], sl[:, 3, :], sl[:, 2, :], ALU.subtract))
            then(v.scalar_tensor_tensor(sl[:, 5, :], sl[:, 4, :], float(P), ce[:, 0:E], ALU.mult, ALU.subtract))
            dve.wait_ge(count_done, 2)
            then(v.tensor_tensor(acc[0:S, :], PS[0:S, 0, 0:EB], cex[0:S, :], ALU.add))
            acc3 = acc[0:S, :].rearrange("p (e b) -> p e b", e=E)
            then(v.tensor_tensor(acc3, acc3, bc(sl[0:S, 5, :], B), ALU.add))
            then(v.tensor_tensor(acc3, acc3, OH[0:S, :, :], ALU.mult))
            then(v.tensor_reduce(pos[0:S, :], acc3.rearrange("p e b -> p b e"), AX, ALU.add))
            then(v.tensor_scalar(slot_f[0:S, :], pos[0:S, :], 1.0 / P, FLOOR, ALU.mult, ALU.add))
            then(v.tensor_scalar(slot_f[0:S, :], slot_f[0:S, :], MAGIC, MAGIC, ALU.add, ALU.subtract))
            v.scalar_tensor_tensor(r_b[0:S, :], slot_f[0:S, :], -float(P), pos[0:S, :], ALU.mult, ALU.add)
            then(v.tensor_copy(slot_b[0:S, :], slot_f[0:S, :]))
            for s in xn2_stored:
                dve.wait_ge(s, 16 * B // 2)
            iota_s = iota_b[0:S, 0:SLOTS].unsqueeze(1).broadcast_to([S, B, SLOTS])
            then(v.tensor_tensor(carry[0:S, :, SLOTS:], bc(slot_b[0:S, :], SLOTS), iota_s, ALU.is_equal))
            then(v.tensor_scalar(carry[0:S, :, 0:SLOTS], carry[0:S, :, SLOTS:], part_no[0:S, :], None, ALU.mult))
            then(v.tensor_tensor(carry[0:S, :, SLOTS:], carry[0:S, :, SLOTS:], batch_no[0:S, :, :], ALU.mult))

            def place_chunk(c):
                v.tensor_tensor(place[0:S, 8 * c:8 * c + 8, :], bc(r_b[0:S, 8 * c:8 * c + 8], P),
                                iota_b[0:S, :].unsqueeze(1).broadcast_to([S, 8, P]), ALU.is_equal).then_inc(place_ready, 1)
            v.tensor_tensor(le[0:1, :, :], sl[0:1, 3, :].unsqueeze(1).broadcast_to([1, SLOTS, E]),
                            bc(iota_row[0:1, 0:SLOTS], E), ALU.is_le).then_inc(plan_seq, 1)
            place_chunk(0)
            n += 1
            dve.wait_ge(plan_seq, n)
            v.tensor_reduce(ex_f[0:1, 0, :], le[0:1, :, :], AX, ALU.add).then_inc(plan_seq, 1)
            place_chunk(1)
            n += 1
            dve.wait_ge(plan_seq, n)
            v.tensor_copy(last_of[0:1, :], ex_f[0:1, 0, :]).then_inc(slots_ready, 1)
            v.tensor_scalar(expert_of[0:1, :], ex_f[0:1, 0, :], E - 1.0, None, ALU.min).then_inc(slots_ready, 1)
            place_chunk(2)
            place_chunk(3)
            v.tensor_copy(pos_u[0:S, :], pos[0:S, :])
            dve.wait_ge(inv_done, 1)
            then(v.tensor_copy(id_b[:, :], PS[:, 2, SLOTS:2 * SLOTS]))
            v.scalar_tensor_tensor(tok_u[:, :], id_b[:, :], float(S), PS[:, 2, 0:SLOTS], ALU.mult, ALU.add).then_inc(tok_ready, 1)
            dve.wait_ge(b2_in, 16)
            v.tensor_scalar(flat(b2_bc[:, :, :]), flat(b2_bc[:, :, :]), tg[:, 2:3], None, ALU.mult).then_inc(b2_scaled, 1)
            dve.wait_ge(slots_ready, 2)
            dve.wait_ge(b2_scaled, 1)
            dve.wait_ge(w_in, 16 * W_DMAS)

            def step2(g, j):
                now, before = behind(g, j, 0, 2, SLOTS), behind(g, j, 1, 2, SLOTS)
                if now:
                    s, sg, r = now
                    ge(dve, x_done, s)
                    ge(dve, xs_in[r], 16 * (sg + 1))
                    v.tensor_scalar(xsw, xs[:, r, 0:D], xs[:, r, D:ROW], None, ALU.mult).then_inc(xsw_ready, 1)
                    e = dve.value_load(expert_of[0:1, bass.ds(s, 1)], min_val=0, max_val=E - 1)
                    v.tensor_copy(b1s[:, r, :], b1_tab[:, e, :]).then_inc(b1_ready, 1)
                    ge_alone(dve, h0_done, s)
                    for k in range(KC):
                        last = v.tensor_copy(w1s[k][:, 0:HID // 2], W1[:, e, k, 0:HID // 2])
                    last.then_inc(w1_ready, 1)
                if before:
                    s, _, r = before
                    ge(dve, b1_ready, s + 1)
                    ge(dve, h1_done, s + 1)
                    for c in range(HC // 2, HC):
                        last = v.tensor_scalar(hT[:, c, :], PS[:, 1, (c - 4) * P:(c - 3) * P], b1s[:, r, c:c + 1], 0.0, ALU.add, ALU.max)
                    last.then_inc(hT1_ready, 1)
                if now:
                    for k in range(KC):
                        last = v.tensor_copy(w1s[k][:, HID // 2:], W1[:, e, k, HID // 2:])
                    last.then_inc(w1_ready, 1)
                if before:
                    s, sg, r = before
                    e = dve.value_load(expert_of[0:1, bass.ds(s, 1)], min_val=0, max_val=E - 1)
                    ge(dve, y_stored[r], 16 * sg)
                    ge(dve, y_done, s + 1)
                    v.scalar_tensor_tensor(ysb[:, r, :], PS[:, 4, 0:D], tg[:, 2:3], b2_bc[:, e, :], ALU.mult, ALU.add).then_inc(y_ready, 1)
            steps(dve, step2, 2, SLOTS, ends=2)

            def step3(g, j):
                H = lambda r, i: amh[0:S, r, i:i + 1]
                Q = lambda r, i: amx[0:S, r, i:i + 1]
                if it := behind(g, j, 4, U, B):
                    b, _, r = it
                    ge(dve, x_seq, 5 * b + 4)
                    v.reciprocal(Q(r, 2), Q(r, 1)).then_inc(x_seq, 1)
                if it := behind(g, j, 5, U, B):
                    b, _, r = it
                    ge(dve, inv1_ready, b + 1)
                    ge(dve, gelu_done, b)
                    ge(dve, f1_done, b + 1)
                    v.scalar_tensor_tensor(hb[0:S, :], flat(PS[0:S, 4:6, :]), inv1[0:S, r:r + 1],
                                           b1_bc[0:S, :], ALU.mult, ALU.add).then_inc(hb_ready, 1)
                if it := behind(g, j, 3, U, B):
                    b, _, r = it
                    ge_alone(dve, x3_seq, 2 * b + 2)
                    v.bn_aggr(mvB[0:S, r, :], st[0:S, 1, :]).then_inc(mv4_ready, 1)
                if it := behind(g, j, 6, U, B):
                    b, _, r = it
                    ge(dve, gelu_done, b + 1)
                    v.tensor_reduce(H(r, 0), hg[0:S, r % 2, :], AX, ALU.max, apply_absolute_value=True).then_inc(h_seq, 1)
                if it := behind(g, j, 3, U, B):
                    b, _, r = it
                    if isinstance(b, int) and b == 0:
                        dve.wait_ge(bc_in, 16 * 4)
                        v.tensor_scalar(gb2_bc, b2raw_bc, tg[:, 3:4], None, ALU.mult).then_inc(gb2_seq, 1)
                    ge(dve, xq_ready, b - 1)
                    ge(dve, mv4_ready, b + 1)
                    v.scalar_tensor_tensor(h0[0:S, r % 2, :], X[0:S, b, :], mvB[0:S, r, 0:1], gamma_bc[0:S, :],
                                           ALU.subtract, ALU.mult).then_inc(x_seq, 1)
                if it := behind(g, j, 0, U, B):
                    b, _, _ = it
                    ge_alone(dve, x2_ready, b + 1)
                    v.bn_stats(st[0:S, 0, :], X[0:S, b, :]).then_inc(stat3_seq, 1)
                if it := behind(g, j, 8, U, B):
                    b, bg, r = it
                    ge(dve, inv2_ready, b + 1)
                    ge(dve, out_stored[r % 2], 16 * (2 * bg + r // 2))
                    ge(dve, xb_ready, b + 1)
                    ge(dve, f2_done, b + 1)
                    v.scalar_tensor_tensor(osb[0:S, r % 2, :], PS[0:S, 3, 0:D], inv2[0:S, r:r + 1], X[0:S, b, :],
                                           ALU.mult, ALU.add).then_inc(out_ready, 1)
                if it := behind(g, j, 3, U, B):
                    b, _, r = it
                    ge(dve, rstd4_ready, b + 1)
                    ge(dve, x_seq, 5 * b + 1)
                    v.scalar_tensor_tensor(h0[0:S, r % 2, :], h0[0:S, r % 2, :], rsB[0:S, r:r + 1], beta_bc[0:S, :],
                                           ALU.mult, ALU.add).then_inc(x_seq, 1)
                if it := behind(g, j, 6, U, B):
                    b, _, r = it
                    ge(dve, h_seq, 3 * b + 1)
                    v.tensor_scalar(H(r, 1), H(r, 0), EPS, 1.0 / 127, ALU.max, ALU.mult).then_inc(h_seq, 1)
                if it := behind(g, j, 0, U, B):
                    b, _, r = it
                    ge_alone(dve, stat3_seq, b + 1)
                    v.bn_aggr(mvA[0:S, r, :], st[0:S, 0, :]).then_inc(mv3_ready, 1)
                if it := behind(g, j, 3, U, B):
                    b, _, r = it
                    ge(dve, x_seq, 5 * b + 2)
                    v.tensor_reduce(Q(r, 0), h0[0:S, r % 2, :], AX, ALU.max, apply_absolute_value=True).then_inc(x_seq, 1)
                if it := behind(g, j, 2, U, B):
                    b, _, _ = it
                    ge(dve, o1_done, b + 1)
                    v.scalar_tensor_tensor(X[0:S, b, :], PS[0:S, 2, 0:D], tg[0:S, 1:2], X[0:S, b, :], ALU.mult, ALU.add).then_inc(x3_seq, 1)
                if it := behind(g, j, 3, U, B):
                    b, _, r = it
                    ge(dve, x_seq, 5 * b + 3)
                    v.tensor_scalar(Q(r, 1), Q(r, 0), EPS, 1.0 / 127, ALU.max, ALU.mult).then_inc(x_seq, 1)
                if it := behind(g, j, 6, U, B):
                    b, _, r = it
                    ge(dve, h_seq, 3 * b + 2)
                    v.reciprocal(H(r, 2), H(r, 1)).then_inc(h_seq, 1)
                if it := behind(g, j, 2, U, B):
                    b, _, _ = it
                    ge_alone(dve, x3_seq, 2 * b + 1)
                    v.bn_stats(st[0:S, 1, :], X[0:S, b, :]).then_inc(x3_seq, 1)
            steps(dve, step3, U, B, ends=3)


LINKS = 22
CONSTS = 13
W_DMAS = 1 + NG + (NG - 2) + 1


_OUTS = [((B, S, D), "float32")]


def kernel(**inputs):
    import numpy as np
    import concourse.bacc as bacc
    from concourse.bass_utils import run_bass_kernel_spmd

    a = {k: np.asarray(v) for k, v in inputs.items()}

    def chunked(w):
        return w.reshape(w.shape[0] // P, P, w.shape[1]).transpose(1, 0, 2)

    def side_by_side(*ws):
        return np.concatenate([w.reshape(P, -1) for w in ws], axis=1)

    ctx = a["ctx_1024"]
    ctxT = ctx.transpose(0, 2, 1).reshape(B, KC, P, SK).transpose(0, 2, 1, 3).reshape(B, P, KC * SK)
    rows = ctx[:, 0:2 * P].reshape(B, 2, P, D).transpose(0, 2, 1, 3).reshape(B, P, 2 * D)
    arrays = [
        ("x", a["x"]),
        ("ctx_pack", np.concatenate([ctxT, rows], axis=2)),
        ("ctx_tail", ctx[:, 2 * P:]),
        ("small", np.concatenate([a["g_xattn"], a["g_ffn"], a["L0_ffn_gate_b"]])),
        ("w_qk", side_by_side(chunked(a["L0_xattn_Q_weight"]), chunked(a["L0_xattn_K_weight"]))),
        ("w_vo", side_by_side(chunked(a["L0_xattn_V_weight"]), chunked(a["L0_xattn_O_weight"].T))),
        ("low", np.stack([a[f"L0_xattn_{n}_{ab}"] if ab == "A" else a[f"L0_xattn_{n}_{ab}"].T
                          for n in "QKV" for ab in "AB"], axis=1).reshape(R, 3, 2, D)),
        ("gateT", chunked(a["L0_ffn_gate_w"].T)),
        ("w1m", a["L0_ffn_w1"].transpose(2, 0, 1).reshape(KC, P, E, HID).transpose(1, 2, 0, 3).reshape(P, -1)),
        ("b1m", a["L0_ffn_b1"].reshape(E, HC, P).transpose(2, 0, 1)),
        ("w2m", a["L0_ffn_w2"].transpose(2, 0, 1).reshape(HC, P, E, D).transpose(1, 2, 0, 3).reshape(P, -1)),
        ("b2m", a["L0_ffn_b2"]),
        ("w1l", chunked(a["L1_ffn_w1"].T).reshape(P, -1)), ("b1l", a["L1_ffn_b1"]),
        ("w2l", chunked(a["L1_ffn_w2"].T).reshape(P, -1)), ("b2l", a["L1_ffn_b2"]),
        ("gamma", a["L1_ffn_gamma"]), ("beta", a["L1_ffn_beta"]),
    ]
    nc = bacc.Bacc("TRN2", target_bir_lowering=False, num_devices=1)
    feeds, args = {}, []
    for name, arr in arrays:
        arr = np.ascontiguousarray(arr)
        feeds[f"in_{name}"] = arr
        args.append(nc.dram_tensor(f"in_{name}", arr.shape, mybir.dt.from_np(arr.dtype), kind="ExternalInput").ap())
    for i, (shape, dtype) in enumerate(_OUTS):
        args.append(nc.dram_tensor(f"out_{i}", shape, mybir.dt.from_np(np.dtype(dtype)), kind="ExternalOutput").ap())
    flamingo_kernel(nc, *args)
    r = run_bass_kernel_spmd(nc, [feeds], core_ids=[0])
    return r.results[0]["out_0"]
```
